# Optimizing a Trainium2 kernel written in Bass

```python
import numpy as np
import jax
import jax.numpy as jnp

def _softmax(x, axis=-1):
    return jax.nn.softmax(x, axis=axis)

def _gelu(x):
    return jax.nn.gelu(x, approximate=True)

def _silu(x):
    return jax.nn.silu(x)

def _sigmoid(x):
    return jax.nn.sigmoid(x)

def _layernorm(x, axis=-1, eps=1e-05):
    m = jnp.mean(x, axis=axis, keepdims=True)
    v = jnp.var(x, axis=axis, keepdims=True)
    return (x - m) / jnp.sqrt(v + eps)

def _scatter_add(tgt, idx, src, axis=0):
    return tgt.at[idx].add(src)

def _segment_sum(src, seg, n):
    return jax.ops.segment_sum(src, seg, n)
kernel_name = 'mk_recurrent_d2_jaxref_r8_7e1c09'

def setup_inputs(seed: int=0):
    np.random.seed(seed)
    _w = jnp.asarray

    def _L0_attn_setup():
        import jax, jax.numpy as jnp
        import numpy as np
        D_MODEL = 128
        NUM_HEADS = 16
        D_HEAD = D_MODEL // NUM_HEADS
        THETA = 10000.0

        def _rope_tables(seq_len, d_k, theta):
            inv_powers = theta ** (-jnp.arange(0, d_k, 2, dtype=jnp.float32) / d_k)
            positions = jnp.arange(seq_len, dtype=jnp.float32)
            angles = jnp.outer(positions, inv_powers)
            return (jnp.cos(angles), jnp.sin(angles))

        def _apply_rope(x, cos, sin):
            x_even = x[..., 0::2]
            x_odd = x[..., 1::2]
            r_even = x_even * cos - x_odd * sin
            r_odd = x_even * sin + x_odd * cos
            return jnp.stack([r_even, r_odd], axis=-1).reshape(x.shape)
        key = jax.random.key(seed)
        ks = jax.random.split(key, 5)
        B, S = (2, 256)
        sigma = (2.0 / (D_MODEL + D_MODEL)) ** 0.5
        x = jax.random.normal(ks[0], (B, S, D_MODEL), dtype=jnp.float32)
        wq = jax.random.normal(ks[1], (D_MODEL, D_MODEL), dtype=jnp.float32) * sigma
        wk = jax.random.normal(ks[2], (D_MODEL, D_MODEL), dtype=jnp.float32) * sigma
        wv = jax.random.normal(ks[3], (D_MODEL, D_MODEL), dtype=jnp.float32) * sigma
        wo = jax.random.normal(ks[4], (D_MODEL, D_MODEL), dtype=jnp.float32) * sigma
        return {'x': x, 'wq': wq, 'wk': wk, 'wv': wv, 'wo': wo}
    _L0_attn_in = _L0_attn_setup()

    def _L0_ffn_setup():
        import jax, jax.numpy as jnp
        import numpy as np
        B, S, D = (2, 128, 128)
        H, HD = (16, 64)
        E_R = 31
        K_ACT = 3
        INTER = 128
        EPS = 1e-05
        BASE = 10000.0

        def _rmsnorm(x, gamma):
            rms = jnp.sqrt(jnp.mean(x * x, axis=-1, keepdims=True) + EPS)
            return x / rms * gamma

        def _rope(x, theta):
            seq = x.shape[2]
            angles = jnp.arange(seq, dtype=theta.dtype)[:, None] * theta
            cos = jnp.cos(angles)[None, None]
            sin = jnp.sin(angles)[None, None]
            x1, x2 = (x[..., 0::2], x[..., 1::2])
            return jnp.concatenate([x1 * cos - x2 * sin, x1 * sin + x2 * cos], axis=-1)

        def _forward(x, theta, gamma1, gamma2, q_w, q_b, k_w, k_b, v_w, v_b, o_w, o_b, router_w, router_b, sh_w1, sh_b1, sh_w2, sh_b2, re_w1, re_b1, re_w2, re_b2):
            b, s, d = x.shape
            xn = _rmsnorm(x, gamma1)
            q = (xn @ q_w + q_b).reshape(b, s, H, HD).transpose(0, 2, 1, 3)
            k = (xn @ k_w + k_b).reshape(b, s, H, HD).transpose(0, 2, 1, 3)
            v = (xn @ v_w + v_b).reshape(b, s, H, HD).transpose(0, 2, 1, 3)
            q = _rope(q, theta)
            k = _rope(k, theta)
            scale = 1.0 / np.sqrt(HD)
            scores = jnp.einsum('bhqd,bhkd->bhqk', q, k) * scale
            causal = jnp.tril(jnp.ones((s, s), dtype=bool))
            scores = jnp.where(causal, scores, -jnp.inf)
            attn = jax.nn.softmax(scores, axis=-1)
            ctx = jnp.einsum('bhqk,bhkd->bhqd', attn, v)
            ctx = ctx.transpose(0, 2, 1, 3).reshape(b, s, H * HD)
            attn_out = ctx @ o_w + o_b + xn
            an = _rmsnorm(attn_out, gamma2)
            shared = jax.nn.gelu(an @ sh_w1 + sh_b1, approximate=False) @ sh_w2 + sh_b2
            logits = an @ router_w + router_b
            aff = jax.nn.softmax(logits, axis=-1)
            topv, topi = jax.lax.top_k(aff, K_ACT)
            gates = jnp.sum(jax.nn.one_hot(topi, E_R, dtype=aff.dtype) * topv[..., None], axis=-2)
            h = jax.nn.gelu(jnp.einsum('bsd,edh->besh', an, re_w1) + re_b1[None, :, None, :], approximate=False)
            routed = jnp.einsum('bse,besh,ehd->bsd', gates, h, re_w2) + jnp.einsum('bse,ed->bsd', gates, re_b2)
            return shared + routed + an + attn_out
        key = jax.random.key(seed)
        ks = jax.random.split(key, 24)
        s = 0.02
        theta = BASE ** (-jnp.arange(HD // 2, dtype=jnp.float32) * 2.0 / HD)
        inp = {'x': jax.random.normal(ks[0], (B, S, D), jnp.float32), 'positions': jnp.arange(S, dtype=jnp.int32), 'theta': theta, 'gamma1': jnp.ones((D,), jnp.float32), 'gamma2': jnp.ones((D,), jnp.float32), 'q_w': jax.random.normal(ks[1], (D, H * HD), jnp.float32) * s, 'q_b': jnp.zeros((H * HD,), jnp.float32), 'k_w': jax.random.normal(ks[2], (D, H * HD), jnp.float32) * s, 'k_b': jnp.zeros((H * HD,), jnp.float32), 'v_w': jax.random.normal(ks[3], (D, H * HD), jnp.float32) * s, 'v_b': jnp.zeros((H * HD,), jnp.float32), 'o_w': jax.random.normal(ks[4], (H * HD, D), jnp.float32) * s, 'o_b': jnp.zeros((D,), jnp.float32), 'router_w': jax.random.normal(ks[5], (D, E_R), jnp.float32) * s, 'router_b': jnp.zeros((E_R,), jnp.float32), 'sh_w1': jax.random.normal(ks[6], (D, INTER), jnp.float32) * s, 'sh_b1': jnp.zeros((INTER,), jnp.float32), 'sh_w2': jax.random.normal(ks[7], (INTER, D), jnp.float32) * s, 'sh_b2': jnp.zeros((D,), jnp.float32), 're_w1': jax.random.normal(ks[8], (E_R, D, INTER), jnp.float32) * s, 're_b1': jnp.zeros((E_R, INTER), jnp.float32), 're_w2': jax.random.normal(ks[9], (E_R, INTER, D), jnp.float32) * s, 're_b2': jnp.zeros((E_R, D), jnp.float32)}
        return inp
    _L0_ffn_in = _L0_ffn_setup()

    def _L1_attn_setup():
        import jax, jax.numpy as jnp
        import numpy as np
        import math
        B, L, D = (2, 512, 128)
        H, DK, DV = (4, 32, 32)
        CHUNK = 32
        PROB_FLOOR = 0.02

        def _l2norm(x, eps=1e-06):
            return x * jax.lax.rsqrt(jnp.sum(x * x, -1, keepdims=True) + eps)

        def _silu(x):
            return x * jax.nn.sigmoid(x)

        def _short_conv(x, w):
            K = w.shape[-1]
            xp = jnp.pad(x, ((0, 0), (K - 1, 0), (0, 0)))
            y = sum((xp[:, j:j + x.shape[1], :] * w[:, j] for j in range(K)))
            return _silu(y)

        def _fir_conv(x, filt):
            b, l, h, d = x.shape
            K = filt.shape[-1]
            xf = jnp.pad(x.reshape(b, l, h * d).transpose(0, 2, 1), ((0, 0), (0, 0), (K - 1, 0)))
            w = filt.reshape(h * d, 1, K)
            y = jax.lax.conv_general_dilated(xf, w, (1,), 'VALID', dimension_numbers=('NCH', 'OIH', 'NCH'), feature_group_count=h * d)
            return y.transpose(0, 2, 1).reshape(b, l, h, d)

        def _delta_rule_chunkwise(q, k, v, beta, chunk=CHUNK):
            b, h, Lq, dk = q.shape
            dv = v.shape[-1]
            n = Lq // chunk
            q = _l2norm(q)
            k = _l2norm(k)
            v = v * beta[..., None]
            kb = k * beta[..., None]
            rs = lambda t: t.reshape(b, h, n, chunk, t.shape[-1])
            qc, kc, vc, kbc = (rs(q), rs(k), rs(v), rs(kb))
            strict_lower = jnp.tril(jnp.ones((chunk, chunk), bool), -1)
            M = jnp.where(strict_lower, jnp.einsum('bhncd,bhnmd->bhncm', kbc, kc), 0.0)
            eye = jnp.eye(chunk, dtype=q.dtype)
            T = jax.scipy.linalg.solve_triangular(eye + M, jnp.broadcast_to(eye, M.shape), lower=True, unit_diagonal=True)
            u = T @ vc
            w = T @ kbc
            incl_lower = jnp.tril(jnp.ones((chunk, chunk), bool), 0)

            def step(S, xs):
                q_i, k_i, u_i, w_i = xs
                attn = jnp.where(incl_lower, q_i @ k_i.swapaxes(-1, -2), 0.0)
                u_adj = u_i - w_i @ S
                out_i = q_i @ S + attn @ u_adj
                S = S + k_i.swapaxes(-1, -2) @ u_adj
                return (S, out_i)
            S0 = jnp.zeros((b, h, dk, dv), q.dtype)
            xs = tuple((jnp.moveaxis(t, 2, 0) for t in (qc, kc, u, w)))
            S, out = jax.lax.scan(step, S0, xs)
            out = jnp.moveaxis(out, 0, 2).reshape(b, h, Lq, dv)
            return (out, S)

        def _rmsnorm(x, w, eps=1e-05):
            return x * jax.lax.rsqrt(jnp.mean(x * x, -1, keepdims=True) + eps) * w

        def _per_head_stats(x):
            mean = jnp.mean(x, -1, keepdims=True)
            var = jnp.var(x, -1, keepdims=True)
            am = jnp.mean(jnp.abs(x), -1, keepdims=True)
            l2 = jnp.sqrt(jnp.sum(x * x, -1, keepdims=True))
            return jnp.concatenate([mean, var, am, l2], -1)

        def _forward(hidden_states, q_w, k_w, v_w, b_w, q_cw, k_cw, v_cw, fir_short_w, fir_long_w, mlp1_w, mlp1_b, mlp2_w, mlp2_b, logit_temp, conv_res_logit, norm_w, o_w):
            b, l, _ = hidden_states.shape
            q_in = _short_conv(hidden_states @ q_w.T, q_cw)
            k_in = _short_conv(hidden_states @ k_w.T, k_cw)
            v_in = _short_conv(hidden_states @ v_w.T, v_cw)
            q = q_in.reshape(b, l, H, DK)
            k = k_in.reshape(b, l, H, DK)
            v_direct = v_in.reshape(b, l, H, DV)
            beta = jnp.maximum(jax.nn.sigmoid(hidden_states @ b_w.T), 1e-06)
            delta_out, _S = _delta_rule_chunkwise(q.transpose(0, 2, 1, 3), k.transpose(0, 2, 1, 3), v_direct.transpose(0, 2, 1, 3), beta.transpose(0, 2, 1))
            delta_out = delta_out.transpose(0, 2, 1, 3)
            local_short = _fir_conv(v_direct, fir_short_w)
            local_long = _fir_conv(v_direct, fir_long_w)
            stats = jnp.concatenate([_per_head_stats(local_short), _per_head_stats(local_long), _per_head_stats(delta_out), _per_head_stats(v_direct)], -1)
            hs_exp = jnp.broadcast_to(hidden_states[:, :, None, :], (b, l, H, hidden_states.shape[-1]))
            gate_in = jnp.concatenate([hs_exp, stats], -1)
            h1 = jax.nn.gelu(gate_in @ mlp1_w.T + mlp1_b)
            logits = h1 @ mlp2_w.T + mlp2_b
            temp = jax.nn.softplus(logit_temp)
            p = jax.nn.softmax(logits / temp, -1)
            p = jnp.maximum(p, PROB_FLOOR)
            p = p / jnp.sum(p, -1, keepdims=True)
            o = p[..., 0:1] * local_short + p[..., 1:2] * local_long + p[..., 2:3] * delta_out + p[..., 3:4] * v_direct
            o = o + jax.nn.sigmoid(conv_res_logit)[None, None, :, None] * local_short
            o = _rmsnorm(o, norm_w)
            o = o.reshape(b, l, H * DV) @ o_w.T
            return o
        key = jax.random.key(seed)
        ks = jax.random.split(key, 16)
        s = 0.02
        hidden_gate = D * 2 // 2
        gate_in_dim = D + 16
        inp = {'hidden_states': jax.random.normal(ks[0], (B, L, D), jnp.float32), 'q_w': jax.random.normal(ks[1], (D, D), jnp.float32) * s, 'k_w': jax.random.normal(ks[2], (D, D), jnp.float32) * s, 'v_w': jax.random.normal(ks[3], (D, D), jnp.float32) * s, 'b_w': jax.random.normal(ks[4], (H, D), jnp.float32) * s, 'q_cw': jax.random.normal(ks[5], (D, 4), jnp.float32) * s, 'k_cw': jax.random.normal(ks[6], (D, 4), jnp.float32) * s, 'v_cw': jax.random.normal(ks[7], (D, 4), jnp.float32) * s, 'fir_short_w': jax.random.normal(ks[8], (H, DV, 5), jnp.float32) * s, 'fir_long_w': jax.random.normal(ks[9], (H, DV, 64), jnp.float32) * s, 'mlp1_w': jax.random.normal(ks[10], (hidden_gate, gate_in_dim), jnp.float32) * s, 'mlp1_b': jnp.zeros((hidden_gate,), jnp.float32), 'mlp2_w': jax.random.normal(ks[11], (4, hidden_gate), jnp.float32) * s, 'mlp2_b': jnp.array([-0.5, -0.5, 1.0, 3.0], jnp.float32), 'logit_temp': jnp.full((1,), math.log(math.expm1(0.7)), jnp.float32), 'conv_res_logit': jnp.full((H,), -2.0, jnp.float32), 'norm_w': jnp.ones((DV,), jnp.float32), 'o_w': jax.random.normal(ks[12], (D, D), jnp.float32) * s}
        return inp
    _L1_attn_in = _L1_attn_setup()

    def _L1_ffn_setup():
        import jax, jax.numpy as jnp
        import numpy as np
        EPS = 0.05
        N_ITERS = 20
        TOP_K = 2

        def _sinkhorn(cost, n_iters=N_ITERS, epsilon=EPS):
            la = cost / epsilon
            for _ in range(n_iters):
                la = la - jax.scipy.special.logsumexp(la, axis=-1, keepdims=True)
                la = la - jax.scipy.special.logsumexp(la, axis=-2, keepdims=True)
            return jnp.exp(la)
        key = jax.random.key(seed)
        k0, k1, k2, k3, k4 = jax.random.split(key, 5)
        B, T, D, F, E = (2, 256, 128, 512, 8)
        x = jax.random.normal(k0, (B, T, D), dtype=jnp.float32)
        gate_W = jax.random.normal(k1, (E, D), dtype=jnp.float32) * 0.02
        W_gate = jax.random.normal(k2, (E, F, D), dtype=jnp.float32) * 0.02
        W_up = jax.random.normal(k3, (E, F, D), dtype=jnp.float32) * 0.02
        W_down = jax.random.normal(k4, (E, D, F), dtype=jnp.float32) * 0.02
        return {'x': x, 'gate_W': gate_W, 'W_gate': W_gate, 'W_up': W_up, 'W_down': W_down}
    _L1_ffn_in = _L1_ffn_setup()
    _d = {'L0_attn_x': _L0_attn_in['x'], 'L0_attn_wq': _L0_attn_in['wq'], 'L0_attn_wk': _L0_attn_in['wk'], 'L0_attn_wv': _L0_attn_in['wv'], 'L0_attn_wo': _L0_attn_in['wo'], 'L0_ffn_positions': _L0_ffn_in['positions'], 'L0_ffn_theta': _L0_ffn_in['theta'], 'L0_ffn_gamma1': _L0_ffn_in['gamma1'], 'L0_ffn_gamma2': _L0_ffn_in['gamma2'], 'L0_ffn_q_w': _L0_ffn_in['q_w'], 'L0_ffn_q_b': _L0_ffn_in['q_b'], 'L0_ffn_k_w': _L0_ffn_in['k_w'], 'L0_ffn_k_b': _L0_ffn_in['k_b'], 'L0_ffn_v_w': _L0_ffn_in['v_w'], 'L0_ffn_v_b': _L0_ffn_in['v_b'], 'L0_ffn_o_w': _L0_ffn_in['o_w'], 'L0_ffn_o_b': _L0_ffn_in['o_b'], 'L0_ffn_router_w': _L0_ffn_in['router_w'], 'L0_ffn_router_b': _L0_ffn_in['router_b'], 'L0_ffn_sh_w1': _L0_ffn_in['sh_w1'], 'L0_ffn_sh_b1': _L0_ffn_in['sh_b1'], 'L0_ffn_sh_w2': _L0_ffn_in['sh_w2'], 'L0_ffn_sh_b2': _L0_ffn_in['sh_b2'], 'L0_ffn_re_w1': _L0_ffn_in['re_w1'], 'L0_ffn_re_b1': _L0_ffn_in['re_b1'], 'L0_ffn_re_w2': _L0_ffn_in['re_w2'], 'L0_ffn_re_b2': _L0_ffn_in['re_b2'], 'L1_attn_q_w': _L1_attn_in['q_w'], 'L1_attn_k_w': _L1_attn_in['k_w'], 'L1_attn_v_w': _L1_attn_in['v_w'], 'L1_attn_b_w': _L1_attn_in['b_w'], 'L1_attn_q_cw': _L1_attn_in['q_cw'], 'L1_attn_k_cw': _L1_attn_in['k_cw'], 'L1_attn_v_cw': _L1_attn_in['v_cw'], 'L1_attn_fir_short_w': _L1_attn_in['fir_short_w'], 'L1_attn_fir_long_w': _L1_attn_in['fir_long_w'], 'L1_attn_mlp1_w': _L1_attn_in['mlp1_w'], 'L1_attn_mlp1_b': _L1_attn_in['mlp1_b'], 'L1_attn_mlp2_w': _L1_attn_in['mlp2_w'], 'L1_attn_mlp2_b': _L1_attn_in['mlp2_b'], 'L1_attn_logit_temp': _L1_attn_in['logit_temp'], 'L1_attn_conv_res_logit': _L1_attn_in['conv_res_logit'], 'L1_attn_norm_w': _L1_attn_in['norm_w'], 'L1_attn_o_w': _L1_attn_in['o_w'], 'L1_ffn_gate_W': _L1_ffn_in['gate_W'], 'L1_ffn_W_gate': _L1_ffn_in['W_gate'], 'L1_ffn_W_up': _L1_ffn_in['W_up'], 'L1_ffn_W_down': _L1_ffn_in['W_down']}
    _x0 = _d['L0_attn_x']
    _d['L0_attn_x'] = jax.random.normal(jax.random.fold_in(jax.random.key(seed), 1), (8, 512, 128), dtype=_x0.dtype)
    del _x0
    return _d

def reference(L0_attn_x, L0_attn_wq, L0_attn_wk, L0_attn_wv, L0_attn_wo, L0_ffn_positions, L0_ffn_theta, L0_ffn_gamma1, L0_ffn_gamma2, L0_ffn_q_w, L0_ffn_q_b, L0_ffn_k_w, L0_ffn_k_b, L0_ffn_v_w, L0_ffn_v_b, L0_ffn_o_w, L0_ffn_o_b, L0_ffn_router_w, L0_ffn_router_b, L0_ffn_sh_w1, L0_ffn_sh_b1, L0_ffn_sh_w2, L0_ffn_sh_b2, L0_ffn_re_w1, L0_ffn_re_b1, L0_ffn_re_w2, L0_ffn_re_b2, L1_attn_q_w, L1_attn_k_w, L1_attn_v_w, L1_attn_b_w, L1_attn_q_cw, L1_attn_k_cw, L1_attn_v_cw, L1_attn_fir_short_w, L1_attn_fir_long_w, L1_attn_mlp1_w, L1_attn_mlp1_b, L1_attn_mlp2_w, L1_attn_mlp2_b, L1_attn_logit_temp, L1_attn_conv_res_logit, L1_attn_norm_w, L1_attn_o_w, L1_ffn_gate_W, L1_ffn_W_gate, L1_ffn_W_up, L1_ffn_W_down):

    def _L0_attn_ref(x, wq, wk, wv, wo):
        import jax, jax.numpy as jnp
        import numpy as np
        D_MODEL = 128
        NUM_HEADS = 16
        D_HEAD = D_MODEL // NUM_HEADS
        THETA = 10000.0

        def _rope_tables(seq_len, d_k, theta):
            inv_powers = theta ** (-jnp.arange(0, d_k, 2, dtype=jnp.float32) / d_k)
            positions = jnp.arange(seq_len, dtype=jnp.float32)
            angles = jnp.outer(positions, inv_powers)
            return (jnp.cos(angles), jnp.sin(angles))

        def _apply_rope(x, cos, sin):
            x_even = x[..., 0::2]
            x_odd = x[..., 1::2]
            r_even = x_even * cos - x_odd * sin
            r_odd = x_even * sin + x_odd * cos
            return jnp.stack([r_even, r_odd], axis=-1).reshape(x.shape)
        B, S, D = x.shape
        H, Dh = (NUM_HEADS, D_HEAD)
        q = jnp.einsum('bsd,od->bso', x, wq)
        k = jnp.einsum('bsd,od->bso', x, wk)
        v = jnp.einsum('bsd,od->bso', x, wv)
        q = q.reshape(B, S, H, Dh).transpose(0, 2, 1, 3)
        k = k.reshape(B, S, H, Dh).transpose(0, 2, 1, 3)
        v = v.reshape(B, S, H, Dh).transpose(0, 2, 1, 3)
        cos, sin = _rope_tables(S, Dh, THETA)
        q = _apply_rope(q, cos, sin)
        k = _apply_rope(k, cos, sin)
        scale = 1.0 / jnp.sqrt(jnp.float32(Dh))
        scores = jnp.einsum('bhqd,bhkd->bhqk', q, k) * scale
        causal = jnp.tril(jnp.ones((S, S), dtype=bool))
        scores = jnp.where(causal, scores, -jnp.inf)
        probs = jax.nn.softmax(scores, axis=-1)
        attn = jnp.einsum('bhqk,bhkd->bhqd', probs, v)
        attn = attn.transpose(0, 2, 1, 3).reshape(B, S, D)
        return jnp.einsum('bsd,od->bso', attn, wo)

    def _L0_ffn_ref(x, positions, theta, gamma1, gamma2, q_w, q_b, k_w, k_b, v_w, v_b, o_w, o_b, router_w, router_b, sh_w1, sh_b1, sh_w2, sh_b2, re_w1, re_b1, re_w2, re_b2):
        import jax, jax.numpy as jnp
        import numpy as np
        B, S, D = (2, 128, 128)
        H, HD = (16, 64)
        E_R = 31
        K_ACT = 3
        INTER = 128
        EPS = 1e-05
        BASE = 10000.0

        def _rmsnorm(x, gamma):
            rms = jnp.sqrt(jnp.mean(x * x, axis=-1, keepdims=True) + EPS)
            return x / rms * gamma

        def _rope(x, theta):
            seq = x.shape[2]
            angles = jnp.arange(seq, dtype=theta.dtype)[:, None] * theta
            cos = jnp.cos(angles)[None, None]
            sin = jnp.sin(angles)[None, None]
            x1, x2 = (x[..., 0::2], x[..., 1::2])
            return jnp.concatenate([x1 * cos - x2 * sin, x1 * sin + x2 * cos], axis=-1)

        def _forward(x, theta, gamma1, gamma2, q_w, q_b, k_w, k_b, v_w, v_b, o_w, o_b, router_w, router_b, sh_w1, sh_b1, sh_w2, sh_b2, re_w1, re_b1, re_w2, re_b2):
            b, s, d = x.shape
            xn = _rmsnorm(x, gamma1)
            q = (xn @ q_w + q_b).reshape(b, s, H, HD).transpose(0, 2, 1, 3)
            k = (xn @ k_w + k_b).reshape(b, s, H, HD).transpose(0, 2, 1, 3)
            v = (xn @ v_w + v_b).reshape(b, s, H, HD).transpose(0, 2, 1, 3)
            q = _rope(q, theta)
            k = _rope(k, theta)
            scale = 1.0 / np.sqrt(HD)
            scores = jnp.einsum('bhqd,bhkd->bhqk', q, k) * scale
            causal = jnp.tril(jnp.ones((s, s), dtype=bool))
            scores = jnp.where(causal, scores, -jnp.inf)
            attn = jax.nn.softmax(scores, axis=-1)
            ctx = jnp.einsum('bhqk,bhkd->bhqd', attn, v)
            ctx = ctx.transpose(0, 2, 1, 3).reshape(b, s, H * HD)
            attn_out = ctx @ o_w + o_b + xn
            an = _rmsnorm(attn_out, gamma2)
            shared = jax.nn.gelu(an @ sh_w1 + sh_b1, approximate=False) @ sh_w2 + sh_b2
            logits = an @ router_w + router_b
            aff = jax.nn.softmax(logits, axis=-1)
            topv, topi = jax.lax.top_k(aff, K_ACT)
            gates = jnp.sum(jax.nn.one_hot(topi, E_R, dtype=aff.dtype) * topv[..., None], axis=-2)
            h = jax.nn.gelu(jnp.einsum('bsd,edh->besh', an, re_w1) + re_b1[None, :, None, :], approximate=False)
            routed = jnp.einsum('bse,besh,ehd->bsd', gates, h, re_w2) + jnp.einsum('bse,ed->bsd', gates, re_b2)
            return shared + routed + an + attn_out
        del positions
        return _forward(x, theta, gamma1, gamma2, q_w, q_b, k_w, k_b, v_w, v_b, o_w, o_b, router_w, router_b, sh_w1, sh_b1, sh_w2, sh_b2, re_w1, re_b1, re_w2, re_b2)

    def _L1_attn_ref(hidden_states, q_w, k_w, v_w, b_w, q_cw, k_cw, v_cw, fir_short_w, fir_long_w, mlp1_w, mlp1_b, mlp2_w, mlp2_b, logit_temp, conv_res_logit, norm_w, o_w):
        import jax, jax.numpy as jnp
        import numpy as np
        import math
        B, L, D = (2, 512, 128)
        H, DK, DV = (4, 32, 32)
        CHUNK = 32
        PROB_FLOOR = 0.02

        def _l2norm(x, eps=1e-06):
            return x * jax.lax.rsqrt(jnp.sum(x * x, -1, keepdims=True) + eps)

        def _silu(x):
            return x * jax.nn.sigmoid(x)

        def _short_conv(x, w):
            K = w.shape[-1]
            xp = jnp.pad(x, ((0, 0), (K - 1, 0), (0, 0)))
            y = sum((xp[:, j:j + x.shape[1], :] * w[:, j] for j in range(K)))
            return _silu(y)

        def _fir_conv(x, filt):
            b, l, h, d = x.shape
            K = filt.shape[-1]
            xf = jnp.pad(x.reshape(b, l, h * d).transpose(0, 2, 1), ((0, 0), (0, 0), (K - 1, 0)))
            w = filt.reshape(h * d, 1, K)
            y = jax.lax.conv_general_dilated(xf, w, (1,), 'VALID', dimension_numbers=('NCH', 'OIH', 'NCH'), feature_group_count=h * d)
            return y.transpose(0, 2, 1).reshape(b, l, h, d)

        def _delta_rule_chunkwise(q, k, v, beta, chunk=CHUNK):
            b, h, Lq, dk = q.shape
            dv = v.shape[-1]
            n = Lq // chunk
            q = _l2norm(q)
            k = _l2norm(k)
            v = v * beta[..., None]
            kb = k * beta[..., None]
            rs = lambda t: t.reshape(b, h, n, chunk, t.shape[-1])
            qc, kc, vc, kbc = (rs(q), rs(k), rs(v), rs(kb))
            strict_lower = jnp.tril(jnp.ones((chunk, chunk), bool), -1)
            M = jnp.where(strict_lower, jnp.einsum('bhncd,bhnmd->bhncm', kbc, kc), 0.0)
            eye = jnp.eye(chunk, dtype=q.dtype)
            T = jax.scipy.linalg.solve_triangular(eye + M, jnp.broadcast_to(eye, M.shape), lower=True, unit_diagonal=True)
            u = T @ vc
            w = T @ kbc
            incl_lower = jnp.tril(jnp.ones((chunk, chunk), bool), 0)

            def step(S, xs):
                q_i, k_i, u_i, w_i = xs
                attn = jnp.where(incl_lower, q_i @ k_i.swapaxes(-1, -2), 0.0)
                u_adj = u_i - w_i @ S
                out_i = q_i @ S + attn @ u_adj
                S = S + k_i.swapaxes(-1, -2) @ u_adj
                return (S, out_i)
            S0 = jnp.zeros((b, h, dk, dv), q.dtype)
            xs = tuple((jnp.moveaxis(t, 2, 0) for t in (qc, kc, u, w)))
            S, out = jax.lax.scan(step, S0, xs)
            out = jnp.moveaxis(out, 0, 2).reshape(b, h, Lq, dv)
            return (out, S)

        def _rmsnorm(x, w, eps=1e-05):
            return x * jax.lax.rsqrt(jnp.mean(x * x, -1, keepdims=True) + eps) * w

        def _per_head_stats(x):
            mean = jnp.mean(x, -1, keepdims=True)
            var = jnp.var(x, -1, keepdims=True)
            am = jnp.mean(jnp.abs(x), -1, keepdims=True)
            l2 = jnp.sqrt(jnp.sum(x * x, -1, keepdims=True))
            return jnp.concatenate([mean, var, am, l2], -1)

        def _forward(hidden_states, q_w, k_w, v_w, b_w, q_cw, k_cw, v_cw, fir_short_w, fir_long_w, mlp1_w, mlp1_b, mlp2_w, mlp2_b, logit_temp, conv_res_logit, norm_w, o_w):
            b, l, _ = hidden_states.shape
            q_in = _short_conv(hidden_states @ q_w.T, q_cw)
            k_in = _short_conv(hidden_states @ k_w.T, k_cw)
            v_in = _short_conv(hidden_states @ v_w.T, v_cw)
            q = q_in.reshape(b, l, H, DK)
            k = k_in.reshape(b, l, H, DK)
            v_direct = v_in.reshape(b, l, H, DV)
            beta = jnp.maximum(jax.nn.sigmoid(hidden_states @ b_w.T), 1e-06)
            delta_out, _S = _delta_rule_chunkwise(q.transpose(0, 2, 1, 3), k.transpose(0, 2, 1, 3), v_direct.transpose(0, 2, 1, 3), beta.transpose(0, 2, 1))
            delta_out = delta_out.transpose(0, 2, 1, 3)
            local_short = _fir_conv(v_direct, fir_short_w)
            local_long = _fir_conv(v_direct, fir_long_w)
            stats = jnp.concatenate([_per_head_stats(local_short), _per_head_stats(local_long), _per_head_stats(delta_out), _per_head_stats(v_direct)], -1)
            hs_exp = jnp.broadcast_to(hidden_states[:, :, None, :], (b, l, H, hidden_states.shape[-1]))
            gate_in = jnp.concatenate([hs_exp, stats], -1)
            h1 = jax.nn.gelu(gate_in @ mlp1_w.T + mlp1_b)
            logits = h1 @ mlp2_w.T + mlp2_b
            temp = jax.nn.softplus(logit_temp)
            p = jax.nn.softmax(logits / temp, -1)
            p = jnp.maximum(p, PROB_FLOOR)
            p = p / jnp.sum(p, -1, keepdims=True)
            o = p[..., 0:1] * local_short + p[..., 1:2] * local_long + p[..., 2:3] * delta_out + p[..., 3:4] * v_direct
            o = o + jax.nn.sigmoid(conv_res_logit)[None, None, :, None] * local_short
            o = _rmsnorm(o, norm_w)
            o = o.reshape(b, l, H * DV) @ o_w.T
            return o
        return _forward(hidden_states, q_w, k_w, v_w, b_w, q_cw, k_cw, v_cw, fir_short_w, fir_long_w, mlp1_w, mlp1_b, mlp2_w, mlp2_b, logit_temp, conv_res_logit, norm_w, o_w)

    def _L1_ffn_ref(x, gate_W, W_gate, W_up, W_down):
        import jax, jax.numpy as jnp
        import numpy as np
        EPS = 0.05
        N_ITERS = 20
        TOP_K = 2

        def _sinkhorn(cost, n_iters=N_ITERS, epsilon=EPS):
            la = cost / epsilon
            for _ in range(n_iters):
                la = la - jax.scipy.special.logsumexp(la, axis=-1, keepdims=True)
                la = la - jax.scipy.special.logsumexp(la, axis=-2, keepdims=True)
            return jnp.exp(la)
        B, T, D = x.shape
        xf = x.reshape(B * T, D)
        logits = xf @ gate_W.T
        pi = _sinkhorn(-logits)
        _, top_idx = jax.lax.top_k(pi, TOP_K)
        g = jnp.einsum('nd,efd->enf', xf, W_gate)
        u = jnp.einsum('nd,efd->enf', xf, W_up)
        y = jnp.einsum('enf,edf->end', jax.nn.silu(g) * u, W_down)
        n_ar = jnp.arange(xf.shape[0])
        out = jnp.zeros_like(xf)
        for k in range(TOP_K):
            out = out + y[top_idx[:, k], n_ar] * pi[:, k:k + 1]
        return out.reshape(B, T, D)
    x = L0_attn_x
    xn = _layernorm(x, axis=-1)
    s = _L0_attn_ref(xn, L0_attn_wq, L0_attn_wk, L0_attn_wv, L0_attn_wo)
    g = _silu(_L0_ffn_ref(xn, L0_ffn_positions, L0_ffn_theta, L0_ffn_gamma1, L0_ffn_gamma2, L0_ffn_q_w, L0_ffn_q_b, L0_ffn_k_w, L0_ffn_k_b, L0_ffn_v_w, L0_ffn_v_b, L0_ffn_o_w, L0_ffn_o_b, L0_ffn_router_w, L0_ffn_router_b, L0_ffn_sh_w1, L0_ffn_sh_b1, L0_ffn_sh_w2, L0_ffn_sh_b2, L0_ffn_re_w1, L0_ffn_re_b1, L0_ffn_re_w2, L0_ffn_re_b2))
    x = x + s * g
    xn = _layernorm(x, axis=-1)
    s = _L1_attn_ref(xn, L1_attn_q_w, L1_attn_k_w, L1_attn_v_w, L1_attn_b_w, L1_attn_q_cw, L1_attn_k_cw, L1_attn_v_cw, L1_attn_fir_short_w, L1_attn_fir_long_w, L1_attn_mlp1_w, L1_attn_mlp1_b, L1_attn_mlp2_w, L1_attn_mlp2_b, L1_attn_logit_temp, L1_attn_conv_res_logit, L1_attn_norm_w, L1_attn_o_w)
    g = _silu(_L1_ffn_ref(xn, L1_ffn_gate_W, L1_ffn_W_gate, L1_ffn_W_up, L1_ffn_W_down))
    x = x + s * g
    return x

_drawn_inputs = setup_inputs


def setup_inputs(seed=0):
    import zlib

    import numpy as np

    out = dict(_drawn_inputs(seed))
    spreads = {'L0_ffn_gamma1': (1.0, 0.2),
     'L0_ffn_gamma2': (1.0, 0.559),
     'L0_ffn_q_b': (0.0, 0.8),
     'L0_ffn_k_b': (0.0, 0.8),
     'L0_ffn_v_b': (0.0, 0.574),
     'L0_ffn_o_b': (0.0, 0.351),
     'L0_ffn_router_b': (0.0, 0.8),
     'L0_ffn_sh_b1': (0.0, 0.8),
     'L0_ffn_sh_b2': (0.0, 0.645),
     'L0_ffn_re_b1': (0.0, 0.8),
     'L0_ffn_re_b2': (0.0, 0.8),
     'L1_attn_mlp1_b': (0.0, 2.0),
     'L1_attn_conv_res_logit': (-2.0, 0.6),
     'L1_attn_norm_w': (1.0, 0.6)}
    factors = {'L0_ffn_theta': 8.0,
     'L0_ffn_q_w': 8.0,
     'L0_ffn_k_w': 8.0,
     'L0_ffn_v_w': 4.802,
     'L0_ffn_o_w': 3.028,
     'L0_ffn_router_w': 8.0,
     'L0_ffn_sh_w1': 8.0,
     'L0_ffn_sh_w2': 8.0,
     'L0_ffn_re_w1': 8.0,
     'L0_ffn_re_w2': 8.0,
     'L1_attn_q_w': 64.0,
     'L1_attn_k_w': 64.0,
     'L1_attn_v_w': 58.575,
     'L1_attn_b_w': 64.0,
     'L1_attn_q_cw': 64.0,
     'L1_attn_k_cw': 64.0,
     'L1_attn_v_cw': 62.012,
     'L1_attn_fir_short_w': 64.0,
     'L1_attn_fir_long_w': 64.0,
     'L1_attn_mlp1_w': 64.0,
     'L1_attn_mlp2_w': 8.0,
     'L1_attn_mlp2_b': 57.349,
     'L1_attn_o_w': 56.125,
     'L1_ffn_gate_W': 58.555,
     'L1_ffn_W_gate': 62.731,
     'L1_ffn_W_up': 55.947,
     'L1_ffn_W_down': 56.336}
    for name, (base, spread) in spreads.items():
        noise = np.random.default_rng([zlib.crc32(name.encode()), seed]).standard_normal(out[name].shape)
        drawn = base * np.exp(spread * noise) if base else spread * noise
        out[name] = jnp.asarray(drawn.astype(out[name].dtype))
    for name, factor in factors.items():
        out[name] = (out[name] * factor).astype(out[name].dtype)
    return out
```

```python
from contextlib import ExitStack

import concourse.bass as bass
from concourse import mybir
import numpy as np

F32 = mybir.dt.float32
BF16 = mybir.dt.bfloat16
ALU = mybir.AluOpType
ACT = mybir.ActivationFunctionType
AX = mybir.AxisListType

P = 128
B, S = 8, 512
NB = S // P
NT = B * NB
NEG = -1.0e30
LN_EPS = 1e-5
H0, D0 = 16, 8
GROUPS_Q = (0, 0, 1, 1, 0, 2)
GROUPS_K = (0, 1, 0, 1, 2, 0)
R0 = len(GROUPS_Q) * D0
H1, D1 = 16, 64
NPAIR = H1 // 2
WCOLS = 5 * P + 4

NE, TOPK = 31, 3

HL, CH, KC, KF, KL = 4, 32, 4, 5, 64
NE2, DF, TOPK2, SINKHORN, SK_EPS = 8, 512, 2, 20, 0.05

WIDTHS = [P * (i + 1) for i in range(NB)]


class Chain:

    def __init__(self, eng, sem):
        self.eng, self.sem, self.n = eng, sem, 0

    def restart(self):
        self.eng.sem_clear(self.sem)
        self.n = 0

    def __call__(self, ins):
        self.n += 1
        ins.then_inc(self.sem, 1)
        self.eng.wait_ge(self.sem, self.n)


class Signals:

    def __init__(self, nc, ctx, prefix):
        self.nc, self.prefix, self.handles = nc, prefix, []
        ctx.callback(self.close)

    def __call__(self, name):
        self.handles.append(self.nc.alloc_semaphore(self.prefix + name))
        return self.handles[-1]

    def close(self):
        self.nc.clear_and_free_semaphores(self.handles)
        self.nc.all_engine_barrier()


def after(eng, sem, count):
    if not isinstance(count, int) or count > 0:
        eng.wait_ge(sem, count)


def bc(ap, n, axis=1):
    u = ap.unsqueeze(axis)
    shape = list(u.shape)
    shape[axis] = n
    return u.to_broadcast(shape)



def prepare(nc, d, st):
    with ExitStack() as ctx:
        sb = lambda name, shape, dt=F32: ctx.enter_context(nc.sbuf_tensor("p_" + name, shape, dt))
        ps = [ctx.enter_context(nc.psum_tensor(f"prep_ps{i}", [P, 512], F32)) for i in range(7)]
        sem = Signals(nc, ctx, "p_")
        xs = sb("xs", [P, NB, P])
        xn = sb("xn", [P, NB, P])
        xf = sb("xf", [P, NB, P])
        sq = sb("sq", [P, NB, P])
        stats = sb("stats", [P, NB, 6])
        mv = sb("mv", [P, NB, 2])
        var = sb("var", [P, NB])
        sd = sb("sd", [P, NB])
        rstd = sb("rstd", [P, NB])
        ssq = sb("ssq", [P, NB])
        ms = sb("ms", [P, NB])
        rms = sb("rms", [P, NB])
        rrms = sb("rrms", [P, NB])
        xnT = sb("xnT", [P, 512])
        xfT = sb("xfT", [P, 512])
        w0 = sb("w0", [P, 6 * P])
        gamma = sb("gamma", [P, P])
        ob = sb("ob", [P, P])
        c0 = sb("c0", [P, S])
        s0 = sb("s0", [P, S])
        t1 = [sb(f"t1{i}", [P, S]) for i in range(2)]
        t2 = [sb(f"t2{i}", [P, S]) for i in range(2)]
        rot = [sb(f"rot{i}", [P, S]) for i in range(2)]
        rest = [sb(f"rest{i}", [P, S]) for i in range(2)]
        parts = [sb(f"parts{i}", [P, 3, S], BF16) for i in range(2)]
        theta = sb("theta", [P, 1])
        sign = sb("sign", [P, 1])
        pos = sb("pos", [P, S])
        ang = sb("ang", [P, S])
        turns = sb("turns", [P, S])
        red = sb("red", [P, S])
        over = sb("over", [P, S])
        consts_in, x_in = sem("consts_in"), sem("x_in")
        var_ready, sd_ready, xn_ready, ssq_ready = sem("var_ready"), sem("sd_ready"), sem("xn_ready"), sem("ssq_ready")
        ms_ready, rms_ready, xf_ready, acc_ready = sem("ms_ready"), sem("rms_ready"), sem("xf_ready"), sem("acc_ready")
        xnT_done, xfT_done, xnT_ready, xfT_ready = sem("xnT_done"), sem("xfT_done"), sem("xnT_ready"), sem("xfT_ready")
        qk_done, v_done, v_ready = sem("qk_done"), sem("v_done"), sem("v_ready")
        prod_ready, rot_ready, high_ready, rest_ready = sem("prod_ready"), sem("rot_ready"), sem("high_ready"), sem("rest_ready")
        mid_ready, low_ready, stores = sem("mid_ready"), sem("low_ready"), sem("stores")
        red_ready, sin_ready, dve, masks_ready = sem("red_ready"), sem("sin_ready"), sem("dve_steps"), sem("masks_ready")
        block = ctx.enter_context(nc.Block())
        n_consts = 12

        @block.sync
        def _(sp):
            for dst, src in ((w0[:, :], d["w0"]), (c0[:, :], d["cos0"]), (s0[:, :], d["sin0"]),
                             (st["ident"][:, :], d["ident"]), (st["maskf"][:, 0, :], d["mask_q"]),
                             (st["maskf"][:, 1, :], d["mask_k"]), (theta[:, :], d["theta"]),
                             (sign[:, :], d["sign"]), (st["self"][:, :, :], d["sel"]),
                             (gamma[:, :], d["gamma1"].partition_broadcast(P)),
                             (ob[:, :], d["o_b"].partition_broadcast(P)),
                             (pos[:, :], d["pos"].partition_broadcast(P))):
                sp.dma_start(dst, src).then_inc(consts_in, 16)
            with sp.Fori(0, B) as b:
                sp.wait_ge(xn_ready, b)
                sp.dma_start(xs[:, :, :], d["x"][b, :, :].rearrange("(t p) d -> p t d", p=P)).then_inc(x_in, 16)
                sp.wait_ge(xfT_ready, b + 1)
                sp.dma_start(d["xfT"][b, :, :], xfT[:, :]).then_inc(stores, 16)
                for i in range(2):
                    sp.wait_ge(low_ready, 2 * b + i + 1)
                    sp.dma_start(d["parts"][i, b, :, :, :].rearrange("t p s -> p t s"),
                                 parts[i][:, :, :]).then_inc(stores, 16)
            sp.wait_ge(stores, 48 * B)

        @block.vector
        def _(v):
            step = Chain(v, dve)
            v.wait_ge(consts_in, 16 * n_consts)
            for dst, src in ((st["identb"][:, :], st["ident"][:, :]), (st["maskb"][:, :, :], st["maskf"][:, :, :]),
                             (st["selb"][:, :, :], st["self"][:, :, :])):
                last = nc.vector.tensor_copy(dst, src)
            last.then_inc(masks_ready, 1)
            step(nc.vector.memset(st["v0"][:, :, :, :], 1.0))
            step(nc.vector.tensor_scalar(ang[:, :], pos[:, :], theta[:, 0:1], None, ALU.mult))
            step(nc.vector.tensor_scalar(turns[:, :], ang[:, :], float(1 / (2 * np.pi)), None, ALU.mult))
            step(nc.vector.tensor_scalar(turns[:, :], turns[:, :], 12582912.0, None, ALU.add))
            step(nc.vector.tensor_scalar(turns[:, :], turns[:, :], 12582912.0, None, ALU.subtract))
            c1 = 6.28125
            c2 = float(np.float32(np.round((2 * np.pi - c1) * 2**21) / 2**21))
            c3 = float(2 * np.pi - c1 - c2)
            cur = ang
            for c in (c1, c2, c3):
                step(nc.vector.scalar_tensor_tensor(out=red[:, :], in0=turns[:, :], scalar=-c, in1=cur[:, :],
                                                    op0=ALU.mult, op1=ALU.add))
                cur = red
            pi = float(np.nextafter(np.float32(np.pi), np.float32(0)))
            step(nc.vector.tensor_scalar(ang[:, :], red[:, :], pi, -pi, ALU.min, ALU.max))
            step(nc.vector.tensor_scalar(red[:, :], red[:, :], float(np.pi / 2), None, ALU.add))
            step(nc.vector.tensor_scalar(over[:, :], red[:, :], float(np.pi), float(2 * np.pi), ALU.is_gt, ALU.mult))
            step(nc.vector.tensor_tensor(red[:, :], red[:, :], over[:, :], ALU.subtract))
            nc.vector.tensor_scalar(red[:, :], red[:, :], pi, -pi, ALU.min, ALU.max).then_inc(red_ready, 1)
            v.wait_ge(sin_ready, 1)
            step(nc.vector.tensor_scalar(st["sin1"][:, :], st["sin1"][:, :], sign[:, 0:1], None, ALU.mult))
            with v.Fori(0, B) as b:
                step.restart()
                v.wait_ge(x_in, 16 * b + 16)
                for t in range(NB):
                    last = nc.vector.bn_stats(stats[:, t, :], xs[:, t, :])
                step(last)
                for t in range(NB):
                    last = nc.vector.bn_aggr(mv[:, t, :], stats[:, t, :])
                step(last)
                nc.vector.tensor_scalar(var[:, :], mv[:, :, 1], LN_EPS, None, ALU.add).then_inc(var_ready, 1)
                v.wait_ge(sd_ready, b + 1)
                step(nc.vector.reciprocal(rstd[:, :], sd[:, :]))
                v.wait_ge(xnT_done, b)
                v.wait_ge(ssq_ready, b)
                for t in range(NB):
                    last = nc.vector.tensor_scalar(xn[:, t, :], xs[:, t, :], mv[:, t, 0:1], rstd[:, t:t + 1],
                                                   ALU.subtract, ALU.mult)
                last.then_inc(xn_ready, 1)
                v.wait_ge(ssq_ready, b + 1)
                nc.vector.tensor_scalar(ms[:, :], ssq[:, :], 1.0 / P, LN_EPS, ALU.mult, ALU.add).then_inc(ms_ready, 1)
                v.wait_ge(rms_ready, b + 1)
                step(nc.vector.reciprocal(rrms[:, :], rms[:, :]))
                v.wait_ge(xn_ready, b + 1)
                v.wait_ge(xfT_done, b)
                for t in range(NB):
                    last = nc.vector.scalar_tensor_tensor(out=xf[:, t, :], in0=xn[:, t, :], scalar=rrms[:, t:t + 1],
                                                          in1=gamma[:, :], op0=ALU.mult, op1=ALU.mult)
                last.then_inc(xf_ready, 1)
                v.wait_ge(xf_ready, b + 1)
                nc.vector.tensor_tensor(st["acc"][:, bass.ds(b * NB, NB), :], xf[:, :, :], bc(ob[:, :], NB), ALU.add)\
                    .then_inc(acc_ready, 1)
                for i in range(2):
                    v.wait_ge(qk_done, 2 * b + i + 1)
                    v.wait_ge(rot_ready, 2 * b + i)
                    nc.vector.tensor_tensor(t1[i][:, :], ps[2 + 2 * i][:, :], c0[:, :], ALU.mult)
                    nc.vector.tensor_tensor(t2[i][:, :], ps[3 + 2 * i][:, :], s0[:, :], ALU.mult).then_inc(prod_ready, 1)

        @block.gpsimd
        def _(g):
            with g.Fori(0, B) as b:
                for i in range(2):
                    g.wait_ge(prod_ready, 2 * b + i + 1)
                    nc.gpsimd.tensor_tensor(rot[i][:, :], t1[i][:, :], t2[i][:, :], ALU.add).then_inc(rot_ready, 1)
                    g.wait_ge(high_ready, 2 * b + i + 1)
                    nc.gpsimd.tensor_tensor(rest[i][:, :], rot[i][:, :], parts[i][:, 0, :], ALU.subtract)\
                        .then_inc(rest_ready, 1)
                    g.wait_ge(mid_ready, 2 * b + i + 1)
                    nc.gpsimd.tensor_tensor(parts[i][:, 2, :], rest[i][:, :], parts[i][:, 1, :], ALU.subtract)\
                        .then_inc(low_ready, 1)

        @block.scalar
        def _(a):
            a.wait_ge(red_ready, 1)
            nc.scalar.activation(st["sin1"][:, :], ang[:, :], ACT.Sin)
            nc.scalar.activation(st["cos1"][:, :], red[:, :], ACT.Sin).then_inc(sin_ready, 1)
            with a.Fori(0, B) as b:
                a.wait_ge(var_ready, b + 1)
                nc.scalar.activation(sd[:, :], var[:, :], ACT.Sqrt).then_inc(sd_ready, 1)
                a.wait_ge(xn_ready, b + 1)
                for t in range(NB):
                    last = nc.scalar.activation(sq[:, t, :], xn[:, t, :], ACT.Square, accum_out=ssq[:, t:t + 1])
                last.then_inc(ssq_ready, 1)
                a.wait_ge(ms_ready, b + 1)
                nc.scalar.activation(rms[:, :], ms[:, :], ACT.Sqrt).then_inc(rms_ready, 1)
                a.wait_ge(xnT_done, b + 1)
                a.wait_ge(v_done, b)
                nc.scalar.copy(xnT[:, :], ps[0][:, :]).then_inc(xnT_ready, 1)
                a.wait_ge(xfT_done, b + 1)
                a.wait_ge(stores, 48 * b)
                nc.scalar.copy(xfT[:, :], ps[1][:, :]).then_inc(xfT_ready, 1)
                a.wait_ge(v_done, b + 1)
                nc.scalar.copy(st["v0"][:, bass.ds(b * NB, NB), :, 0:D0],
                               ps[6][:, :].rearrange("p (t h e) -> p t h e", t=NB, h=H0)).then_inc(v_ready, 1)
                for i in range(2):
                    a.wait_ge(rot_ready, 2 * b + i + 1)
                    nc.scalar.copy(parts[i][:, 0, :], rot[i][:, :]).then_inc(high_ready, 1)
                    a.wait_ge(rest_ready, 2 * b + i + 1)
                    nc.scalar.copy(parts[i][:, 1, :], rest[i][:, :]).then_inc(mid_ready, 1)

        @block.tensor
        def _(pe):
            pe.wait_ge(consts_in, 16 * n_consts)
            with pe.Fori(0, B) as b:
                pe.wait_ge(xn_ready, b + 1)
                pe.wait_ge(xnT_ready, b)
                for t in range(NB):
                    last = nc.tensor.transpose(ps[0][:, t * P:(t + 1) * P], xn[:, t, :], st["ident"][:, :])
                last.then_inc(xnT_done, 1)
                pe.wait_ge(xnT_ready, b + 1)
                for i in range(2):
                    pe.wait_ge(prod_ready, 2 * b + i)
                    for k in range(2):
                        j = 2 * i + k
                        last = nc.tensor.matmul(ps[2 + j][:, :], w0[:, j * P:(j + 1) * P], xnT[:, :], start=True, stop=True)
                    last.then_inc(qk_done, 1)
                pe.wait_ge(v_ready, b)
                for t in range(NB):
                    last = nc.tensor.matmul(ps[6][:, t * P:(t + 1) * P], xnT[:, t * P:(t + 1) * P],
                                            w0[:, 4 * P:5 * P], start=True, stop=True)
                last.then_inc(v_done, 1)
                pe.wait_ge(xf_ready, b + 1)
                pe.wait_ge(xfT_ready, b)
                for t in range(NB):
                    last = nc.tensor.transpose(ps[1][:, t * P:(t + 1) * P], xf[:, t, :], st["ident"][:, :])
                last.then_inc(xfT_done, 1)



class Regions:

    def __init__(self, nc, ctx, name):
        self.banks = [ctx.enter_context(nc.psum_tensor(f"{name}{i}", [P, 512], F32)) for i in range(8)]

    def scores(self, r, i):
        b0, b1, b2 = self.banks[3 * r:3 * r + 3]
        return (b1[:, 384:512], b2[:, 0:256], b1[:, 0:384], b0[:, :])[i]

    def shift_rows(self, r):
        return self.banks[3 * r + 2][0:2, 256:512].bitcast(BF16)

    def whole(self, r):
        b0, b1, b2 = self.banks[3 * r:3 * r + 3]
        return b0[:, :], b1[:, :], b2[:, 0:256]


E_AT = [0, 512, 1024, 512 + 384]


def e_cols(j, i):
    at = E_AT[j] + (i - j) * P
    return slice(at, at + P)


def attn0(nc, d, st):
    n_heads = B * H0
    per = 8
    n_quads, rounds = n_heads // 4, n_heads // per
    scale = float(1.0 / np.sqrt(np.float32(D0)))
    with ExitStack() as ctx:
        sb = lambda name, shape, dt=F32: ctx.enter_context(nc.sbuf_tensor("a0_" + name, shape, dt))
        sem = Signals(nc, ctx, "a0_")
        rg = Regions(nc, ctx, "a0_ps")
        oT_ps, o_ps = rg.banks[6:8]
        qs = sb("qs", [P, 2, H0, S], BF16)
        ks = sb("ks", [P, 2, H0, S], BF16)
        shift = [sb(f"shift{i}", [P, NB]) for i in range(2)]
        shift2 = [sb(f"shift2{i}", [P, NB, 2], BF16) for i in range(2)]
        rows = [sb(f"rows{i}", [2, 512], BF16) for i in range(2)]
        e = [sb(f"e{i}", [P, 1280]) for i in range(per)]
        vq = [sb(f"vq{i}", [P, NB, 4, 32]) for i in range(2)]
        oT = [sb(f"oT{i}", [P, S]) for i in range(2)]
        rden = [sb(f"rden{i}", [P, NB, 4]) for i in range(2)]
        zero, vq_zero = sem("zero"), sem("vq_zero")
        stacks_in = [sem("stacks_in0"), sem("stacks_in1")]
        s_part, max_ready, high_ready, shift_ready = sem("s_part"), sem("max_ready"), sem("high_ready"), sem("shift_ready")
        rowsT_done, rows_ready, sT_part, e_part = sem("rowsT_done"), sem("rows_ready"), sem("sT_part"), sem("e_part")
        vq_ready, oT_done, oT_ready, o_done = sem("vq_ready"), sem("oT_done"), sem("oT_ready"), sem("o_done")
        rden_ready, o_ready = sem("rden_ready"), sem("o_ready")
        block = ctx.enter_context(nc.Block())

        def heads(eng, round_):
            round_(0, True, False)
            with eng.Fori(1, rounds - 1) as i:
                round_(i, False, False)
            round_(rounds - 1, False, True)

        @block.sync
        def _(sp):
            def load(b, slot):
                for dst, i, groups in ((qs, 0, GROUPS_Q), (ks, 1, GROUPS_K)):
                    for r, part in enumerate(groups):
                        sp.dma_start(dst[r * D0:(r + 1) * D0, slot, :, :],
                                     d["parts"][i, b, part, :, :].rearrange("(h e) s -> e h s", e=D0))\
                            .then_inc(stacks_in[slot], 16)
            sp.wait_ge(zero, 2)
            load(0, 0)
            load(1, 1)
            with sp.Fori(1, B // 2) as i:
                for slot in range(2):
                    b = 2 * i + slot
                    sp.wait_ge(sT_part, 3 * H0 * (b - 1))
                    load(b, slot)

        @block.gpsimd
        def _(gp):
            nc.gpsimd.memset(qs[:, :, :, :], 0.0).then_inc(zero, 1)
            for s in range(2):
                last = nc.gpsimd.memset(vq[s][:, :, :, :], 0.0)
            last.then_inc(vq_zero, 1)
            gp.wait_ge(vq_zero, 1)

            def copy_v(q, s):
                after(gp, oT_done, q - 1)
                b, h = q // 4, (q % 4) * 4
                nc.gpsimd.tensor_copy(vq[s][:, :, :, 0:D0 + 1], st["v0"][:, bass.ds(b * NB, NB), bass.ds(h, 4), :])\
                    .then_inc(vq_ready, 1)

            for q in range(2):
                copy_v(q, q)
            with gp.Fori(1, n_quads // 2) as i:
                for s in range(2):
                    copy_v(2 * i + s, s)

        @block.tensor
        def _(pe):
            def scores(n, r):
                b, h = n // H0, n % H0
                for part, blocks in enumerate(((3,), (2, 0), (1,))):
                    after(pe, e_part, 3 * (n - 2) + (part + 1))
                    for i in blocks:
                        out = rg.scores(r, i)
                        nc.tensor.matmul(out, qs[:, b % 2, h, i * P:(i + 1) * P], ks[:, b % 2, h, 0:(i + 1) * P],
                                         start=True, stop=False)
                        last = nc.tensor.matmul(out[:, i * P:(i + 1) * P], st["identb"][:, :], st["maskb"][:, 0, :],
                                                start=False, stop=True)
                    last.then_inc(s_part, 1)

            def shift_rows(n, r):
                pe.wait_ge(shift_ready, n + 1)
                for i in range(NB):
                    last = nc.tensor.transpose(rg.shift_rows(r)[:, i * P:(i + 1) * P], shift2[r][:, i, :],
                                               st["identb"][:, :])
                last.then_inc(rowsT_done, 1)

            def transposed(n, r):
                b, h = n // H0, n % H0
                pe.wait_ge(rows_ready, n + 1)
                for blocks in ((0,), (1, 3), (2,)):
                    for j in blocks:
                        out = rg.scores(r, NB - 1 - j)
                        nc.tensor.matmul(out, ks[:, b % 2, h, j * P:(j + 1) * P], qs[:, b % 2, h, j * P:S],
                                         start=True, stop=False)
                        nc.tensor.matmul(out[:, 0:P], st["identb"][:, :], st["maskb"][:, 1, :], start=False, stop=False)
                        last = nc.tensor.matmul(out, st["selb"][0:2, 0, :], rows[r][:, j * P:S], start=False, stop=True)
                    last.then_inc(sT_part, 1)

            def values(q, s):
                pe.wait_ge(e_part, 12 * q + 12)
                pe.wait_ge(vq_ready, q + 1)
                after(pe, oT_ready, q)
                for j in range(NB):
                    for k in range(4):
                        last = nc.tensor.matmul(oT_ps[32 * k:32 * k + 32, j * P:S], vq[s][:, j, k, :],
                                                e[4 * s + k][:, E_AT[j]:E_AT[j] + S - j * P],
                                                start=(j == 0), stop=(j == NB - 1), skip_group_check=True)
                last.then_inc(oT_done, 1)

            def by_token(q, s):
                pe.wait_ge(oT_ready, q + 1)
                after(pe, o_ready, q)
                for t in range(NB):
                    last = nc.tensor.transpose(o_ps[:, t * P:(t + 1) * P], oT[s][:, t * P:(t + 1) * P], st["ident"][:, :])
                last.then_inc(o_done, 1)

            def round_(i, first, last):
                for k in range(per):
                    n, r, q, s = i * per + k, k % 2, 2 * i + k // 4, k // 4
                    shift_rows(n, r)
                    if k == per - 1 and not last:
                        b = (n + 1) // H0
                        pe.wait_ge(stacks_in[0], ((b // 2) + 1) * (12 * 16))
                        pe.wait_ge(stacks_in[1], ((b + 1) // 2) * (12 * 16))
                    if not (k == per - 1 and last):
                        scores(n + 1, 1 - r)
                    transposed(n, r)
                    if k % 4 == 1 and not (first and s == 0):
                        values(q - 1, 1 - s)
                    if k % 4 == 3 and not (first and s == 0):
                        by_token(q - 1, 1 - s)

            pe.wait_ge(stacks_in[0], 12 * 16)
            scores(0, 0)
            heads(pe, round_)
            values(n_quads - 1, 1)
            by_token(n_quads - 1, 1)

        @block.vector
        def _(v):
            def maxima(n, r):
                after(v, rowsT_done, n - 1)
                for part, blocks in enumerate(((3,), (2, 0), (1,))):
                    v.wait_ge(s_part, 3 * n + (part + 1))
                    for i in blocks:
                        last = nc.vector.tensor_reduce(shift[r][:, i:i + 1], rg.scores(r, i), AX.X, ALU.max, negate=True)
                last.then_inc(max_ready, 1)
                v.wait_ge(max_ready, n + 1)
                nc.vector.tensor_copy(shift2[r][:, :, 0], shift[r][:, :]).then_inc(high_ready, 1)
                v.wait_ge(high_ready, n + 1)
                nc.vector.tensor_tensor(shift2[r][:, :, 1], shift[r][:, :], shift2[r][:, :, 0], ALU.subtract)\
                    .then_inc(shift_ready, 1)

            def normed(q, s):
                v.wait_ge(o_done, q + 1)
                b, h = q // 4, (q % 4) * 4
                o = o_ps[:, :].rearrange("p (t h e) -> p t h e", t=NB, h=4)
                nc.vector.reciprocal(rden[s][:, :, :], o[:, :, :, D0]).then_inc(rden_ready, 1)
                v.wait_ge(rden_ready, q + 1)
                out = st["ctx0"][:, bass.ds(b * NB, NB), bass.ds(h * D0, 4 * D0)].rearrange("p t (h e) -> p t h e", h=4)
                nc.vector.tensor_tensor(out, o[:, :, :, 0:D0], bc(rden[s][:, :, :], D0, 3), ALU.mult).then_inc(o_ready, 1)

            def round_(i, first, last):
                for k in range(per):
                    n, r, q, s = i * per + k, k % 2, 2 * i + k // 4, k // 4
                    if not (k == per - 1 and last):
                        maxima(n + 1, 1 - r)
                    if k % 4 == 3 and not (first and s == 0):
                        normed(q - 1, 1 - s)

            nc.vector.memset(ks[:, :, :, :], 0.0).then_inc(zero, 1)
            maxima(0, 0)
            heads(v, round_)
            normed(n_quads - 1, 1)

        @block.scalar
        def _(a):
            def copy_rows(n, r):
                a.wait_ge(rowsT_done, n + 1)
                after(a, sT_part, 3 * (n - 1))
                nc.scalar.copy(rows[r][:, :], rg.shift_rows(r)).then_inc(rows_ready, 1)

            def exps(n, r, k):
                at = 0
                for part, piece in enumerate(rg.whole(r)):
                    a.wait_ge(sT_part, 3 * n + (part + 1))
                    nc.scalar.activation(e[k][:, at:at + piece.shape[1]], piece, ACT.Exp, scale=scale).then_inc(e_part, 1)
                    at += piece.shape[1]

            def copy_values(q, s):
                a.wait_ge(oT_done, q + 1)
                after(a, o_done, q - 1)
                nc.scalar.copy(oT[s][:, :], oT_ps[:, :]).then_inc(oT_ready, 1)

            def round_(i, first, last):
                for k in range(per):
                    n, r, q, s = i * per + k, k % 2, 2 * i + k // 4, k // 4
                    copy_rows(n, r)
                    if k % 4 == 0:
                        after(a, oT_done, q - 1)
                    exps(n, r, k)
                    if k % 4 == 2 and not (first and s == 0):
                        copy_values(q - 1, 1 - s)

            heads(a, round_)
            copy_values(n_quads - 1, 1)


def state(nc, ctx):
    sb = lambda name, shape, dt=F32: ctx.enter_context(nc.sbuf_tensor(name, shape, dt))
    return {
        "ident": sb("ident", [P, P]), "identb": sb("identb", [P, P], BF16),
        "maskf": sb("maskf", [P, 2, P]), "maskb": sb("maskb", [P, 2, P], BF16),
        "self": sb("self", [4, 2, P]), "selb": sb("selb", [4, 2, P], BF16),
        "sin1": sb("sin1", [P, S]), "cos1": sb("cos1", [P, S]),
    }



def attn1(nc, d, st):
    n_pairs = NPAIR * B
    scale = float(1.0 / np.sqrt(D1))
    with ExitStack() as ctx:
        sb = lambda name, shape, dt=F32: ctx.enter_context(nc.sbuf_tensor("a1_" + name, shape, dt))
        sem = Signals(nc, ctx, "a1_")
        two = lambda name, shape, dt=F32: [sb(f"{name}{i}", shape, dt) for i in range(2)]
        rg = Regions(nc, ctx, "a1_ps")
        X, Y = rg.banks[6], rg.banks[7]
        w = two("w", [P, WCOLS])
        wo = two("wo", [P, P])
        vb = two("vb", [1, P])
        xT = two("xT", [P, S])
        qT = two("qT", [P, S])
        kT = [[sb(f"kT{i}{h}", [P, S]) for h in range(2)] for i in range(2)]
        t1 = two("t1", [P, S])
        t2 = two("t2", [P, S])
        va = two("va", [P, NB, 2, D1 + 1])
        shift = two("shift", [P, NB])
        shift2 = two("shift2", [P, NB, 2], BF16)
        rows = two("rows", [2, S], BF16)
        e = two("e", [P, 1280])
        rden = two("rden", [P, NB])
        cx = two("cx", [P, NB, P])
        cxT = two("cxT", [P, S])
        ones = sb("ones", [1, P])
        ones_ready, zero = sem("ones_ready"), sem("zero")
        pair_in = sem("in0"), sem("in1")
        wo_in = sem("wo0"), sem("wo1")
        qk_done, v_done = sem("qk_done"), sem("v_done")
        prod_ready, rot_ready, v_ready = sem("prod_ready"), sem("rot_ready"), sem("v_ready")
        s_part, max_ready, high_ready, shift_ready = sem("s_part"), sem("max_ready"), sem("high_ready"), sem("shift_ready")
        rowsT_done, rows_ready, sT_part, e_part = sem("rowsT_done"), sem("rows_ready"), sem("sT_part"), sem("e_part")
        o_done, rden_ready, cx_ready = sem("o_done"), sem("rden_ready"), sem("cx_ready")
        cxT_done, cxT_ready, y_done, acc_ready = sem("cxT_done"), sem("cxT_ready"), sem("y_done"), sem("acc_ready")
        block = ctx.enter_context(nc.Block())

        def pairs(eng, pair):
            for n in range(3):
                pair(n, n % 2, n == 0, False)
            with eng.Fori(0, (n_pairs - 4) // 2) as i:
                for j in range(2):
                    pair(2 * i + 3 + j, (1 + j) % 2, False, False)
            pair(n_pairs - 1, 1, False, True)

        @block.sync
        def _(sp):
            def load(n, s):
                if not isinstance(n, int):
                    sp.wait_ge(s_part, 6 * n - 11)
                sp.dma_start(w[s][:, :], d["w1"][n // B, :, :]).then_inc(pair_in[s], 16)
                sp.dma_start(vb[s][:, :], d["v_b"][n // B, :, :]).then_inc(pair_in[s], 16)
                sp.dma_start(xT[s][:, :], d["xfT"][n % B, :, :]).then_inc(pair_in[s], 16)

            def load_out(n, s):
                after(sp, y_done, n - 1)
                sp.dma_start(wo[s][:, :], d["wo1"][n // B, :, :]).then_inc(wo_in[s], 16)

            load(0, 0)
            load(1, 1)
            load_out(0, 0)
            with sp.Fori(1, n_pairs // 2) as i:
                for s in range(2):
                    load(2 * i + s, s)
                    load_out(2 * i + s - 1, 1 - s)
            load_out(n_pairs - 1, 1)

        @block.tensor
        def _(pe):
            def project(n, s):
                pe.wait_ge(pair_in[s], ((n // 2) + 1) * 48)
                for c, out in enumerate((X, Y, X, Y)):
                    if c == 0:
                        after(pe, cxT_ready, n - 1)
                    elif c == 1:
                        after(pe, acc_ready, n - 1)
                    else:
                        pe.wait_ge(prod_ready, 4 * n + (c - 1))
                    nc.tensor.matmul(out[:, :], w[s][:, c * P:(c + 1) * P], xT[s][:, :], start=True, stop=True)\
                        .then_inc(qk_done, 1)
                pe.wait_ge(prod_ready, 4 * n + 3)
                for t in range(NB):
                    out = X[:, t * P:(t + 1) * P]
                    nc.tensor.matmul(out, ones[0:1, :], vb[s][:, :], start=True, stop=False)
                    last = nc.tensor.matmul(out, xT[s][:, t * P:(t + 1) * P], w[s][:, 4 * P:5 * P], start=False, stop=True)
                last.then_inc(v_done, 1)

            def scores(g, n, s, h):
                pe.wait_ge(rot_ready, 2 * n + 2)
                for part, blocks in enumerate(((3,), (2, 0), (1,))):
                    after(pe, e_part, 3 * (g - 2) + (part + 1))
                    for i in blocks:
                        out = rg.scores(h, i)
                        nc.tensor.matmul(out, qT[s][:, i * P:(i + 1) * P], kT[s][h][:, 0:(i + 1) * P],
                                         start=True, stop=False)
                        last = nc.tensor.matmul(out[:, i * P:(i + 1) * P], st["identb"][:, :], st["maskb"][:, 0, :],
                                                start=False, stop=True)
                    last.then_inc(s_part, 1)

            def shift_rows(g, h):
                pe.wait_ge(shift_ready, g + 1)
                for i in range(NB):
                    last = nc.tensor.transpose(rg.shift_rows(h)[:, i * P:(i + 1) * P], shift2[h][:, i, :],
                                               st["identb"][:, :])
                last.then_inc(rowsT_done, 1)

            def transposed(g, s, h):
                pe.wait_ge(rows_ready, g + 1)
                for blocks in ((0,), (1, 3), (2,)):
                    for j in blocks:
                        out = rg.scores(h, NB - 1 - j)
                        nc.tensor.matmul(out, kT[s][h][:, j * P:(j + 1) * P], qT[s][:, j * P:S], start=True, stop=False)
                        nc.tensor.matmul(out[:, 0:P], st["identb"][:, :], st["maskb"][:, 1, :], start=False, stop=False)
                        last = nc.tensor.matmul(out, st["selb"][0:2, 0, :], rows[h][:, j * P:S], start=False, stop=True)
                    last.then_inc(sT_part, 1)

            def values(g, n, s, h, last_pair):
                pe.wait_ge(e_part, 3 * g + 3)
                pe.wait_ge(v_ready, n + 1)
                if h == 1:
                    pe.wait_ge(cx_ready, g)
                elif last_pair:
                    pe.wait_ge(acc_ready, n)
                else:
                    pe.wait_ge(prod_ready, 4 * n + 8)
                for i in range(NB):
                    for j in range(i + 1):
                        last = nc.tensor.matmul(Y[:, i * 65:(i + 1) * 65], e[h][:, e_cols(j, i)],
                                                va[s][:, j, h, :], start=(j == 0), stop=(j == i))
                last.then_inc(o_done, 1)

            def context(n, s):
                pe.wait_ge(cx_ready, 2 * n + 2)
                if isinstance(n, int) and n == n_pairs - 1:
                    pe.wait_ge(v_ready, n + 1)
                else:
                    pe.wait_ge(v_ready, n + 2)
                for t in range(NB):
                    last = nc.tensor.transpose(X[:, t * P:(t + 1) * P], cx[s][:, t, :], st["ident"][:, :])
                last.then_inc(cxT_done, 1)

            def output(n, s):
                pe.wait_ge(cxT_ready, n + 1)
                pe.wait_ge(wo_in[s], ((n // 2) + 1) * 16)
                for t in range(NB):
                    last = nc.tensor.matmul(Y[:, t * P:(t + 1) * P], cxT[s][:, t * P:(t + 1) * P],
                                            wo[s][:, :], start=True, stop=True)
                last.then_inc(y_done, 1)

            pe.wait_ge(ones_ready, 1)
            project(0, 0)
            scores(0, 0, 0, 0)

            def pair(n, s, first, last):
                g = 2 * n
                scores(g + 1, n, s, 1)
                shift_rows(g, 0)
                if not first:
                    context(n - 1, 1 - s)
                transposed(g, s, 0)
                if not first:
                    output(n - 1, 1 - s)
                shift_rows(g + 1, 1)
                if not last:
                    project(n + 1, 1 - s)
                transposed(g + 1, s, 1)
                values(g, n, s, 0, last)
                if not last:
                    scores(g + 2, n + 1, 1 - s, 0)
                values(g + 1, n, s, 1, last)

            pairs(pe, pair)
            context(n_pairs - 1, 1)
            output(n_pairs - 1, 1)

        @block.vector
        def _(v):
            def rotate(n, s):
                for c, (src, dst, table) in enumerate(((X, t1[0], "cos1"), (Y, t2[0], "sin1"),
                                                       (X, t1[1], "cos1"), (Y, t2[1], "sin1"))):
                    v.wait_ge(qk_done, 4 * n + (c + 1))
                    after(v, rot_ready, 2 * n + (c // 2) - 1)
                    nc.vector.scalar_tensor_tensor(out=dst[:, :], in0=src[:, :], scalar=w[s][:, 5 * P + c:5 * P + c + 1],
                                                   in1=st[table][:, :], op0=ALU.add, op1=ALU.mult).then_inc(prod_ready, 1)

            def maxima(g, h):
                after(v, rowsT_done, g - 1)
                for part, blocks in enumerate(((3,), (2, 0), (1,))):
                    v.wait_ge(s_part, 3 * g + (part + 1))
                    for i in blocks:
                        last = nc.vector.tensor_reduce(shift[h][:, i:i + 1], rg.scores(h, i), AX.X, ALU.max, negate=True)
                last.then_inc(max_ready, 1)
                v.wait_ge(max_ready, g + 1)
                nc.vector.tensor_copy(shift2[h][:, :, 0], shift[h][:, :]).then_inc(high_ready, 1)
                v.wait_ge(high_ready, g + 1)
                nc.vector.tensor_tensor(shift2[h][:, :, 1], shift[h][:, :], shift2[h][:, :, 0], ALU.subtract)\
                    .then_inc(shift_ready, 1)

            def normed(g, n, s, h):
                v.wait_ge(o_done, g + 1)
                after(v, cxT_done, n - 1)
                o = Y[:, 0:NB * 65].rearrange("p (t e) -> p t e", e=65)
                nc.vector.reciprocal(rden[h][:, :], o[:, :, D1]).then_inc(rden_ready, 1)
                v.wait_ge(rden_ready, g + 1)
                nc.vector.tensor_tensor(cx[s][:, :, h * D1:(h + 1) * D1], o[:, :, 0:D1],
                                        bc(rden[h][:, :], D1, 2), ALU.mult).then_inc(cx_ready, 1)

            def add(n):
                v.wait_ge(y_done, n + 1)
                b = n % B
                at = st["acc"][:, bass.ds(b * NB, NB), :]
                nc.vector.tensor_tensor(at, at, Y[:, :].rearrange("p (t d) -> p t d", d=P), ALU.add).then_inc(acc_ready, 1)

            step = lambda ins, k: (ins.then_inc(ones_ready, 1), v.wait_ge(ones_ready, k))
            for i in range(2):
                nc.vector.memset(va[i][:, :, :, :], 1.0)
            step(nc.vector.memset(ones[:, :], 1.0), 1)
            rotate(0, 0)
            maxima(0, 0)

            def pair(n, s, first, last):
                g = 2 * n
                maxima(g + 1, 1)
                if not first:
                    add(n - 1)
                if not last:
                    rotate(n + 1, 1 - s)
                normed(g, n, s, 0)
                if not last:
                    maxima(g + 2, 0)
                normed(g + 1, n, s, 1)

            pairs(v, pair)
            add(n_pairs - 1)

        @block.gpsimd
        def _(gp):
            def pair(n, s, first, last):
                gp.wait_ge(rot_ready, 2 * n)
                gp.wait_ge(prod_ready, 4 * n + 2)
                after(gp, sT_part, 6 * (n - 1))
                nc.gpsimd.tensor_tensor(qT[s][:, :], t1[0][:, :], t2[0][:, :], ALU.add).then_inc(rot_ready, 1)
                gp.wait_ge(rot_ready, 2 * n + 1)
                gp.wait_ge(prod_ready, 4 * n + 4)
                for h in range(2):
                    hh = slice(h * D1, (h + 1) * D1)
                    last = nc.gpsimd.tensor_tensor(kT[s][h][hh, :], t1[1][hh, :], t2[1][hh, :], ALU.add)
                last.then_inc(rot_ready, 1)

            for s in range(2):
                for h in range(2):
                    last = nc.gpsimd.memset(kT[s][h][:, :], 0.0)
            last.then_inc(zero, 1)
            gp.wait_ge(zero, 1)

            pairs(gp, pair)

        @block.scalar
        def _(a):
            def copy_rows(g, h):
                a.wait_ge(rowsT_done, g + 1)
                after(a, sT_part, 3 * (g - 1))
                nc.scalar.copy(rows[h][:, :], rg.shift_rows(h)).then_inc(rows_ready, 1)

            def exps(g, h):
                after(a, o_done, g - 1)
                at = 0
                for part, piece in enumerate(rg.whole(h)):
                    a.wait_ge(sT_part, 3 * g + (part + 1))
                    nc.scalar.activation(e[h][:, at:at + piece.shape[1]], piece, ACT.Exp, scale=scale).then_inc(e_part, 1)
                    at += piece.shape[1]

            def copy_v(n, s):
                a.wait_ge(v_done, n + 1)
                after(a, o_done, 2 * (n - 1))
                nc.scalar.copy(va[s][:, :, :, 0:D1],
                               X[:, :].rearrange("p (t h e) -> p t h e", t=NB, h=2)).then_inc(v_ready, 1)

            def copy_context(n, s):
                a.wait_ge(cxT_done, n + 1)
                after(a, y_done, n - 1)
                nc.scalar.copy(cxT[s][:, :], X[:, :]).then_inc(cxT_ready, 1)

            a.wait_ge(ones_ready, 1)
            copy_v(0, 0)

            def pair(n, s, first, last):
                g = 2 * n
                copy_rows(g, 0)
                if not first:
                    copy_context(n - 1, 1 - s)
                exps(g, 0)
                copy_rows(g + 1, 1)
                if not last:
                    copy_v(n + 1, 1 - s)
                exps(g + 1, 1)

            pairs(a, pair)
            copy_context(n_pairs - 1, 1)



def route(nc, d, st):
    with ExitStack() as ctx:
        sb = lambda name, shape, dt=F32: ctx.enter_context(nc.sbuf_tensor("r_" + name, shape, dt))
        sem = Signals(nc, ctx, "r_")
        psb = lambda name: ctx.enter_context(nc.psum_tensor("r_" + name, [P, 512], F32))
        anT_ps, lg_ps, g3_ps, gT_ps = psb("anT_ps"), psb("lg_ps"), psb("g3_ps"), psb("gT_ps")
        sq = sb("sq", [P, NB, P])
        ssq, ms, rms, rr = (sb(n, [P, NB]) for n in ("ssq", "ms", "rms", "rr"))
        an = sb("an", [P, NB, P])
        anT = sb("anT", [P, S])
        gamma = sb("gamma", [P, P])
        wr = sb("wr", [P, NE])
        rb = sb("rb", [1, NE])
        ones = sb("ones", [1, P])
        down = sb("down", [P, NE])
        top, den, rden, vmax, kmax = (sb(n, [P, NB]) for n in ("top", "den", "rden", "vmax", "kmax"))
        lg, ex, aff, rem, eq, key, hot, gk, gates, rest = (sb(n, [P, NB, NE]) for n in
                                                           ("lg", "ex", "aff", "rem", "eq", "key", "hot", "gk", "gates", "rest"))
        g3 = sb("g3", [P, NB, 3 * NE], BF16)
        g3T = sb("g3T", [3 * NE, S], BF16)
        gT = sb("gT", [NE, S])
        consts_in, stores, dve, ready = sem("consts_in"), sem("stores"), sem("dve_steps"), sem("ones_ready")
        ssq_ready, ms_ready, rms_ready, an_ready = sem("ssq_ready"), sem("ms_ready"), sem("rms_ready"), sem("an_ready")
        anT_done, anT_ready, lg_done, lg_ready = sem("anT_done"), sem("anT_ready"), sem("lg_done"), sem("lg_ready")
        ex_ready, gates_ready, gT_done, gT_ready = sem("ex_ready"), sem("gates_ready"), sem("gT_done"), sem("gT_ready")
        block = ctx.enter_context(nc.Block())

        @block.sync
        def _(sp):
            for dst, src in ((gamma[:, :], d["gamma2"].partition_broadcast(P)), (wr[:, :], d["router_w"]),
                             (rb[:, :], d["router_b"]), (down[:, :], d["down"].partition_broadcast(P))):
                sp.dma_start(dst, src).then_inc(consts_in, 16)
            with sp.Fori(0, B) as b:
                sp.wait_ge(anT_ready, b + 1)
                sp.dma_start(d["anT"][b, :, :], anT[:, :]).then_inc(stores, 16)
                sp.wait_ge(gT_ready, b + 1)
                sp.dma_start(d["g3T"][b, :, :], g3T[:, :]).then_inc(stores, 16)
                sp.dma_start(d["gT"][b, :, :], gT[:, :]).then_inc(stores, 16)
            sp.wait_ge(stores, 48 * B)

        @block.vector
        def _(v):
            step = Chain(v, dve)
            nc.vector.memset(ones[:, :], 1.0).then_inc(ready, 1)
            v.wait_ge(consts_in, 64)
            with v.Fori(0, B) as b:
                step.restart()
                at = st["acc"][:, bass.ds(b * NB, NB), :]
                v.wait_ge(ssq_ready, b + 1)
                nc.vector.tensor_scalar(ms[:, :], ssq[:, :], 1.0 / P, LN_EPS, ALU.mult, ALU.add).then_inc(ms_ready, 1)
                v.wait_ge(rms_ready, b + 1)
                step(nc.vector.reciprocal(rr[:, :], rms[:, :]))
                v.wait_ge(anT_done, b)
                for t in range(NB):
                    last = nc.vector.scalar_tensor_tensor(out=an[:, t, :], in0=st["acc"][:, b * NB + t, :],
                                                          scalar=rr[:, t:t + 1], in1=gamma[:, :],
                                                          op0=ALU.mult, op1=ALU.mult)
                last.then_inc(an_ready, 1)
                v.wait_ge(an_ready, b + 1)
                nc.vector.tensor_tensor(at, at, an[:, :, :], ALU.add)
                v.wait_ge(lg_done, b + 1)
                z = lg_ps[:, 0:NB * NE].rearrange("p (t e) -> p t e", e=NE)
                step(nc.vector.tensor_reduce(top[:, :], z, AX.X, ALU.max))
                nc.vector.tensor_tensor(lg[:, :, :], z, bc(top[:, :], NE, 2), ALU.subtract).then_inc(lg_ready, 1)
                v.wait_ge(ex_ready, b + 1)
                step(nc.vector.tensor_reduce(den[:, :], ex[:, :, :], AX.X, ALU.add))
                step(nc.vector.reciprocal(rden[:, :], den[:, :]))
                step(nc.vector.tensor_tensor(rem[:, :, :], ex[:, :, :], bc(rden[:, :], NE, 2), ALU.mult))
                for k in range(TOPK):
                    step(nc.vector.tensor_reduce(vmax[:, :], rem[:, :, :], AX.X, ALU.max))
                    step(nc.vector.tensor_tensor(eq[:, :, :], rem[:, :, :], bc(vmax[:, :], NE, 2), ALU.is_equal))
                    step(nc.vector.tensor_tensor(key[:, :, :], eq[:, :, :], bc(down[:, :], NB), ALU.mult))
                    step(nc.vector.tensor_reduce(kmax[:, :], key[:, :, :], AX.X, ALU.max))
                    step(nc.vector.tensor_tensor(hot[:, :, :], key[:, :, :], bc(kmax[:, :], NE, 2), ALU.is_equal))
                    if k == 0:
                        v.wait_ge(gT_done, b)
                        step(nc.vector.tensor_tensor(gates[:, :, :], hot[:, :, :], bc(vmax[:, :], NE, 2), ALU.mult))
                    else:
                        step(nc.vector.tensor_tensor(gk[:, :, :], hot[:, :, :], bc(vmax[:, :], NE, 2), ALU.mult))
                        step(nc.vector.tensor_tensor(gates[:, :, :], gates[:, :, :], gk[:, :, :], ALU.add))
                    if k < TOPK - 1:
                        step(nc.vector.scalar_tensor_tensor(out=rem[:, :, :], in0=hot[:, :, :], scalar=-4.0,
                                                            in1=rem[:, :, :], op0=ALU.mult, op1=ALU.add))
                hi, mid, lo = (g3[:, :, i * NE:(i + 1) * NE] for i in range(3))
                step(nc.vector.tensor_copy(hi, gates[:, :, :]))
                step(nc.vector.tensor_tensor(rest[:, :, :], gates[:, :, :], hi, ALU.subtract))
                step(nc.vector.tensor_copy(mid, rest[:, :, :]))
                nc.vector.tensor_tensor(lo, rest[:, :, :], mid, ALU.subtract).then_inc(gates_ready, 1)

        @block.scalar
        def _(a):
            with a.Fori(0, B) as b:
                for t in range(NB):
                    last = nc.scalar.activation(sq[:, t, :], st["acc"][:, b * NB + t, :], ACT.Square,
                                                accum_out=ssq[:, t:t + 1])
                last.then_inc(ssq_ready, 1)
                a.wait_ge(ms_ready, b + 1)
                nc.scalar.activation(rms[:, :], ms[:, :], ACT.Sqrt).then_inc(rms_ready, 1)
                a.wait_ge(anT_done, b + 1)
                a.wait_ge(lg_done, b)
                a.wait_ge(stores, 48 * b)
                nc.scalar.copy(anT[:, :], anT_ps[:, :]).then_inc(anT_ready, 1)
                a.wait_ge(lg_ready, b + 1)
                nc.scalar.activation(ex[:, :, :], lg[:, :, :], ACT.Exp).then_inc(ex_ready, 1)
                a.wait_ge(gT_done, b + 1)
                nc.scalar.copy(g3T[:, :], g3_ps[0:3 * NE, 0:S // 2].bitcast(BF16))
                nc.scalar.copy(gT[:, :], gT_ps[0:NE, :]).then_inc(gT_ready, 1)

        @block.tensor
        def _(pe):
            pe.wait_ge(consts_in, 64)
            pe.wait_ge(ready, 1)
            with pe.Fori(0, B) as b:
                pe.wait_ge(an_ready, b + 1)
                pe.wait_ge(anT_ready, b)
                for t in range(NB):
                    last = nc.tensor.transpose(anT_ps[:, t * P:(t + 1) * P], an[:, t, :], st["ident"][:, :])
                last.then_inc(anT_done, 1)
                pe.wait_ge(anT_ready, b + 1)
                pe.wait_ge(lg_ready, b)
                for t in range(NB):
                    out = lg_ps[:, t * NE:(t + 1) * NE]
                    nc.tensor.matmul(out, ones[0:1, :], rb[:, :], start=True, stop=False)
                    last = nc.tensor.matmul(out, anT[:, t * P:(t + 1) * P], wr[:, :], start=False, stop=True)
                last.then_inc(lg_done, 1)
                pe.wait_ge(gates_ready, b + 1)
                pe.wait_ge(gT_ready, b)
                for t in range(NB):
                    nc.tensor.transpose(g3_ps[0:3 * NE, 64 * t:64 * t + 64].bitcast(BF16), g3[:, t, :], st["identb"][:, :])
                    last = nc.tensor.transpose(gT_ps[0:NE, t * P:(t + 1) * P], gates[:, t, :], st["ident"][:, :])
                last.then_inc(gT_done, 1)


def experts(nc, d, st):
    n_exp = NE + 1
    per = 2 * n_exp
    with ExitStack() as ctx:
        sb = lambda name, shape, dt=F32: ctx.enter_context(nc.sbuf_tensor("x_" + name, shape, dt))
        sem = Signals(nc, ctx, "x_")
        psb = lambda name: ctx.enter_context(nc.psum_tensor("x_" + name, [P, 512], F32))
        two = lambda name, shape, dt=F32: [sb(f"{name}{i}", shape, dt) for i in range(2)]
        h_ps, g_ps, y_ps = ([psb(f"{n}{i}") for i in range(2)] for n in ("h_ps", "g_ps", "y_ps"))
        w = two("w", [P, 2 * P + 1])
        b2 = sb("b2", [NE, P])
        sh_b2 = sb("sh_b2", [P, 1])
        sel = sb("sel", [3 * NE, NE, P], BF16)
        self_ = sb("self", [3 * NE, NE, P])
        sel_ready = sem("sel_ready")
        anT = two("anT", [P, S])
        g3T = two("g3T", [3 * NE, S], BF16)
        gT = two("gT", [NE, S])
        h = two("h", [P, S])
        hg = two("hg", [P, S])
        y = two("y", [P, S])
        consts_in, stores = sem("consts_in"), sem("stores")
        seq_in = [sem(f"seq_in{i}") for i in range(2)]
        w_in = [sem(f"w_in{i}") for i in range(2)]
        h_done, h_ready, hg_ready = sem("h_done"), sem("h_ready"), sem("hg_ready")
        used = [sem(f"used{i}") for i in range(2)]
        y_done, y_ready = sem("y_done"), sem("y_ready")
        block = ctx.enter_context(nc.Block())
        half = n_exp // 2

        number = lambda r, i, k, q: r * per + i * 4 + (2 * k + q)
        routed = lambda r, i, k, q: r * (per - 2) + i * 4 + (2 * k + q - 2)

        def rounds(eng, unit, head=None, tail=None):
            with eng.Fori(0, B // 2) as r:
                if head:
                    head(r)
                for k in range(2):
                    for q in range(2):
                        unit(r, 0, k, q)
                with eng.Fori(1, half) as i:
                    for k in range(2):
                        for q in range(2):
                            unit(r, i, k, q)
                if tail:
                    tail(r)

        def wait_used_before(eng, r, i, k, q):
            first = isinstance(i, int)
            if k == 1:
                eng.wait_ge(used[0], r * (2 * half) + i * 2 + (q + 1))
            elif first:
                eng.wait_ge(used[1], r * (2 * half))
            else:
                eng.wait_ge(used[1], r * (2 * half) + i * 2 + (q - 1))

        @block.sync
        def _(sp):
            for dst, src in ((b2[:, :], d["b2"]), (sh_b2[:, :], d["sh_b2"]),
                             (self_[:, :, :], d["sel_e"])):
                sp.dma_start(dst, src).then_inc(consts_in, 16)
            with sp.Fori(0, B // 2) as r:
                sp.wait_ge(y_ready, r * 2)
                for q in range(2):
                    for dst, name in ((anT, "anT"), (g3T, "g3T"), (gT, "gT")):
                        sp.dma_start(dst[q][:, :], d[name][r * 2 + q, :, :]).then_inc(seq_in[q], 16)
                with sp.Fori(0, half) as i:
                    for k in range(2):
                        sp.wait_ge(used[k], r * (2 * half) + i * 2)
                        sp.dma_start(w[k][:, :], d["w2"][i * 2 + k, :, :]).then_inc(w_in[k], 16)
                for q in range(2):
                    sp.wait_ge(y_ready, r * 2 + (q + 1))
                    sp.dma_start(d["yT"][r * 2 + q, :, :], y[q][:, :]).then_inc(stores, 16)
            sp.wait_ge(stores, 16 * B)

        @block.tensor
        def _(pe):
            pe.wait_ge(consts_in, 48)
            pe.wait_ge(sel_ready, 1)

            def first_product(r, i, k, q):
                first = isinstance(i, int) and k == 0
                if q == 0:
                    pe.wait_ge(w_in[k], r * (16 * half) + i * 16 + 16)
                pe.wait_ge(h_ready, r * per if first else number(r, i, k, q) - 1)
                last = nc.tensor.matmul(h_ps[q][:, :], w[k][:, 0:P], anT[q][:, :], start=True, stop=True)
                if not first:
                    if k == 1 and isinstance(i, int):
                        pe.wait_ge(hg_ready, r * (per - 2))
                    else:
                        pe.wait_ge(hg_ready, routed(r, i, k, q) - 1)
                    last = nc.tensor.matmul(g_ps[q][:, :], sel[:, i * 2 + (k - 1), :], g3T[q][:, :], start=True, stop=True)
                last.then_inc(h_done, 1)

            def second_product(r, i, k, q):
                first = isinstance(i, int) and k == 0
                if first:
                    pe.wait_ge(h_ready, r * per + (q + 1))
                else:
                    pe.wait_ge(hg_ready, routed(r, i, k, q) + 1)
                nc.tensor.matmul(y_ps[q][:, :], w[k][:, P:2 * P], (h if first else hg)[q][:, :], start=first, stop=False)\
                    .then_inc(used[k], 1)

            def head(r):
                for q in range(2):
                    pe.wait_ge(seq_in[q], r * 48 + 48)
                pe.wait_ge(y_ready, r * 2)

            def unit(r, i, k, q):
                first_product(r, i, k, q)
                if q == 1:
                    second_product(r, i, k, 0)
                elif k == 1:
                    second_product(r, i, 0, 1)
                elif not isinstance(i, int):
                    pe.wait_ge(hg_ready, routed(r, i, 0, 0))
                    nc.tensor.matmul(y_ps[1][:, :], w[1][:, P:2 * P], hg[1][:, :], start=False, stop=False)\
                        .then_inc(used[1], 1)

            def tail(r):
                second_product(r, half - 1, 1, 1)
                for q in range(2):
                    last = nc.tensor.matmul(y_ps[q][:, :], b2[:, :], gT[q][:, :], start=False, stop=True)
                last.then_inc(y_done, 1)

            rounds(pe, unit, head, tail)

        @block.scalar
        def _(a):
            a.wait_ge(consts_in, 48)

            def unit(r, i, k, q):
                a.wait_ge(h_done, number(r, i, k, q) + 1)
                if isinstance(i, int):
                    if k == 1:
                        a.wait_ge(used[0], r * (2 * half) + (q + 1))
                    else:
                        a.wait_ge(hg_ready, r * (per - 2))
                else:
                    a.wait_ge(hg_ready, routed(r, i, k, q) - 1)
                nc.scalar.activation(h[q][:, :], h_ps[q][:, :], ACT.Gelu, bias=w[k][:, 2 * P:2 * P + 1])\
                    .then_inc(h_ready, 1)

            rounds(a, unit)

        @block.vector
        def _(v):
            v.wait_ge(consts_in, 48)
            nc.vector.tensor_copy(sel[:, :, :], self_[:, :, :]).then_inc(sel_ready, 1)

            def unit(r, i, k, q):
                if isinstance(i, int) and k == 0:
                    return
                v.wait_ge(h_ready, number(r, i, k, q) + 1)
                wait_used_before(v, r, i, k, q)
                nc.vector.tensor_tensor(hg[q][:, :], h[q][:, :], g_ps[q][:, :], ALU.mult).then_inc(hg_ready, 1)

            def tail(r):
                v.wait_ge(y_done, r + 1)
                v.wait_ge(stores, r * 32)
                for q in range(2):
                    nc.vector.tensor_scalar(y[q][:, :], y_ps[q][:, :], sh_b2[:, 0:1], None, ALU.add).then_inc(y_ready, 1)

            rounds(v, unit, None, tail)



def join0(nc, d, st):
    with ExitStack() as ctx:
        sb = lambda name, shape, dt=F32: ctx.enter_context(nc.sbuf_tensor("j_" + name, shape, dt))
        sem = Signals(nc, ctx, "j_")
        psb = lambda name: ctx.enter_context(nc.psum_tensor("j_" + name, [P, 512], F32))
        y_ps, cT_ps, s_ps, hT_ps = psb("y_ps"), psb("cT_ps"), psb("s_ps"), psb("hT_ps")
        wo = sb("wo", [P, P])
        yT = sb("yT", [P, S])
        xs, cs, f, g, t, hs, x1 = (sb(n, [P, NB, P]) for n in ("xs", "cs", "f", "g", "t", "hs", "x1"))
        cT = sb("cT", [P, S])
        stats = sb("stats", [P, NB, 6])
        mv = sb("mv", [P, NB, 2])
        var, sd, rstd = (sb(n, [P, NB]) for n in ("var", "sd", "rstd"))
        w_in, tile_in = sem("w_in"), sem("tile_in")
        y_done, cT_done, s_done, hT_done = sem("y_done"), sem("cT_done"), sem("s_done"), sem("hT_done")
        cs_ready, cT_ready, f_ready, g_ready = sem("cs_ready"), sem("cT_ready"), sem("f_ready"), sem("g_ready")
        x_ready, var_ready, sd_ready, hs_ready, hT_ready = (sem(n) for n in
                                                            ("x_ready", "var_ready", "sd_ready", "hs_ready", "hT_ready"))
        dve, kept = sem("dve_steps"), sem("kept")
        block = ctx.enter_context(nc.Block())

        @block.sync
        def _(sp):
            sp.dma_start(wo[:, :], d["w0"][:, 5 * P:6 * P]).then_inc(w_in, 16)
            with sp.Fori(0, B) as b:
                sp.wait_ge(x_ready, b)
                sp.dma_start(yT[:, :], d["yT"][b, :, :]).then_inc(tile_in, 16)
                sp.dma_start(xs[:, :, :], d["x"][b, :, :].rearrange("(t p) d -> p t d", p=P)).then_inc(tile_in, 16)

        @block.gpsimd
        def _(gp):
            with gp.Fori(0, B) as b:
                gp.wait_ge(cT_done, b)
                nc.gpsimd.tensor_copy(cs[:, :, :], st["ctx0"][:, bass.ds(b * NB, NB), :]).then_inc(cs_ready, 1)

        @block.tensor
        def _(pe):
            pe.wait_ge(w_in, 16)
            with pe.Fori(0, B) as b:
                pe.wait_ge(tile_in, b * 32 + 32)
                pe.wait_ge(f_ready, b)
                for k in range(NB):
                    last = nc.tensor.transpose(y_ps[:, k * P:(k + 1) * P], yT[:, k * P:(k + 1) * P], st["ident"][:, :])
                last.then_inc(y_done, 1)
                pe.wait_ge(cs_ready, b + 1)
                pe.wait_ge(cT_ready, b)
                for k in range(NB):
                    last = nc.tensor.transpose(cT_ps[:, k * P:(k + 1) * P], cs[:, k, :], st["ident"][:, :])
                last.then_inc(cT_done, 1)
                pe.wait_ge(cT_ready, b + 1)
                pe.wait_ge(x_ready, b)
                for k in range(NB):
                    last = nc.tensor.matmul(s_ps[:, k * P:(k + 1) * P], cT[:, k * P:(k + 1) * P], wo[:, :],
                                            start=True, stop=True)
                last.then_inc(s_done, 1)
                pe.wait_ge(hs_ready, b + 1)
                pe.wait_ge(hT_ready, b)
                for k in range(NB):
                    last = nc.tensor.transpose(hT_ps[:, k * P:(k + 1) * P], hs[:, k, :], st["ident"][:, :])
                last.then_inc(hT_done, 1)

        @block.vector
        def _(v):
            step = Chain(v, dve)
            with v.Fori(0, B) as b:
                step.restart()
                at = st["acc"][:, bass.ds(b * NB, NB), :]
                tiles = lambda ap: ap.rearrange("p (t d) -> p t d", d=P)
                v.wait_ge(y_done, b + 1)
                v.wait_ge(g_ready, b)
                nc.vector.tensor_tensor(f[:, :, :], tiles(y_ps[:, :]), at, ALU.add).then_inc(f_ready, 1)
                v.wait_ge(g_ready, b + 1)
                v.wait_ge(s_done, b + 1)
                step(nc.vector.tensor_tensor(t[:, :, :], tiles(s_ps[:, :]), g[:, :, :], ALU.mult))
                v.wait_ge(tile_in, b * 32 + 32)
                v.wait_ge(kept, b)
                nc.vector.tensor_tensor(x1[:, :, :], t[:, :, :], xs[:, :, :], ALU.add).then_inc(x_ready, 1)
                v.wait_ge(x_ready, b + 1)
                for k in range(NB):
                    last = nc.vector.bn_stats(stats[:, k, :], x1[:, k, :])
                step(last)
                for k in range(NB):
                    last = nc.vector.bn_aggr(mv[:, k, :], stats[:, k, :])
                step(last)
                nc.vector.tensor_scalar(var[:, :], mv[:, :, 1], LN_EPS, None, ALU.add).then_inc(var_ready, 1)
                v.wait_ge(sd_ready, b + 1)
                step(nc.vector.reciprocal(rstd[:, :], sd[:, :]))
                v.wait_ge(hT_done, b)
                for k in range(NB):
                    last = nc.vector.tensor_scalar(hs[:, k, :], x1[:, k, :], mv[:, k, 0:1],
                                                   rstd[:, k:k + 1], ALU.subtract, ALU.mult)
                last.then_inc(hs_ready, 1)

        @block.scalar
        def _(a):
            with a.Fori(0, B) as b:
                a.wait_ge(cT_done, b + 1)
                a.wait_ge(s_done, b)
                nc.scalar.copy(cT[:, :], cT_ps[:, :]).then_inc(cT_ready, 1)
                a.wait_ge(f_ready, b + 1)
                a.wait_ge(x_ready, b)
                nc.scalar.activation(g[:, :, :], f[:, :, :], ACT.Silu).then_inc(g_ready, 1)
                a.wait_ge(x_ready, b + 1)
                nc.scalar.copy(st["acc"][:, bass.ds(b * NB, NB), :], x1[:, :, :]).then_inc(kept, 1)
                a.wait_ge(var_ready, b + 1)
                nc.scalar.activation(sd[:, :], var[:, :], ACT.Sqrt).then_inc(sd_ready, 1)
                a.wait_ge(hT_done, b + 1)
                nc.scalar.copy(st["hsT"][:, bass.ds(b * S, S)], hT_ps[:, :]).then_inc(hT_ready, 1)


def project1(nc, d, st):
    with ExitStack() as ctx:
        sb = lambda name, shape, dt=F32: ctx.enter_context(nc.sbuf_tensor("q_" + name, shape, dt))
        sem = Signals(nc, ctx, "q_")
        ps = [ctx.enter_context(nc.psum_tensor(f"q_ps{i}", [P, 512], F32)) for i in range(8)]
        w = sb("w", [P, 3 * P + HL])
        cw = sb("cw", [P, 3, KC])
        fw = sb("fw", [P, KF])
        lead = 16
        pre = [sb(f"pre{i}", [P, lead + S]) for i in range(3)]
        conv = [sb(f"conv{i}", [P, S]) for i in range(3)]
        hT = sb("hT", [P, S])
        qT, kT = sb("qT", [P, S]), sb("kT", [P, S])
        vT = sb("vT", [P, lead + S])
        shT = sb("shT", [P, S])
        sq = sb("sq", [P, 2, S])
        beta = sb("beta", [P, NB, HL])
        ss, rt, rn = (sb(n, [P, 2, NB * HL]) for n in ("ss", "rt", "rn"))
        qn, kn, kb, vb = (sb(n, [P, NB, P]) for n in ("qn", "kn", "kb", "vb"))
        nT = [sb(f"nT{i}", [P, S]) for i in range(3)]
        m = sb("m", [P, HL, NB, P])
        mask = sb("mask", [P, P])
        consts_in, stores, dve = sem("consts_in"), sem("stores"), sem("dve_steps")
        hT_ready, proj_done, pre_ready, conv_ready, silu_ready = (sem(n) for n in
            ("hT_ready", "proj_done", "pre_ready", "conv_ready", "silu_ready"))
        short_ready, tok_done, sq_ready, ss_ready, rt_ready = (sem(n) for n in
            ("short_ready", "tok_done", "sq_ready", "ss_ready", "rt_ready"))
        beta_done, norm_ready, nT_done, nT_ready = (sem(n) for n in
            ("beta_done", "norm_ready", "nT_done", "nT_ready"))
        m_done, m_ready, sh_done, vd_ready = sem("m_done"), sem("m_ready"), sem("sh_done"), sem("vd_ready")
        sg_ready, zero = sem("sg_ready"), sem("zero")
        block = ctx.enter_context(nc.Block())
        n_stores = 5 + NB * HL

        @block.sync
        def _(sp):
            for dst, src in ((w[:, :], d["w3"]), (cw[:, :, :], d["cw"]), (fw[:, :], d["fir_short"]),
                             (mask[:, :], d["mask_m"])):
                sp.dma_start(dst, src).then_inc(consts_in, 16)
            with sp.Fori(0, B) as b:
                sp.wait_ge(norm_ready, b + 1)
                for i, src in enumerate((kn, kb, vb)):
                    sp.dma_start(d["tok"][i, b, :, :, :].rearrange("t p c -> p t c"), src[:, :, :]).then_inc(stores, 16)
                sp.wait_ge(nT_ready, b + 1)
                for i in range(2):
                    sp.dma_start(d["chan"][i, b, :, :], nT[i][:, :]).then_inc(stores, 16)
                sp.wait_ge(m_ready, b + 1)
                for h in range(HL):
                    for c in range(NB):
                        cc = slice(c * CH, (c + 1) * CH)
                        sp.dma_start(d["m"][b, h, :, c, :, :].rearrange("t i j -> i t j"), m[cc, h, :, cc])\
                            .then_inc(stores, 16)
            sp.wait_ge(stores, 16 * n_stores * B)

        @block.gpsimd
        def _(gp):
            for t in pre + [vT]:
                nc.gpsimd.memset(t[:, 0:lead], 0.0)
            for b in range(B):
                last = nc.gpsimd.memset(st["vd"][:, b * (NB + 1), :], 0.0)
            last.then_inc(zero, 1)
            with gp.Fori(0, B) as b:
                gp.wait_ge(beta_done, b)
                nc.gpsimd.tensor_copy(hT[:, :], st["hsT"][:, bass.ds(b * S, S)]).then_inc(hT_ready, 1)

        @block.tensor
        def _(pe):
            pe.wait_ge(consts_in, 64)
            with pe.Fori(0, B) as b:
                pe.wait_ge(hT_ready, b + 1)
                pe.wait_ge(m_ready, b)
                for i in range(3):
                    nc.tensor.matmul(ps[i][:, :], w[:, i * P:(i + 1) * P], hT[:, :], start=True, stop=True)\
                        .then_inc(proj_done, 1)
                for t in range(NB):
                    last = nc.tensor.matmul(ps[3][:, t * HL:(t + 1) * HL], hT[:, t * P:(t + 1) * P],
                                            w[:, 3 * P:3 * P + HL], start=True, stop=True)
                last.then_inc(beta_done, 1)
                pe.wait_ge(nT_ready, b)
                for i, src in enumerate((qT[:, :], kT[:, :], vT[:, lead:lead + S])):
                    pe.wait_ge(silu_ready, b * 3 + (i + 1))
                    for t in range(NB):
                        last = nc.tensor.transpose(ps[4 + i][:, t * P:(t + 1) * P], src[:, t * P:(t + 1) * P],
                                                   st["ident"][:, :])
                last.then_inc(tok_done, 1)
                pe.wait_ge(short_ready, b + 1)
                pe.wait_ge(vd_ready, b)
                for t in range(NB):
                    last = nc.tensor.transpose(ps[7][:, t * P:(t + 1) * P], shT[:, t * P:(t + 1) * P], st["ident"][:, :])
                last.then_inc(sh_done, 1)
                pe.wait_ge(norm_ready, b + 1)
                pe.wait_ge(vd_ready, b + 1)
                for i, src in enumerate((qn, kn, kb)):
                    for t in range(NB):
                        last = nc.tensor.transpose(ps[4 + i][:, t * P:(t + 1) * P], src[:, t, :], st["ident"][:, :])
                last.then_inc(nT_done, 1)
                pe.wait_ge(nT_ready, b + 1)
                pe.wait_ge(sg_ready, b + 1)
                for h in range(HL):
                    hh = slice(h * CH, (h + 1) * CH)
                    for t in range(NB):
                        tt = slice(t * P, (t + 1) * P)
                        last = nc.tensor.matmul(ps[h][:, tt], nT[2][hh, tt], nT[1][hh, tt], start=True, stop=True)
                last.then_inc(m_done, 1)

        @block.vector
        def _(v):
            step = Chain(v, dve)
            v.wait_ge(consts_in, 64)
            v.wait_ge(zero, 1)
            with v.Fori(0, B) as b:
                step.restart()
                for i in range(3):
                    v.wait_ge(pre_ready, b * 3 + (i + 1))
                    v.wait_ge(silu_ready, b * 3)
                    x = lambda j: pre[i][:, lead - KC + 1 + j:lead - KC + 1 + j + S]
                    step(nc.vector.tensor_scalar(conv[i][:, :], x(0), cw[:, i, 0:1], None, ALU.mult))
                    for j in range(1, KC):
                        op = nc.vector.scalar_tensor_tensor(out=conv[i][:, :], in0=x(j), scalar=cw[:, i, j:j + 1],
                                                            in1=conv[i][:, :], op0=ALU.mult, op1=ALU.add)
                        if j < KC - 1:
                            step(op)
                        else:
                            op.then_inc(conv_ready, 1)
                v.wait_ge(silu_ready, b * 3 + 3)
                v.wait_ge(sh_done, b)
                x = lambda j: vT[:, lead - KF + 1 + j:lead - KF + 1 + j + S]
                step(nc.vector.tensor_scalar(shT[:, :], x(0), fw[:, 0:1], None, ALU.mult))
                for j in range(1, KF):
                    op = nc.vector.scalar_tensor_tensor(out=shT[:, :], in0=x(j), scalar=fw[:, j:j + 1],
                                                        in1=shT[:, :], op0=ALU.mult, op1=ALU.add)
                    if j < KF - 1:
                        step(op)
                    else:
                        op.then_inc(short_ready, 1)
                v.wait_ge(sq_ready, b + 1)
                step(nc.vector.tensor_reduce(ss[:, :, :], sq[:, :, :].rearrange("p i (g e) -> p i g e", e=CH),
                                             AX.X, ALU.add))
                nc.vector.tensor_scalar(ss[:, :, :], ss[:, :, :], 1e-6, None, ALU.add).then_inc(ss_ready, 1)
                v.wait_ge(rt_ready, b + 1)
                step(nc.vector.reciprocal(rn[:, :, :], rt[:, :, :]))
                v.wait_ge(sg_ready, b + 1)
                step(nc.vector.tensor_scalar(beta[:, :, :], beta[:, :, :], 1e-6, None, ALU.max))
                v.wait_ge(nT_done, b)
                v.wait_ge(stores, b * (16 * n_stores))
                heads = lambda ap: ap.rearrange("p (g e) -> p g e", e=CH)
                flat = lambda ap: ap.rearrange("p t (h e) -> p (t h) e", e=CH)
                betas = bc(beta[:, :, :].rearrange("p t h -> p (t h)"), CH, 2)
                nc.vector.tensor_tensor(flat(qn[:, :, :]), heads(ps[4][:, :]), bc(rn[:, 0, :], CH, 2), ALU.mult)
                nc.vector.tensor_tensor(flat(vb[:, :, :]), heads(ps[6][:, :]), betas, ALU.mult)
                step(nc.vector.tensor_tensor(flat(kn[:, :, :]), heads(ps[5][:, :]), bc(rn[:, 1, :], CH, 2), ALU.mult))
                nc.vector.tensor_tensor(flat(kb[:, :, :]), flat(kn[:, :, :]), betas, ALU.mult).then_inc(norm_ready, 1)
                v.wait_ge(m_done, b + 1)
                for h in range(HL):
                    last = nc.vector.tensor_tensor(m[:, h, :, :], ps[h][:, :].rearrange("p (t j) -> p t j", j=P),
                                                   bc(mask[:, :], NB), ALU.mult)
                last.then_inc(m_ready, 1)

        @block.scalar
        def _(a):
            with a.Fori(0, B) as b:
                for i in range(3):
                    a.wait_ge(proj_done, b * 3 + (i + 1))
                    a.wait_ge(conv_ready, b * 3)
                    nc.scalar.copy(pre[i][:, lead:], ps[i][:, :]).then_inc(pre_ready, 1)
                a.wait_ge(beta_done, b + 1)
                nc.scalar.activation(beta[:, :, :], ps[3][:, 0:NB * HL].rearrange("p (t h) -> p t h", h=HL), ACT.Sigmoid)\
                    .then_inc(sg_ready, 1)
                for i, dst in enumerate((qT[:, :], kT[:, :], vT[:, lead:lead + S])):
                    a.wait_ge(conv_ready, b * 3 + (i + 1))
                    a.wait_ge(tok_done, b)
                    a.wait_ge(short_ready, b)
                    nc.scalar.activation(dst, conv[i][:, :], ACT.Silu).then_inc(silu_ready, 1)
                a.wait_ge(tok_done, b + 1)
                for i in range(2):
                    last = nc.scalar.activation(sq[:, i, :], ps[4 + i][:, :], ACT.Square)
                last.then_inc(sq_ready, 1)
                a.wait_ge(ss_ready, b + 1)
                nc.scalar.activation(rt[:, :, :], ss[:, :, :], ACT.Sqrt).then_inc(rt_ready, 1)
                a.wait_ge(norm_ready, b + 1)
                tiles = lambda ap: ap.rearrange("p (t c) -> p t c", c=P)
                nc.scalar.copy(st["vd"][:, bass.ds(b * 5 + 1, NB), :], tiles(ps[6][:, :]))
                a.wait_ge(sh_done, b + 1)
                nc.scalar.copy(st["short"][:, bass.ds(b * NB, NB), :], tiles(ps[7][:, :])).then_inc(vd_ready, 1)
                a.wait_ge(nT_done, b + 1)
                a.wait_ge(m_done, b)
                a.wait_ge(stores, b * (16 * n_stores))
                for i in range(3):
                    last = nc.scalar.copy(nT[i][:, :], ps[4 + i][:, :])
                last.then_inc(nT_ready, 1)



def long_filter(nc, d, st):
    per = 8
    n = P // per
    with ExitStack() as ctx:
        sb = lambda name, shape, dt=F32: ctx.enter_context(nc.sbuf_tensor("l_" + name, shape, dt))
        sem = Signals(nc, ctx, "l_")
        ps = [ctx.enter_context(nc.psum_tensor(f"l_ps{i}", [P, 512], F32)) for i in range(2)]
        band = [sb(f"band{i}", [P, per, P + KL]) for i in range(2)]
        flip = sb("flip", [P, P])
        back = sb("back", [P, B * (NB + 1), P])
        flip_in, back_done, back_ready = sem("flip_in"), sem("back_done"), sem("back_ready")
        cuts = B * (NB + 1) * P // 512
        piece = lambda ap, i: ap[:, i * 4:(i + 1) * 4, :].rearrange("p t c -> p (t c)")
        band_in = [sem(f"band_in{i}") for i in range(2)]
        done, ready = sem("done"), sem("ready")
        taps = bass.AP(d["fir_long"].tensor, 0, [[per * 3 * P, n], [1, P], [3 * P, per], [1, P + KL]])
        block = ctx.enter_context(nc.Block())

        @block.sync
        def _(sp):
            sp.dma_start(flip[:, :], d["flip"]).then_inc(flip_in, 16)
            for s in range(2):
                sp.dma_start(band[s][:, :, :], taps[s, :, :, :]).then_inc(band_in[s], 16)
            with sp.Fori(1, n // 2) as i:
                for s in range(2):
                    sp.wait_ge(done, i * 2 + (s - 1))
                    sp.dma_start(band[s][:, :, :], taps[i * 2 + s, :, :, :]).then_inc(band_in[s], 16)

        @block.tensor
        def _(pe):
            pe.wait_ge(flip_in, 16)
            for i in range(cuts):
                if i >= 2:
                    pe.wait_ge(back_ready, i - 1)
                nc.tensor.matmul(ps[i % 2][:, :], flip[:, :], piece(st["vd"], i), start=True, stop=True).then_inc(back_done, 1)
            pe.wait_ge(back_ready, cuts)
            tiles = back[:, :, :].rearrange("p (b t) c -> p b t c", t=NB + 1)
            with pe.Fori(0, n // 2) as i:
                for s in range(2):
                    pe.wait_ge(band_in[s], i * 16 + 16)
                    pe.wait_ge(ready, i * 2)
                    for k in range(per):
                        c = i * (2 * per) + (s * per + k)
                        out = ps[s][:, k * NT:(k + 1) * NT]
                        nc.tensor.matmul(out, band[s][:, k, 0:P], tiles[:, :, 1:NB + 1, c], start=True, stop=False,
                                         skip_group_check=True)
                        last = nc.tensor.matmul(out[0:KL, :], band[s][:, k, P:P + KL], tiles[:, :, 0:NB, c],
                                                start=False, stop=True, skip_group_check=True)
                    last.then_inc(done, 1)

        @block.vector
        def _(v):
            for i in range(cuts):
                v.wait_ge(back_done, i + 1)
                nc.vector.tensor_copy(piece(back, i), ps[i % 2][:, :]).then_inc(back_ready, 1)
            with v.Fori(0, n // 2) as i:
                for s in range(2):
                    v.wait_ge(done, i * 2 + (s + 1))
                    nc.vector.tensor_copy(st["long"][:, :, bass.ds(i * (2 * per) + s * per, per)],
                                          ps[s][:, 0:per * NT].rearrange("p (c t) -> p t c", t=NT)).then_inc(ready, 1)


def solve(nc, d, st):
    with ExitStack() as ctx:
        sb = lambda name, shape, dt=F32: ctx.enter_context(nc.sbuf_tensor("s_" + name, shape, dt))
        sem = Signals(nc, ctx, "s_")
        m = sb("m", [P, NB, CH, CH])
        inv = sb("inv", [P, NB, CH, CH])
        prod = sb("prod", [P, NB, CH, CH])
        m_in, stored, dve, ready = sem("m_in"), sem("stored"), sem("dve_steps"), sem("ready")
        block = ctx.enter_context(nc.Block())

        @block.sync
        def _(sp):
            sp.dma_start(m[:, :, :, :], d["m"].rearrange("b h t c i j -> (b h t) c i j")).then_inc(m_in, 16)
            sp.wait_ge(ready, 1)
            sp.dma_start(d["t"].rearrange("b h t c m j -> (b h t) c m j"), inv[:, :, :, :]).then_inc(stored, 16)
            sp.wait_ge(stored, 16)

        @block.vector
        def _(v):
            step = Chain(v, dve)
            step(nc.vector.memset(inv[:, :, :, :], 0.0))
            diag = inv[:, :, :, :].rearrange("p c m j -> p c (m j)")[:, :, 0:CH * CH:CH + 1]
            step(nc.vector.memset(diag, 1.0))
            v.wait_ge(m_in, 16)
            for i in range(1, CH):
                row = bc(m[:, :, i, 0:i], i, 2)
                step(nc.vector.tensor_tensor(prod[:, :, 0:i, 0:i], inv[:, :, 0:i, 0:i], row, ALU.mult))
                last = nc.vector.tensor_reduce(inv[:, :, 0:i, i], prod[:, :, 0:i, 0:i], AX.X, ALU.add)
                if i < CH - 1:
                    step(last)
            last.then_inc(ready, 1)


def scan(nc, d, st):
    with ExitStack() as ctx:
        sb = lambda name, shape, dt=F32: ctx.enter_context(nc.sbuf_tensor("c_" + name, shape, dt))
        sem = Signals(nc, ctx, "c_")
        ps = [ctx.enter_context(nc.psum_tensor(f"c_ps{i}", [P, 512], F32)) for i in range(8)]
        A, WS, DS, OUT = ps[0:2], ps[2:4], ps[4:6], ps[6:8]
        inv = sb("inv", [P, B * HL, P])
        kn, kb, vb = (sb(n, [P, B, P]) for n in ("kn", "kb", "vb"))
        qT, kT = sb("qT", [P, B, P]), sb("kT", [P, B, P])
        u, wT, ua = (sb(n, [P, B, P]) for n in ("u", "wT", "ua"))
        at = sb("at", [P, HL, B, P])
        state_ = sb("state", [P, B, P])
        mask = sb("mask", [P, P])
        hmask = sb("hmask", [P, P])
        zeros = sb("zeros", [1, 512])
        consts_in, zero, tile_in = sem("consts_in"), sem("zero"), sem("tile_in")
        u_done, u_ready, w_done, w_ready = sem("u_done"), sem("u_ready"), sem("w_done"), sem("w_ready")
        at_done, at_ready, ws_done, ua_ready = sem("at_done"), sem("at_ready"), sem("ws_done"), sem("ua_ready")
        ds_done, state_ready, out_done, out_ready = sem("ds_done"), sem("state_ready"), sem("out_done"), sem("out_ready")
        block = ctx.enter_context(nc.Block())
        half = B // 2

        @block.sync
        def _(sp):
            sp.dma_start(mask[:, :], d["mask_a"]).then_inc(consts_in, 16)
            sp.dma_start(hmask[:, :], d["mask_h"]).then_inc(consts_in, 16)
            sp.wait_ge(zero, 1)
            with sp.Fori(0, NB) as t:
                sp.wait_ge(out_done, t)
                for i, dst in enumerate((kn, kb, vb)):
                    sp.dma_start(dst[:, :, :], d["tok"][i, :, t, :, :].rearrange("b p c -> p b c")).then_inc(tile_in, 16)
                for i, dst in enumerate((qT, kT)):
                    sp.dma_start(dst[:, :, :], d["chan"][i, :, :, bass.ds(t * P, P)].rearrange("b c s -> c b s"))\
                        .then_inc(tile_in, 16)
                for c in range(NB):
                    cc = slice(c * CH, (c + 1) * CH)
                    sp.dma_start(inv[cc, :, cc], d["t"][:, :, t, c, :, :].rearrange("b h m j -> m (b h) j"))\
                        .then_inc(tile_in, 16)

        @block.gpsimd
        def _(gp):
            nc.gpsimd.memset(zeros[:, :], 0.0)
            nc.gpsimd.memset(state_[:, :, :], 0.0)
            nc.gpsimd.memset(inv[:, :, :], 0.0).then_inc(zero, 1)

        @block.tensor
        def _(pe):
            pe.wait_ge(zero, 1)

            def clear(banks):
                for bank in banks:
                    nc.tensor.matmul(bank[:, :], zeros[0:1, 0:P], zeros[0:1, :], start=True, stop=False,
                                     skip_group_check=True)

            clear(DS)
            with pe.Fori(0, NB) as t:
                pe.wait_ge(tile_in, t * (9 * 16) + 9 * 16)
                pe.wait_ge(at_ready, t * HL * 2)
                for b in range(B):
                    for h in range(HL):
                        hh = slice(h * CH, (h + 1) * CH)
                        at_ = (b % half) * P
                        last = nc.tensor.matmul(A[b // half][:, at_ + h * CH:at_ + (h + 1) * CH],
                                                inv[:, b * HL + h, :], vb[:, b, hh], start=True, stop=True)
                last.then_inc(u_done, 1)
                pe.wait_ge(u_ready, t + 1)
                for b in range(B):
                    for h in range(HL):
                        hh = slice(h * CH, (h + 1) * CH)
                        at_ = (b % half) * P
                        last = nc.tensor.matmul(A[b // half][hh, at_:at_ + P], kb[:, b, hh], inv[:, b * HL + h, :],
                                                start=True, stop=True)
                last.then_inc(w_done, 1)
                pe.wait_ge(w_ready, t + 1)
                for k in range(HL * 2):
                    h, s = k // 2, k % 2
                    hh = slice(h * CH, (h + 1) * CH)
                    if k >= 2:
                        pe.wait_ge(at_ready, t * (HL * 2) + (k - 1))
                    for i in range(half):
                        last = nc.tensor.matmul(A[s][:, i * P:(i + 1) * P], kT[hh, s * half + i, :],
                                                qT[hh, s * half + i, :], start=True, stop=True)
                    last.then_inc(at_done, 1)
                pe.wait_ge(out_ready, t)
                clear(OUT)
                for c in range(NB):
                    cc = slice(c * CH, (c + 1) * CH)
                    pe.wait_ge(state_ready, t * NB + c)
                    for b in range(B):
                        last = nc.tensor.matmul(WS[b // half][cc, (b % half) * P:(b % half + 1) * P],
                                                wT[:, b, cc], state_[:, b, :], start=True, stop=True)
                    last.then_inc(ws_done, 1)
                    for b in range(B):
                        nc.tensor.matmul(OUT[b // half][cc, (b % half) * P:(b % half + 1) * P],
                                         qT[:, b, cc], state_[:, b, :], start=False, stop=False, skip_group_check=True)
                    pe.wait_ge(ua_ready, t * NB + (c + 1))
                    for b in range(B):
                        last = nc.tensor.matmul(DS[b // half][:, (b % half) * P:(b % half + 1) * P],
                                                kn[cc, b, :], ua[cc, b, :], start=False, stop=False,
                                                skip_group_check=True)
                    last.then_inc(ds_done, 1)
                pe.wait_ge(at_ready, t * (HL * 2) + HL * 2)
                for b in range(B):
                    for h in range(HL):
                        hh = slice(h * CH, (h + 1) * CH)
                        at_ = (b % half) * P
                        last = nc.tensor.matmul(OUT[b // half][:, at_ + h * CH:at_ + (h + 1) * CH], at[:, h, b, :],
                                                ua[:, b, hh], start=False, stop=False, skip_group_check=True)
                last.then_inc(out_done, 1)

        @block.vector
        def _(v):
            v.wait_ge(consts_in, 32)
            v.wait_ge(zero, 1)
            seqs = lambda bank: bank[:, :].rearrange("p (b c) -> p b c", c=P)
            with v.Fori(0, NB) as t:
                v.wait_ge(out_done, t)
                for k in range(HL * 2):
                    h, s = k // 2, k % 2
                    v.wait_ge(at_done, t * (HL * 2) + (k + 1))
                    nc.vector.tensor_tensor(at[:, h, s * half:(s + 1) * half, :], seqs(A[s]), bc(mask[:, :], half), ALU.mult)\
                        .then_inc(at_ready, 1)
                for c in range(NB):
                    cc = slice(c * CH, (c + 1) * CH)
                    v.wait_ge(ws_done, t * NB + (c + 1))
                    v.wait_ge(u_ready, t + 1)
                    for s in range(2):
                        last = nc.vector.tensor_tensor(ua[cc, s * half:(s + 1) * half, :], u[cc, s * half:(s + 1) * half, :],
                                                       seqs(WS[s])[cc, :, :], ALU.subtract)
                    last.then_inc(ua_ready, 1)
                    v.wait_ge(ds_done, t * NB + (c + 1))
                    for s in range(2):
                        last = nc.vector.tensor_tensor(state_[:, s * half:(s + 1) * half, :], seqs(DS[s]),
                                                       bc(hmask[:, :], half), ALU.mult)
                    last.then_inc(state_ready, 1)

        @block.scalar
        def _(a):
            seqs = lambda bank: bank[:, :].rearrange("p (b c) -> p b c", c=P)
            with a.Fori(0, NB) as t:
                a.wait_ge(u_done, t + 1)
                a.wait_ge(ua_ready, t * NB)
                for s in range(2):
                    last = nc.scalar.copy(u[:, s * half:(s + 1) * half, :], seqs(A[s]))
                last.then_inc(u_ready, 1)
                a.wait_ge(w_done, t + 1)
                a.wait_ge(out_done, t)
                for s in range(2):
                    last = nc.scalar.copy(wT[:, s * half:(s + 1) * half, :], seqs(A[s]))
                last.then_inc(w_ready, 1)
                a.wait_ge(out_done, t + 1)
                for s in range(2):
                    tiles = st["delta"][:, :, :].rearrange("p (b t) c -> p b t c", t=NB)
                    last = nc.scalar.copy(tiles[:, s * half:(s + 1) * half, t, :], seqs(OUT[s]))
                last.then_inc(out_ready, 1)



def gate1(nc, d, st):
    G = NB * HL
    with ExitStack() as ctx:
        sb = lambda name, shape, dt=F32: ctx.enter_context(nc.sbuf_tensor("g_" + name, shape, dt))
        sem = Signals(nc, ctx, "g_")
        ps = [ctx.enter_context(nc.psum_tensor(f"g_ps{i}", [P, 512], F32)) for i in range(8)]
        w1 = sb("w1", [P, (1 + HL) * P])
        w2 = sb("w2", [P, 4])
        wo = sb("wo", [P, P])
        b1 = sb("b1", [P, 1])
        b2 = sb("b2", [1, 4])
        ones = sb("ones", [1, P])
        nw = sb("nw", [P, CH])
        temp, res = sb("temp", [P, 4]), sb("res", [P, HL])
        x = sb("x", [P, 4, S])
        hT = sb("hT", [P, S])
        dev, sq, dsq = (sb(n, [P, 4, S]) for n in ("dev", "sq", "dsq"))
        sums, mean, l2 = (sb(n, [P, 4 * G]) for n in ("sums", "mean", "l2"))
        stat = sb("stat", [P, NB, HL, CH])
        statT = sb("statT", [P, S])
        h1 = [sb(f"h1{i}", [P, S]) for i in range(2)]
        z, ez, pr = (sb(n, [P, G, 4]) for n in ("z", "ez", "pr"))
        top, den, rden, rs = (sb(n, [P, G]) for n in ("top", "den", "rden", "rs"))
        mix, o, on, osq = (sb(n, [P, S]) for n in ("mix", "o", "on", "osq"))
        rt = sb("rt", [P, G])
        oT = sb("oT", [P, S])
        consts_in, zero, dve, act = sem("consts_in"), sem("zero"), sem("dve_steps"), sem("act_steps")
        temp0_ready, temp1_ready, temp2_ready = sem("temp0"), sem("temp1"), sem("temp2")
        x_ready, dev_ready, sq_ready, l2_ready = sem("x_ready"), sem("dev_ready"), sem("sq_ready"), sem("l2_ready")
        sum_ready, stat_ready, statT_done, statT_ready = (sem(n) for n in ("sum_ready", "stat_ready", "statT_done", "statT_ready"))
        h_done, h_ready, z_part, z_ready, ez_ready = (sem(n) for n in ("h_done", "h_ready", "z_part", "z_ready", "ez_ready"))
        o_ready, osq_ready, ms_ready, rt_ready, on_ready = (sem(n) for n in ("o_ready", "osq_ready", "ms_ready", "rt_ready", "on_ready"))
        oT_done, oT_ready, y_done, y_ready = (sem(n) for n in ("oT_done", "oT_ready", "y_done", "y_ready"))
        block = ctx.enter_context(nc.Block())
        groups = lambda ap: ap.rearrange("p (g e) -> p g e", e=CH)

        @block.sync
        def _(sp):
            for dst, src in ((w1[:, :], d["mlp1"]), (w2[:, :], d["mlp2"]), (wo[:, :], d["wo3"]),
                             (b1[:, :], d["mlp1_b"]), (b2[:, :], d["mlp2_b"]),
                             (nw[:, :], d["norm_w"].partition_broadcast(P)),
                             (temp[:, 0:1], d["temp"].partition_broadcast(P)),
                             (res[:, :], d["res"].partition_broadcast(P))):
                sp.dma_start(dst, src).then_inc(consts_in, 16)

        @block.gpsimd
        def _(gp):
            nc.gpsimd.memset(ones[:, :], 1.0)
            nc.gpsimd.memset(stat[:, :, :, :], 0.0).then_inc(zero, 1)
            with gp.Fori(0, B) as b:
                gp.wait_ge(o_ready, b)
                gp.wait_ge(h_done, b * HL)
                for dst, src in ((0, "short"), (1, "long"), (2, "delta")):
                    nc.gpsimd.tensor_copy(x[:, dst, :].rearrange("p (t c) -> p t c", c=P),
                                          st[src][:, bass.ds(b * NB, NB), :])
                nc.gpsimd.tensor_copy(x[:, 3, :].rearrange("p (t c) -> p t c", c=P),
                                      st["vd"][:, bass.ds(b * (NB + 1) + 1, NB), :])
                nc.gpsimd.tensor_copy(hT[:, :], st["hsT"][:, bass.ds(b * S, S)]).then_inc(x_ready, 1)

        @block.vector
        def _(v):
            step = Chain(v, dve)
            v.wait_ge(consts_in, 8 * 16)
            v.wait_ge(zero, 1)
            step(nc.vector.tensor_scalar(temp[:, 1:2], temp[:, 0:1], -1.0, None, ALU.mult))
            nc.vector.tensor_tensor(temp[:, 1:2], temp[:, 1:2], temp[:, 0:1], ALU.min).then_inc(temp0_ready, 1)
            v.wait_ge(temp1_ready, 1)
            step(nc.vector.tensor_scalar(temp[:, 3:4], temp[:, 0:1], 0.0, None, ALU.max))
            step(nc.vector.tensor_tensor(temp[:, 2:3], temp[:, 2:3], temp[:, 3:4], ALU.add))
            step(nc.vector.reciprocal(temp[:, 3:4], temp[:, 2:3]))
            with v.Fori(0, B) as b:
                step.restart()
                v.wait_ge(x_ready, b + 1)
                v.wait_ge(statT_done, b)
                v.wait_ge(osq_ready, b)
                every = x[:, :, :].rearrange("p i (g e) -> p (i g) e", e=CH)
                many = lambda ap: ap.rearrange("p i (g e) -> p (i g) e", e=CH)
                out = lambda k: stat[:, :, :, k:4 * 4:4].rearrange("p t h i -> p i (t h)")
                branch = lambda ap: ap.rearrange("p (i g) -> p i g", i=4)
                step(nc.vector.tensor_reduce(sums[:, :], every, AX.X, ALU.add))
                step(nc.vector.tensor_scalar(mean[:, :], sums[:, :], 1.0 / CH, None, ALU.mult))
                nc.vector.tensor_tensor(many(dev[:, :, :]), every, bc(mean[:, :], CH, 2), ALU.subtract)\
                    .then_inc(dev_ready, 1)
                nc.vector.tensor_copy(out(0), branch(mean[:, :]))
                step(nc.vector.tensor_reduce(sums[:, :], every, AX.X, ALU.add, apply_absolute_value=True))
                step(nc.vector.tensor_scalar(out(2), branch(sums[:, :]), 1.0 / CH, None, ALU.mult))
                v.wait_ge(sq_ready, b * 2 + 1)
                nc.vector.tensor_reduce(l2[:, :], many(sq[:, :, :]), AX.X, ALU.add).then_inc(sum_ready, 1)
                v.wait_ge(sq_ready, b * 2 + 2)
                step(nc.vector.tensor_reduce(sums[:, :], many(dsq[:, :, :]), AX.X, ALU.add))
                step(nc.vector.tensor_scalar(out(1), branch(sums[:, :]), 1.0 / CH, None, ALU.mult))
                v.wait_ge(l2_ready, b + 1)
                nc.vector.tensor_copy(out(3), branch(l2[:, :])).then_inc(stat_ready, 1)
                v.wait_ge(z_part, b * HL + HL)
                zp = ps[4][:, 0:4 * G].rearrange("p (t h k) -> p (t h) k", h=HL, k=4)
                step(nc.vector.tensor_scalar(z[:, :, :], zp, temp[:, 3:4], None, ALU.mult))
                step(nc.vector.tensor_reduce(top[:, :], z[:, :, :], AX.X, ALU.max))
                nc.vector.tensor_tensor(z[:, :, :], z[:, :, :], bc(top[:, :], 4, 2), ALU.subtract).then_inc(z_ready, 1)
                v.wait_ge(ez_ready, b + 1)
                step(nc.vector.tensor_reduce(den[:, :], ez[:, :, :], AX.X, ALU.add))
                step(nc.vector.reciprocal(rden[:, :], den[:, :]))
                step(nc.vector.tensor_tensor(pr[:, :, :], ez[:, :, :], bc(rden[:, :], 4, 2), ALU.mult))
                step(nc.vector.tensor_scalar(pr[:, :, :], pr[:, :, :], 0.02, None, ALU.max))
                step(nc.vector.tensor_reduce(den[:, :], pr[:, :, :], AX.X, ALU.add))
                step(nc.vector.reciprocal(rden[:, :], den[:, :]))
                step(nc.vector.tensor_tensor(pr[:, :, :], pr[:, :, :], bc(rden[:, :], 4, 2), ALU.mult))
                p0 = pr[:, :, 0].rearrange("p (t h) -> p t h", h=HL)
                v.wait_ge(temp2_ready, 1)
                step(nc.vector.tensor_tensor(p0, p0, bc(res[:, :], NB), ALU.add))
                v.wait_ge(osq_ready, b)
                for i in range(4):
                    dst = o if i == 0 else mix
                    step(nc.vector.tensor_tensor(groups(dst[:, :]), groups(x[:, i, :]), bc(pr[:, :, i], CH, 2), ALU.mult))
                    if i:
                        last = nc.vector.tensor_tensor(o[:, :], o[:, :], mix[:, :], ALU.add)
                        if i < 3:
                            step(last)
                last.then_inc(o_ready, 1)
                v.wait_ge(osq_ready, b + 1)
                step(nc.vector.tensor_reduce(rs[:, :], groups(osq[:, :]), AX.X, ALU.add))
                nc.vector.tensor_scalar(rs[:, :], rs[:, :], 1.0 / CH, LN_EPS, ALU.mult, ALU.add).then_inc(ms_ready, 1)
                v.wait_ge(rt_ready, b + 1)
                step(nc.vector.reciprocal(rden[:, :], rt[:, :]))
                v.wait_ge(oT_done, b)
                step(nc.vector.tensor_tensor(groups(on[:, :]), groups(o[:, :]), bc(rden[:, :], CH, 2), ALU.mult))
                nc.vector.tensor_tensor(groups(on[:, :]), groups(on[:, :]), bc(nw[:, :], G), ALU.mult).then_inc(on_ready, 1)

        @block.scalar
        def _(a):
            a.wait_ge(temp0_ready, 1)
            nc.scalar.activation(temp[:, 2:3], temp[:, 1:2], ACT.Exp).then_inc(act, 1)
            a.wait_ge(act, 1)
            nc.scalar.activation(temp[:, 2:3], temp[:, 2:3], ACT.Ln, bias=1.0).then_inc(temp1_ready, 1)
            nc.scalar.activation(res[:, :], res[:, :], ACT.Sigmoid).then_inc(temp2_ready, 1)
            with a.Fori(0, B) as b:
                a.wait_ge(x_ready, b + 1)
                nc.scalar.activation(sq[:, :, :], x[:, :, :], ACT.Square).then_inc(sq_ready, 1)
                a.wait_ge(dev_ready, b + 1)
                nc.scalar.activation(dsq[:, :, :], dev[:, :, :], ACT.Square).then_inc(sq_ready, 1)
                a.wait_ge(sum_ready, b + 1)
                nc.scalar.activation(l2[:, :], l2[:, :], ACT.Sqrt).then_inc(l2_ready, 1)
                a.wait_ge(statT_done, b + 1)
                a.wait_ge(h_done, b * HL)
                nc.scalar.copy(statT[:, :], ps[0][:, :]).then_inc(statT_ready, 1)
                for h in range(HL):
                    a.wait_ge(h_done, b * HL + (h + 1))
                    if h >= 2:
                        a.wait_ge(z_part, b * HL + (h - 1))
                    else:
                        a.wait_ge(z_part, b * HL)
                    nc.scalar.activation(h1[h % 2][:, :], ps[1 + h % 2][:, :], ACT.Gelu_apprx_tanh, bias=b1[:, 0:1])\
                        .then_inc(h_ready, 1)
                a.wait_ge(z_ready, b + 1)
                nc.scalar.activation(ez[:, :, :], z[:, :, :], ACT.Exp).then_inc(ez_ready, 1)
                a.wait_ge(o_ready, b + 1)
                a.wait_ge(ms_ready, b)
                nc.scalar.activation(osq[:, :], o[:, :], ACT.Square).then_inc(osq_ready, 1)
                a.wait_ge(ms_ready, b + 1)
                nc.scalar.activation(rt[:, :], rs[:, :], ACT.Sqrt).then_inc(rt_ready, 1)
                a.wait_ge(oT_done, b + 1)
                a.wait_ge(y_done, b)
                nc.scalar.copy(oT[:, :], ps[5][:, :]).then_inc(oT_ready, 1)
                a.wait_ge(y_done, b + 1)
                nc.scalar.copy(st["s1"][:, bass.ds(b * NB, NB), :], ps[6][:, :].rearrange("p (t d) -> p t d", d=P))\
                    .then_inc(y_ready, 1)

        @block.tensor
        def _(pe):
            pe.wait_ge(consts_in, 8 * 16)
            pe.wait_ge(zero, 1)
            with pe.Fori(0, B) as b:
                pe.wait_ge(stat_ready, b + 1)
                pe.wait_ge(statT_ready, b)
                for t in range(NB):
                    last = nc.tensor.transpose(ps[0][:, t * P:(t + 1) * P], stat[:, t, :, :].rearrange("p h k -> p (h k)"),
                                               st["ident"][:, :])
                last.then_inc(statT_done, 1)
                pe.wait_ge(statT_ready, b + 1)

                def logits(h):
                    pe.wait_ge(h_ready, b * HL + (h + 1))
                    if h == 0:
                        pe.wait_ge(z_ready, b)
                    for t in range(NB):
                        out = ps[4][:, (t * HL + h) * 4:(t * HL + h) * 4 + 4]
                        nc.tensor.matmul(out, ones[0:1, :], b2[:, :], start=True, stop=False)
                        last = nc.tensor.matmul(out, h1[h % 2][:, t * P:(t + 1) * P], w2[:, :], start=False, stop=True)
                    last.then_inc(z_part, 1)

                for h in range(HL):
                    if h >= 2:
                        pe.wait_ge(h_ready, b * HL + (h - 1))
                    else:
                        pe.wait_ge(h_ready, b * HL)
                    out = ps[1 + h % 2]
                    nc.tensor.matmul(out[:, :], w1[:, 0:P], hT[:, :], start=True, stop=False)
                    nc.tensor.matmul(out[:, :], w1[:, (1 + h) * P:(2 + h) * P], statT[:, :], start=False, stop=True)\
                        .then_inc(h_done, 1)
                    if h:
                        logits(h - 1)
                logits(HL - 1)
                pe.wait_ge(on_ready, b + 1)
                pe.wait_ge(oT_ready, b)
                for t in range(NB):
                    last = nc.tensor.transpose(ps[5][:, t * P:(t + 1) * P], on[:, t * P:(t + 1) * P], st["ident"][:, :])
                last.then_inc(oT_done, 1)
                pe.wait_ge(oT_ready, b + 1)
                pe.wait_ge(y_ready, b)
                for t in range(NB):
                    last = nc.tensor.matmul(ps[6][:, t * P:(t + 1) * P], oT[:, t * P:(t + 1) * P], wo[:, :],
                                            start=True, stop=True)
                last.then_inc(y_done, 1)


def sinkhorn(nc, d, st):
    with ExitStack() as ctx:
        sb = lambda name, shape, dt=F32: ctx.enter_context(nc.sbuf_tensor("k_" + name, shape, dt))
        sem = Signals(nc, ctx, "k_")
        lg_ps, t_ps, m_ps, s_ps = (ctx.enter_context(nc.psum_tensor("k_" + n, [P, 512], F32))
                                   for n in ("lg_ps", "t_ps", "m_ps", "s_ps"))
        w = sb("w", [P, NE2])
        down = sb("down", [P, NE2])
        ones = sb("ones", [P, P])
        c, z, ez, key, hot = (sb(n, [P, NT, NE2]) for n in ("c", "z", "ez", "key", "hot"))
        weight = sb("weight", [P, NT, TOPK2])
        r, rm, rsum, rlog, vmax, kmax = (sb(n, [P, NT]) for n in ("r", "rm", "rsum", "rlog", "vmax", "kmax"))
        q, cm, csum, clog = (sb(n, [P, NE2]) for n in ("q", "cm", "csum", "clog"))
        top = sb("top", [NE2, 1])
        topb = sb("topb", [NE2, P])
        one8 = sb("one8", [NE2, P])
        consts_in, lg_done, zero, dve = sem("consts_in"), sem("lg_done"), sem("zero"), sem("dve_steps")
        row_ready, row_exp, row_sum, row_log = (sem(n) for n in ("row_ready", "row_exp", "row_sum", "row_log"))
        cm_ready, cmT_done, topb_ready, cmb_done = (sem(n) for n in ("cm_ready", "cmT_done", "topb_ready", "cmb_done"))
        col_ready, col_exp, csum_ready, csumb_done, col_log = (sem(n) for n in
            ("col_ready", "col_exp", "csum_ready", "csumb_done", "col_log"))
        last_ready, last_exp = sem("last_ready"), sem("last_exp")
        block = ctx.enter_context(nc.Block())

        @block.sync
        def _(sp):
            sp.dma_start(w[:, :], d["gate_w"]).then_inc(consts_in, 16)
            sp.dma_start(down[:, :], d["down2"].partition_broadcast(P)).then_inc(consts_in, 16)

        @block.tensor
        def _(pe):
            pe.wait_ge(consts_in, 32)
            for t in range(NT):
                last = nc.tensor.matmul(lg_ps[:, t * NE2:(t + 1) * NE2], st["hsT"][:, t * P:(t + 1) * P], w[:, :],
                                        start=True, stop=True)
            last.then_inc(lg_done, 1)
            pe.wait_ge(zero, 1)
            with pe.Fori(0, SINKHORN) as i:
                pe.wait_ge(cm_ready, i + 1)
                nc.tensor.transpose(t_ps[0:NE2, 0:P], cm[:, :], st["ident"][:, :]).then_inc(cmT_done, 1)
                pe.wait_ge(topb_ready, i + 1)
                nc.tensor.matmul(m_ps[:, 0:NE2], topb[:, :], st["ident"][0:NE2, 0:NE2], start=True, stop=True)\
                    .then_inc(cmb_done, 1)
                pe.wait_ge(csum_ready, i + 1)
                nc.tensor.matmul(s_ps[:, 0:NE2], ones[:, :], csum[:, :], start=True, stop=True).then_inc(csumb_done, 1)

        @block.vector
        def _(v):
            step = Chain(v, dve)
            by_expert = lambda ap: ap.rearrange("p t e -> p e t")
            step(nc.vector.memset(ones[:, :], 1.0))
            step(nc.vector.memset(one8[:, :], 1.0))
            nc.vector.memset(q[:, :], 0.0).then_inc(zero, 1)
            v.wait_ge(zero, 1)
            v.wait_ge(consts_in, 32)
            v.wait_ge(lg_done, 1)
            step(nc.vector.tensor_scalar(c[:, :, :], lg_ps[:, 0:NT * NE2].rearrange("p (t e) -> p t e", e=NE2),
                                         float(-1.0 / SK_EPS), None, ALU.mult))
            with v.Fori(0, SINKHORN) as i:
                step.restart()
                step(nc.vector.tensor_tensor(z[:, :, :], c[:, :, :], bc(q[:, :], NT), ALU.add))
                step(nc.vector.tensor_reduce(rm[:, :], z[:, :, :], AX.X, ALU.max))
                nc.vector.tensor_tensor(z[:, :, :], z[:, :, :], bc(rm[:, :], NE2, 2), ALU.subtract).then_inc(row_ready, 1)
                v.wait_ge(row_exp, i + 1)
                nc.vector.tensor_reduce(rsum[:, :], ez[:, :, :], AX.X, ALU.add).then_inc(row_sum, 1)
                v.wait_ge(row_log, i + 1)
                step(nc.vector.scalar_tensor_tensor(out=r[:, :], in0=rlog[:, :], scalar=-1.0, in1=rm[:, :],
                                                    op0=ALU.mult, op1=ALU.subtract))
                step(nc.vector.tensor_tensor(z[:, :, :], c[:, :, :], bc(r[:, :], NE2, 2), ALU.add))
                nc.vector.tensor_reduce(cm[:, :], by_expert(z[:, :, :]), AX.X, ALU.max).then_inc(cm_ready, 1)
                v.wait_ge(cmT_done, i + 1)
                step(nc.vector.tensor_reduce(top[:, :], t_ps[0:NE2, 0:P], AX.X, ALU.max))
                nc.vector.tensor_scalar(topb[:, :], one8[:, :], top[:, 0:1], None, ALU.mult).then_inc(topb_ready, 1)
                v.wait_ge(cmb_done, i + 1)
                nc.vector.tensor_tensor(z[:, :, :], z[:, :, :], bc(m_ps[:, 0:NE2], NT), ALU.subtract).then_inc(col_ready, 1)
                v.wait_ge(col_exp, i + 1)
                nc.vector.tensor_reduce(csum[:, :], by_expert(ez[:, :, :]), AX.X, ALU.add).then_inc(csum_ready, 1)
                v.wait_ge(col_log, i + 1)
                step(nc.vector.scalar_tensor_tensor(out=q[:, :], in0=clog[:, :], scalar=-1.0, in1=m_ps[:, 0:NE2],
                                                    op0=ALU.mult, op1=ALU.subtract))
            step(nc.vector.tensor_tensor(z[:, :, :], c[:, :, :], bc(r[:, :], NE2, 2), ALU.add))
            nc.vector.tensor_tensor(z[:, :, :], z[:, :, :], bc(q[:, :], NT), ALU.add).then_inc(last_ready, 1)
            v.wait_ge(last_exp, 1)
            step(nc.vector.tensor_scalar(key[:, :, :], z[:, :, :], float(np.log(np.finfo(np.float32).tiny)), None,
                                         ALU.is_ge))
            step(nc.vector.tensor_tensor(ez[:, :, :], ez[:, :, :], key[:, :, :], ALU.mult))
            gates = st["gates1"]
            step(nc.vector.tensor_copy(weight[:, :, :], ez[:, :, 0:TOPK2]))
            for k in range(TOPK2):
                step(nc.vector.tensor_reduce(vmax[:, :], ez[:, :, :], AX.X, ALU.max))
                step(nc.vector.tensor_tensor(key[:, :, :], ez[:, :, :], bc(vmax[:, :], NE2, 2), ALU.is_equal))
                step(nc.vector.tensor_tensor(key[:, :, :], key[:, :, :], bc(down[:, :], NT), ALU.mult))
                step(nc.vector.tensor_reduce(kmax[:, :], key[:, :, :], AX.X, ALU.max))
                step(nc.vector.tensor_tensor(hot[:, :, :], key[:, :, :], bc(kmax[:, :], NE2, 2), ALU.is_equal))
                dst = gates if k == 0 else key
                step(nc.vector.tensor_tensor(dst[:, :, :], hot[:, :, :], bc(weight[:, :, k], NE2, 2), ALU.mult))
                if k:
                    step(nc.vector.tensor_tensor(gates[:, :, :], gates[:, :, :], key[:, :, :], ALU.add))
                else:
                    step(nc.vector.scalar_tensor_tensor(out=ez[:, :, :], in0=hot[:, :, :], scalar=-4.0,
                                                        in1=ez[:, :, :], op0=ALU.mult, op1=ALU.add))

        @block.scalar
        def _(a):
            with a.Fori(0, SINKHORN) as i:
                a.wait_ge(row_ready, i + 1)
                nc.scalar.activation(ez[:, :, :], z[:, :, :], ACT.Exp).then_inc(row_exp, 1)
                a.wait_ge(row_sum, i + 1)
                nc.scalar.activation(rlog[:, :], rsum[:, :], ACT.Ln).then_inc(row_log, 1)
                a.wait_ge(col_ready, i + 1)
                nc.scalar.activation(ez[:, :, :], z[:, :, :], ACT.Exp).then_inc(col_exp, 1)
                a.wait_ge(csumb_done, i + 1)
                nc.scalar.activation(clog[:, :], s_ps[:, 0:NE2], ACT.Ln).then_inc(col_log, 1)
            a.wait_ge(last_ready, 1)
            nc.scalar.activation(ez[:, :, :], z[:, :, :], ACT.Exp).then_inc(last_exp, 1)


def experts1(nc, d, st):
    F = DF // P
    with ExitStack() as ctx:
        sb = lambda name, shape, dt=F32: ctx.enter_context(nc.sbuf_tensor("f_" + name, shape, dt))
        sem = Signals(nc, ctx, "f_")
        bank = lambda n: ctx.enter_context(nc.psum_tensor("f_" + n, [P, 512], F32))
        g_ps, u_ps, y_ps = ([bank(f"{n}{i}") for i in range(2)] for n in ("g", "u", "y"))
        wg, wu, wd = ([sb(f"{n}{i}", [P, DF]) for i in range(2)] for n in ("wg", "wu", "wd"))
        g = [sb(f"silu{i}", [P, S]) for i in range(2)]
        act = [sb(f"act{i}", [P, F, S]) for i in range(2)]
        tail = [sb(f"tail{i}", [P, NB, P]) for i in range(2)]
        gb = [sb(f"gb{i}", [P, NB]) for i in range(2)]
        w_in = [sem(f"w_in{i}") for i in range(2)]
        slot_done = [sem(f"slot_done{i}") for i in range(2)]
        gu_done, g_ready, act_ready, sum_ready, stored = (sem(n) for n in
            ("gu_done", "g_ready", "act_ready", "sum_ready", "stored"))
        zero, gb_ready, silu_ready, mul_ready, out_ready = (sem(n) for n in
            ("zero", "gb_ready", "silu_ready", "mul_ready", "out_ready"))
        block = ctx.enter_context(nc.Block())

        def units(eng, unit):
            with eng.Fori(0, NE2 // 2) as i:
                for k in range(2):
                    with eng.Fori(0, B // 2) as j:
                        for s in range(2):
                            unit(i, k, j * 2 + s, s, i * (2 * B) + j * 2 + (k * B + s))

        @block.sync
        def _(sp):
            with sp.Fori(0, NE2 // 2) as i:
                for k in range(2):
                    sp.wait_ge(slot_done[k], i * B)
                    for dst, src in ((wg, "wg"), (wu, "wu"), (wd, "wd")):
                        sp.dma_start(dst[k][:, :], d[src][i * 2 + k, :, :]).then_inc(w_in[k], 16)
            with sp.Fori(0, B // 2) as j:
                for s in range(2):
                    sp.wait_ge(out_ready, j * 2 + (s + 1))
                    sp.dma_start(d["out"][j * 2 + s, :, :].rearrange("(t p) d -> p t d", p=P), tail[s][:, :, :])\
                        .then_inc(stored, 16)
            sp.wait_ge(stored, 16 * B)

        @block.tensor
        def _(pe):
            def hidden(i, k, b, s, n):
                x = st["hsT"][:, bass.ds(b * S, S)]
                for f in range(F):
                    if f >= 2:
                        pe.wait_ge(act_ready, n * F + (f - 1))
                    else:
                        pe.wait_ge(act_ready, n * F)
                    ff = slice(f * P, (f + 1) * P)
                    nc.tensor.matmul(g_ps[f % 2][:, :], wg[k][:, ff], x, start=True, stop=True)
                    nc.tensor.matmul(u_ps[f % 2][:, :], wu[k][:, ff], x, start=True, stop=True).then_inc(gu_done, 1)

            def down(i, k, b, s, n):
                pe.wait_ge(act_ready, n * F + F)
                pe.wait_ge(sum_ready, n)
                for t in range(NB):
                    for f in range(F):
                        last = nc.tensor.matmul(y_ps[s][:, t * P:(t + 1) * P], act[s][:, f, t * P:(t + 1) * P],
                                                wd[k][:, f * P:(f + 1) * P], start=(f == 0), stop=(f == F - 1))
                last.then_inc(slot_done[k], 1)

            def unit(i, k, b, s, n):
                if s == 0:
                    pe.wait_ge(w_in[k], i * 48 + 48)
                hidden(i, k, b, s, n)
                down(i, k, b, s, n)

            units(pe, unit)

        @block.scalar
        def _(a):
            def unit(i, k, b, s, n):
                for f in range(F):
                    a.wait_ge(gu_done, n * F + (f + 1))
                    if f >= 2:
                        a.wait_ge(act_ready, n * F + (f - 1))
                    else:
                        a.wait_ge(act_ready, n * F)
                    nc.scalar.activation(g[f % 2][:, :], g_ps[f % 2][:, :], ACT.Silu).then_inc(g_ready, 1)

            units(a, unit)
            with a.Fori(0, B // 2) as j:
                for s in range(2):
                    b = j * 2 + s
                    a.wait_ge(sum_ready, NE2 * B)
                    a.wait_ge(out_ready, j * 2)
                    nc.scalar.activation(g[s][:, :].rearrange("p (t d) -> p t d", d=P),
                                         st["sum1"][:, bass.ds(b * NB, NB), :], ACT.Silu).then_inc(silu_ready, 1)

        @block.vector
        def _(v):
            nc.vector.memset(st["sum1"][:, :, :], 0.0).then_inc(zero, 1)
            v.wait_ge(zero, 1)

            def unit(i, k, b, s, n):
                v.wait_ge(slot_done[k], i * B)
                v.wait_ge(slot_done[1 - k], i * B + (B if k else 0))
                for f in range(F):
                    v.wait_ge(g_ready, n * F + (f + 1))
                    nc.vector.tensor_tensor(act[s][:, f, :], g[f % 2][:, :], u_ps[f % 2][:, :], ALU.mult)\
                        .then_inc(act_ready, 1)
                v.wait_ge(slot_done[k], i * B + (b + 1))
                nc.vector.tensor_copy(gb[s][:, :], st["gates1"][:, bass.ds(b * NB, NB), bass.ds(i * 2 + k, 1)]
                                      .rearrange("p t e -> p (t e)")).then_inc(gb_ready, 1)
                v.wait_ge(gb_ready, n + 1)
                for t in range(NB):
                    at = st["sum1"][:, b * NB + t, :]
                    last = nc.vector.scalar_tensor_tensor(out=at, in0=y_ps[s][:, t * P:(t + 1) * P],
                                                          scalar=gb[s][:, t:t + 1], in1=at, op0=ALU.mult, op1=ALU.add)
                last.then_inc(sum_ready, 1)

            units(v, unit)
            with v.Fori(0, B // 2) as j:
                for s in range(2):
                    b = j * 2 + s
                    v.wait_ge(silu_ready, j * 2 + (s + 1))
                    v.wait_ge(stored, j * 32)
                    nc.vector.tensor_tensor(tail[s][:, :, :], st["s1"][:, bass.ds(b * NB, NB), :],
                                            g[s][:, :].rearrange("p (t d) -> p t d", d=P), ALU.mult).then_inc(mul_ready, 1)
                    v.wait_ge(mul_ready, j * 2 + (s + 1))
                    nc.vector.tensor_tensor(tail[s][:, :, :], tail[s][:, :, :], st["acc"][:, bass.ds(b * NB, NB), :],
                                            ALU.add).then_inc(out_ready, 1)



def program(nc, d):
    with ExitStack() as ctx:
        sb = lambda name, shape, dt=F32, c=ctx: c.enter_context(nc.sbuf_tensor(name, shape, dt))
        st = state(nc, ctx)
        st["acc"] = sb("acc", [P, NT, P])
        st["hsT"] = sb("hsT", [P, B * S])
        with ExitStack() as c1:
            st["ctx0"] = sb("ctx0", [P, NT, P], F32, c1)
            with ExitStack() as c2:
                st["v0"] = sb("v0", [P, NT, H0, D0 + 1], F32, c2)
                prepare(nc, d, st)
                attn0(nc, d, st)
            attn1(nc, d, st)
            route(nc, d, st)
            experts(nc, d, st)
            join0(nc, d, st)
        st["s1"] = sb("s1", [P, NT, P])
        with ExitStack() as c1:
            st["vd"] = sb("vd", [P, B * (NB + 1), P], F32, c1)
            st["short"] = sb("short", [P, NT, P], F32, c1)
            st["long"] = sb("long", [P, NT, P], F32, c1)
            st["delta"] = sb("delta", [P, NT, P], F32, c1)
            project1(nc, d, st)
            long_filter(nc, d, st)
            solve(nc, d, st)
            scan(nc, d, st)
            gate1(nc, d, st)
        st["gates1"] = sb("gates1", [P, NT, NE2])
        st["sum1"] = sb("sum1", [P, NT, P])
        sinkhorn(nc, d, st)
        experts1(nc, d, st)



def layout(inputs):
    f = lambda name: np.asarray(inputs[name])
    swap = np.arange(P) ^ 1
    a = {"x": f("L0_attn_x")}
    wq, wk, wv, wo = (f("L0_attn_" + n) for n in ("wq", "wk", "wv", "wo"))
    a["w0"] = np.concatenate([wq.T, wq[swap].T, wk.T, wk[swap].T, wv.T, wo.T], axis=1)
    inv = (np.float32(10000.0) ** (-np.arange(0, D0, 2, dtype=np.float32) / np.float32(D0))).astype(np.float32)
    angles = np.outer(np.arange(S, dtype=np.float32), inv).astype(np.float32)
    lane = (np.arange(P) % D0) // 2
    sign = np.where(np.arange(P) % 2 == 0, -1.0, 1.0).astype(np.float32)
    a["cos0"] = np.cos(angles).astype(np.float32).T[lane]
    a["sin0"] = np.sin(angles).astype(np.float32).T[lane] * sign[:, None]
    a["sign"] = sign[:, None]
    a["ident"] = np.eye(P, dtype=np.float32)
    a["flip"] = np.ascontiguousarray(a["ident"][::-1])
    q, k = np.indices((P, P))
    a["mask_q"] = np.where(k > q, np.float32(NEG), np.float32(0))
    a["mask_k"] = np.ascontiguousarray(a["mask_q"].T)
    a["pos"] = np.arange(S, dtype=np.float32)[None]
    a["theta"] = f("L0_ffn_theta")[(np.arange(P) % D1) // 2][:, None]
    sel = np.zeros((4, 2, P), np.float32)
    sel[0:2, 0] = 1
    sel[2:4, 1] = 1
    a["sel"] = sel
    a["gamma1"] = f("L0_ffn_gamma1")[None]
    a["o_b"] = f("L0_ffn_o_b")[None]
    qw, kw, vw, ow = (f("L0_ffn_" + n) for n in ("q_w", "k_w", "v_w", "o_w"))
    qb, kb = f("L0_ffn_q_b"), f("L0_ffn_k_b")
    cols = [np.arange(P) + P * p for p in range(NPAIR)]
    a["w1"] = np.stack([np.concatenate([qw[:, c], qw[:, c][:, swap], kw[:, c], kw[:, c][:, swap], vw[:, c],
                                        qb[c][:, None], qb[c][swap][:, None], kb[c][:, None], kb[c][swap][:, None]],
                                       axis=1) for c in cols])
    a["wo1"] = ow.reshape(NPAIR, P, P)
    a["v_b"] = f("L0_ffn_v_b").reshape(NPAIR, 1, P)
    a["gamma2"] = f("L0_ffn_gamma2")[None]
    a["router_w"] = f("L0_ffn_router_w")
    a["router_b"] = f("L0_ffn_router_b")[None]
    a["down"] = np.arange(NE, 0, -1, dtype=np.float32)[None]
    w1s = np.concatenate([f("L0_ffn_sh_w1")[None], f("L0_ffn_re_w1")])
    w2s = np.concatenate([f("L0_ffn_sh_w2")[None], f("L0_ffn_re_w2")])
    b1s = np.concatenate([f("L0_ffn_sh_b1")[None], f("L0_ffn_re_b1")])
    a["w2"] = np.concatenate([w1s, w2s, b1s[:, :, None]], axis=2)
    a["b2"] = f("L0_ffn_re_b2")
    a["sh_b2"] = f("L0_ffn_sh_b2")[:, None]
    a["sel_e"] = np.tile(np.repeat(np.eye(NE, dtype=np.float32), P, axis=1).reshape(NE, NE, P), (3, 1, 1))
    l = lambda name: f("L1_attn_" + name)
    a["w3"] = np.concatenate([l("q_w").T, l("k_w").T, l("v_w").T, l("b_w").T], axis=1)
    a["cw"] = np.stack([l("q_cw"), l("k_cw"), l("v_cw")], axis=1)
    a["fir_short"] = l("fir_short_w").reshape(P, KF)
    taps = np.zeros((P, 3 * P), np.float32)
    taps[:, P - 1:P - 1 + KL] = l("fir_long_w").reshape(P, KL)[:, ::-1]
    a["fir_long"] = taps
    same = (q // CH) == (k // CH)
    a["mask_m"] = np.where(same & (k < q), np.float32(-1), np.float32(0))
    a["mask_a"] = np.where(same & (k >= q), np.float32(1), np.float32(0))
    a["mask_h"] = same.astype(np.float32)
    mlp1 = l("mlp1_w")
    blocks = [mlp1[:, :P].T]
    for head in range(HL):
        block = np.zeros((P, P), np.float32)
        block[head * CH:head * CH + 16] = mlp1[:, P:].T
        blocks.append(block)
    a["mlp1"] = np.concatenate(blocks, axis=1)
    a["mlp1_b"] = l("mlp1_b")[:, None]
    a["mlp2"] = l("mlp2_w").T
    a["mlp2_b"] = l("mlp2_b")[None]
    a["wo3"] = l("o_w").T
    a["norm_w"] = l("norm_w")[None]
    a["temp"] = l("logit_temp")[None]
    a["res"] = l("conv_res_logit")[None]
    m = lambda name: f("L1_ffn_" + name)
    a["gate_w"] = m("gate_W").T
    a["down2"] = np.arange(NE2, 0, -1, dtype=np.float32)[None]
    a["wg"] = m("W_gate").transpose(0, 2, 1)
    a["wu"] = m("W_up").transpose(0, 2, 1)
    a["wd"] = m("W_down").transpose(0, 2, 1).reshape(NE2, DF // P, P, P).transpose(0, 2, 1, 3).reshape(NE2, P, DF)
    return {k: np.ascontiguousarray(v) for k, v in a.items()}



def scratch(nc, d):
    dr = lambda name, shape, dt=F32: nc.dram_tensor(name, shape, dt, kind="Internal").ap()
    d["xfT"] = dr("xfT_d", (B, P, S))
    d["parts"] = dr("parts_d", (2, B, 3, P, S), BF16)
    d["anT"] = dr("anT_d", (B, P, S))
    d["g3T"] = dr("g3T_d", (B, 3 * NE, S), BF16)
    d["gT"] = dr("gT_d", (B, NE, S))
    d["yT"] = dr("yT_d", (B, P, S))
    d["tok"] = dr("tok_d", (3, B, NB, P, P))
    d["chan"] = dr("chan_d", (2, B, P, S))
    d["m"] = dr("m_d", (B, HL, NB, NB, CH, CH))
    d["t"] = dr("t_d", (B, HL, NB, NB, CH, CH))



def kernel(**inputs):
    import concourse.bacc as bacc
    from concourse.bass_utils import run_bass_kernel_spmd

    nc = bacc.Bacc("TRN2", target_bir_lowering=False, num_devices=1)
    arrays = {"in_" + name: a for name, a in layout(inputs).items()}
    d = {name[3:]: nc.dram_tensor(name, a.shape, mybir.dt.from_np(a.dtype), kind="ExternalInput").ap()
         for name, a in arrays.items()}
    d["out"] = nc.dram_tensor("out", (B, S, P), F32, kind="ExternalOutput").ap()
    scratch(nc, d)
    program(nc, d)
    return run_bass_kernel_spmd(nc, [arrays], core_ids=[0]).results[0]["out"]
```

```python
from contextlib import ExitStack

import concourse.bass as bass
from concourse import mybir
import numpy as np

F32 = mybir.dt.float32
BF16 = mybir.dt.bfloat16
ALU = mybir.AluOpType
ACT = mybir.ActivationFunctionType
AX = mybir.AxisListType

P = 128
B, S = 8, 512
NB = S // P
NT = B * NB
NEG = -1.0e30
LN_EPS = 1e-5
H0, D0 = 16, 8
GROUPS_Q = (0, 0, 1, 1, 0, 2)
GROUPS_K = (0, 1, 0, 1, 2, 0)
R0 = len(GROUPS_Q) * D0
H1, D1 = 16, 64
NPAIR = H1 // 2
WCOLS = 5 * P + 4

NE, TOPK = 31, 3

HL, CH, KC, KF, KL = 4, 32, 4, 5, 64
NE2, DF, TOPK2, SINKHORN, SK_EPS = 8, 512, 2, 20, 0.05

WIDTHS = [P * (i + 1) for i in range(NB)]


class Chain:

    def __init__(self, eng, sem):
        self.eng, self.sem, self.n = eng, sem, 0

    def restart(self):
        self.eng.sem_clear(self.sem)
        self.n = 0

    def __call__(self, ins):
        self.n += 1
        ins.then_inc(self.sem, 1)
        self.eng.wait_ge(self.sem, self.n)


class Signals:

    def __init__(self, nc, ctx, prefix):
        self.nc, self.prefix, self.handles = nc, prefix, []
        ctx.callback(self.close)

    def __call__(self, name):
        self.handles.append(self.nc.alloc_semaphore(self.prefix + name))
        return self.handles[-1]

    def close(self):
        self.nc.clear_and_free_semaphores(self.handles)
        self.nc.all_engine_barrier()


def after(eng, sem, count):
    if not isinstance(count, int) or count > 0:
        eng.wait_ge(sem, count)


def bc(ap, n, axis=1):
    u = ap.unsqueeze(axis)
    shape = list(u.shape)
    shape[axis] = n
    return u.to_broadcast(shape)



def prepare(nc, d, st):
    with ExitStack() as ctx:
        sb = lambda name, shape, dt=F32: ctx.enter_context(nc.sbuf_tensor("p_" + name, shape, dt))
        ps = [ctx.enter_context(nc.psum_tensor(f"prep_ps{i}", [P, 512], F32)) for i in range(7)]
        sem = Signals(nc, ctx, "p_")
        xs = [sb(f"xs{i}", [P, NB, P]) for i in range(2)]
        xn = sb("xn", [P, NB, P])
        xf = sb("xf", [P, NB, P])
        sq = sb("sq", [P, NB, P])
        stats = sb("stats", [P, NB, 6])
        mv = sb("mv", [P, NB, 2])
        var = sb("var", [P, NB])
        sd = sb("sd", [P, NB])
        rstd = sb("rstd", [P, NB])
        ssq = sb("ssq", [P, NB])
        ms = sb("ms", [P, NB])
        rms = sb("rms", [P, NB])
        rrms = sb("rrms", [P, NB])
        xnT = sb("xnT", [P, 512])
        xfT = sb("xfT", [P, 512])
        w0 = sb("w0", [P, 6 * P])
        gamma = sb("gamma", [P, P])
        ob = sb("ob", [P, P])
        c0 = sb("c0", [P, S])
        s0 = sb("s0", [P, S])
        t1 = [sb(f"t1{i}", [P, S]) for i in range(2)]
        t2 = [sb(f"t2{i}", [P, S]) for i in range(2)]
        rot = [sb(f"rot{i}", [P, S]) for i in range(2)]
        rest = [sb(f"rest{i}", [P, S]) for i in range(2)]
        parts = [sb(f"parts{i}", [P, 3, S], BF16) for i in range(2)]
        theta = sb("theta", [P, 1])
        sign = sb("sign", [P, 1])
        pos = sb("pos", [P, S])
        ang = sb("ang", [P, S])
        turns = sb("turns", [P, S])
        red = sb("red", [P, S])
        over = sb("over", [P, S])
        xfT_stored = sem("xfT_stored")
        consts_in, x_in = sem("consts_in"), [sem("x_in0"), sem("x_in1")]
        var_ready, sd_ready, xn_ready, ssq_ready = sem("var_ready"), sem("sd_ready"), sem("xn_ready"), sem("ssq_ready")
        ms_ready, rms_ready, xf_ready, acc_ready = sem("ms_ready"), sem("rms_ready"), sem("xf_ready"), sem("acc_ready")
        xnT_done, xfT_done, xnT_ready, xfT_ready = sem("xnT_done"), sem("xfT_done"), sem("xnT_ready"), sem("xfT_ready")
        qk_done, v_done, v_ready = sem("qk_done"), sem("v_done"), sem("v_ready")
        prod_ready, rot_ready, high_ready, rest_ready = sem("prod_ready"), sem("rot_ready"), sem("high_ready"), sem("rest_ready")
        mid_ready, low_ready, stores = sem("mid_ready"), sem("low_ready"), sem("stores")
        red_ready, sin_ready, dve, masks_ready = sem("red_ready"), sem("sin_ready"), sem("dve_steps"), sem("masks_ready")
        block = ctx.enter_context(nc.Block())
        n_consts = 12

        @block.sync
        def _(sp):
            for dst, src in ((w0[:, :], d["w0"]), (c0[:, :], d["cos0"]), (s0[:, :], d["sin0"]),
                             (st["ident"][:, :], d["ident"]), (st["maskf"][:, 0, :], d["mask_q"]),
                             (st["maskf"][:, 1, :], d["mask_k"]), (theta[:, :], d["theta"]),
                             (sign[:, :], d["sign"]), (st["self"][:, :, :], d["sel"]),
                             (gamma[:, :], d["gamma1"].partition_broadcast(P)),
                             (ob[:, :], d["o_b"].partition_broadcast(P)),
                             (pos[:, :], d["pos"].partition_broadcast(P))):
                sp.dma_start(dst, src).then_inc(consts_in, 16)

            def load(b, s):
                sp.dma_start(xs[s][:, :, :], d["x"][b, :, :].rearrange("(t p) d -> p t d", p=P)).then_inc(x_in[s], 16)

            def store(b):
                sp.wait_ge(xfT_ready, b + 1)
                sp.dma_start(d["xfT"][b, :, :], xfT[:, :]).then_inc(xfT_stored, 16)
                for i in range(2):
                    sp.wait_ge(low_ready, 2 * b + i + 1)
                    sp.dma_start(d["parts"][i, b, :, :, :].rearrange("t p s -> p t s"),
                                 parts[i][:, :, :]).then_inc(stores, 16)

            load(0, 0)
            load(1, 1)
            with sp.Fori(0, B // 2 - 1) as i:
                for s in range(2):
                    b = i * 2 + s
                    sp.wait_ge(xn_ready, b + 1)
                    load(b + 2, s)
                    store(b)
            store(B - 2)
            store(B - 1)
            sp.wait_ge(stores, 32 * B)
            sp.wait_ge(xfT_stored, 16 * B)

        @block.vector
        def _(v):
            step = Chain(v, dve)
            v.wait_ge(consts_in, 16 * n_consts)
            for dst, src in ((st["identb"][:, :], st["ident"][:, :]), (st["maskb"][:, :, :], st["maskf"][:, :, :]),
                             (st["selb"][:, :, :], st["self"][:, :, :])):
                last = nc.vector.tensor_copy(dst, src)
            last.then_inc(masks_ready, 1)
            step(nc.vector.memset(st["v0"][:, :, :, :], 1.0))
            step(nc.vector.tensor_scalar(ang[:, :], pos[:, :], theta[:, 0:1], None, ALU.mult))
            step(nc.vector.tensor_scalar(turns[:, :], ang[:, :], float(1 / (2 * np.pi)), None, ALU.mult))
            step(nc.vector.tensor_scalar(turns[:, :], turns[:, :], 12582912.0, None, ALU.add))
            step(nc.vector.tensor_scalar(turns[:, :], turns[:, :], 12582912.0, None, ALU.subtract))
            c1 = 6.28125
            c2 = float(np.float32(np.round((2 * np.pi - c1) * 2**21) / 2**21))
            c3 = float(2 * np.pi - c1 - c2)
            cur = ang
            for c in (c1, c2, c3):
                step(nc.vector.scalar_tensor_tensor(out=red[:, :], in0=turns[:, :], scalar=-c, in1=cur[:, :],
                                                    op0=ALU.mult, op1=ALU.add))
                cur = red
            pi = float(np.nextafter(np.float32(np.pi), np.float32(0)))
            step(nc.vector.tensor_scalar(ang[:, :], red[:, :], pi, -pi, ALU.min, ALU.max))
            step(nc.vector.tensor_scalar(red[:, :], red[:, :], float(np.pi / 2), None, ALU.add))
            step(nc.vector.tensor_scalar(over[:, :], red[:, :], float(np.pi), float(2 * np.pi), ALU.is_gt, ALU.mult))
            step(nc.vector.tensor_tensor(red[:, :], red[:, :], over[:, :], ALU.subtract))
            nc.vector.tensor_scalar(red[:, :], red[:, :], pi, -pi, ALU.min, ALU.max).then_inc(red_ready, 1)
            v.wait_ge(sin_ready, 1)
            step(nc.vector.tensor_scalar(st["sin1"][:, :], st["sin1"][:, :], sign[:, 0:1], None, ALU.mult))

            def norm(b, s):
                step.restart()
                v.wait_ge(x_in[s], 16 * (b // 2) + 16)
                for t in range(NB):
                    last = nc.vector.bn_stats(stats[:, t, :], xs[s][:, t, :])
                step(last)
                for t in range(NB):
                    last = nc.vector.bn_aggr(mv[:, t, :], stats[:, t, :])
                step(last)
                nc.vector.tensor_scalar(var[:, :], mv[:, :, 1], LN_EPS, None, ALU.add).then_inc(var_ready, 1)
                v.wait_ge(sd_ready, b + 1)
                step(nc.vector.reciprocal(rstd[:, :], sd[:, :]))
                v.wait_ge(xnT_done, b)
                v.wait_ge(ssq_ready, b)
                for t in range(NB):
                    last = nc.vector.tensor_scalar(xn[:, t, :], xs[s][:, t, :], mv[:, t, 0:1], rstd[:, t:t + 1],
                                                   ALU.subtract, ALU.mult)
                last.then_inc(xn_ready, 1)
                v.wait_ge(ssq_ready, b + 1)
                nc.vector.tensor_scalar(ms[:, :], ssq[:, :], 1.0 / P, LN_EPS, ALU.mult, ALU.add).then_inc(ms_ready, 1)
                v.wait_ge(rms_ready, b + 1)
                step(nc.vector.reciprocal(rrms[:, :], rms[:, :]))
                v.wait_ge(xn_ready, b + 1)
                v.wait_ge(xfT_done, b)
                for t in range(NB):
                    last = nc.vector.scalar_tensor_tensor(out=xf[:, t, :], in0=xn[:, t, :], scalar=rrms[:, t:t + 1],
                                                          in1=gamma[:, :], op0=ALU.mult, op1=ALU.mult)
                last.then_inc(xf_ready, 1)
                v.wait_ge(xf_ready, b + 1)
                nc.vector.tensor_tensor(st["acc"][:, bass.ds(b * NB, NB), :], xf[:, :, :], bc(ob[:, :], NB), ALU.add)\
                    .then_inc(acc_ready, 1)

            def products(b):
                for i in range(2):
                    v.wait_ge(qk_done, 2 * b + i + 1)
                    v.wait_ge(rot_ready, 2 * b + i)
                    nc.vector.tensor_tensor(t1[i][:, :], ps[2 + 2 * i][:, :], c0[:, :], ALU.mult)
                    nc.vector.tensor_tensor(t2[i][:, :], ps[3 + 2 * i][:, :], s0[:, :], ALU.mult).then_inc(prod_ready, 1)

            norm(0, 0)
            with v.Fori(0, B // 2 - 1) as i:
                for s in range(2):
                    norm(i * 2 + (s + 1), 1 - s)
                    products(i * 2 + s)
            norm(B - 1, 1)
            products(B - 2)
            products(B - 1)

        @block.gpsimd
        def _(g):
            with g.Fori(0, B) as b:
                for i in range(2):
                    g.wait_ge(prod_ready, 2 * b + i + 1)
                    nc.gpsimd.tensor_tensor(rot[i][:, :], t1[i][:, :], t2[i][:, :], ALU.add).then_inc(rot_ready, 1)
                    g.wait_ge(high_ready, 2 * b + i + 1)
                    nc.gpsimd.tensor_tensor(rest[i][:, :], rot[i][:, :], parts[i][:, 0, :], ALU.subtract)\
                        .then_inc(rest_ready, 1)
                    g.wait_ge(mid_ready, 2 * b + i + 1)
                    nc.gpsimd.tensor_tensor(parts[i][:, 2, :], rest[i][:, :], parts[i][:, 1, :], ALU.subtract)\
                        .then_inc(low_ready, 1)

        @block.scalar
        def _(a):
            a.wait_ge(red_ready, 1)
            nc.scalar.activation(st["sin1"][:, :], ang[:, :], ACT.Sin)
            nc.scalar.activation(st["cos1"][:, :], red[:, :], ACT.Sin).then_inc(sin_ready, 1)

            def roots(b):
                a.wait_ge(var_ready, b + 1)
                nc.scalar.activation(sd[:, :], var[:, :], ACT.Sqrt).then_inc(sd_ready, 1)
                a.wait_ge(xn_ready, b + 1)
                for t in range(NB):
                    last = nc.scalar.activation(sq[:, t, :], xn[:, t, :], ACT.Square, accum_out=ssq[:, t:t + 1])
                last.then_inc(ssq_ready, 1)
                a.wait_ge(ms_ready, b + 1)
                nc.scalar.activation(rms[:, :], ms[:, :], ACT.Sqrt).then_inc(rms_ready, 1)

            def copies(b):
                a.wait_ge(xnT_done, b + 1)
                a.wait_ge(v_done, b)
                nc.scalar.copy(xnT[:, :], ps[0][:, :]).then_inc(xnT_ready, 1)
                a.wait_ge(xfT_done, b + 1)
                a.wait_ge(xfT_stored, 16 * b)
                nc.scalar.copy(xfT[:, :], ps[1][:, :]).then_inc(xfT_ready, 1)
                a.wait_ge(v_done, b + 1)
                nc.scalar.copy(st["v0"][:, bass.ds(b * NB, NB), :, 0:D0],
                               ps[6][:, :].rearrange("p (t h e) -> p t h e", t=NB, h=H0)).then_inc(v_ready, 1)

            def split(b):
                a.wait_ge(stores, 32 * b)
                for i in range(2):
                    a.wait_ge(rot_ready, 2 * b + i + 1)
                    nc.scalar.copy(parts[i][:, 0, :], rot[i][:, :]).then_inc(high_ready, 1)
                    a.wait_ge(rest_ready, 2 * b + i + 1)
                    nc.scalar.copy(parts[i][:, 1, :], rest[i][:, :]).then_inc(mid_ready, 1)

            roots(0)
            copies(0)
            with a.Fori(1, B) as b:
                roots(b)
                split(b - 1)
                copies(b)
            split(B - 1)

        @block.tensor
        def _(pe):
            pe.wait_ge(consts_in, 16 * n_consts)
            with pe.Fori(0, B) as b:
                pe.wait_ge(xn_ready, b + 1)
                pe.wait_ge(xnT_ready, b)
                for t in range(NB):
                    last = nc.tensor.transpose(ps[0][:, t * P:(t + 1) * P], xn[:, t, :], st["ident"][:, :])
                last.then_inc(xnT_done, 1)
                pe.wait_ge(xnT_ready, b + 1)
                pe.wait_ge(prod_ready, 2 * b)
                for i in range(2):
                    for k in range(2):
                        j = 2 * i + k
                        last = nc.tensor.matmul(ps[2 + j][:, :], w0[:, j * P:(j + 1) * P], xnT[:, :], start=True, stop=True)
                    last.then_inc(qk_done, 1)
                pe.wait_ge(v_ready, b)
                for t in range(NB):
                    last = nc.tensor.matmul(ps[6][:, t * P:(t + 1) * P], xnT[:, t * P:(t + 1) * P],
                                            w0[:, 4 * P:5 * P], start=True, stop=True)
                last.then_inc(v_done, 1)
                pe.wait_ge(xf_ready, b + 1)
                pe.wait_ge(xfT_ready, b)
                for t in range(NB):
                    last = nc.tensor.transpose(ps[1][:, t * P:(t + 1) * P], xf[:, t, :], st["ident"][:, :])
                last.then_inc(xfT_done, 1)



class Regions:

    def __init__(self, nc, ctx, name):
        self.banks = [ctx.enter_context(nc.psum_tensor(f"{name}{i}", [P, 512], F32)) for i in range(8)]

    def scores(self, r, i):
        b0, b1, b2 = self.banks[3 * r:3 * r + 3]
        return (b1[:, 384:512], b2[:, 0:256], b1[:, 0:384], b0[:, :])[i]

    def shift_rows(self, r):
        return self.banks[3 * r + 2][0:2, 256:512].bitcast(BF16)

    def whole(self, r):
        b0, b1, b2 = self.banks[3 * r:3 * r + 3]
        return b0[:, :], b1[:, :], b2[:, 0:256]


E_AT = [0, 512, 1024, 512 + 384]


def e_cols(j, i):
    at = E_AT[j] + (i - j) * P
    return slice(at, at + P)


def attn0(nc, d, st):
    n_heads = B * H0
    per = 8
    n_quads, rounds = n_heads // 4, n_heads // per
    scale = float(1.0 / np.sqrt(np.float32(D0)))
    with ExitStack() as ctx:
        sb = lambda name, shape, dt=F32: ctx.enter_context(nc.sbuf_tensor("a0_" + name, shape, dt))
        sem = Signals(nc, ctx, "a0_")
        rg = Regions(nc, ctx, "a0_ps")
        oT_ps, o_ps = rg.banks[6:8]
        qs = sb("qs", [P, 2, H0, S], BF16)
        ks = sb("ks", [P, 2, H0, S], BF16)
        shift = [sb(f"shift{i}", [P, NB]) for i in range(2)]
        shift2 = [sb(f"shift2{i}", [P, NB, 2], BF16) for i in range(2)]
        rows = [sb(f"rows{i}", [2, 512], BF16) for i in range(2)]
        e = [sb(f"e{i}", [P, 1280]) for i in range(per)]
        vq = [sb(f"vq{i}", [P, NB, 4, 32]) for i in range(2)]
        oT = [sb(f"oT{i}", [P, S]) for i in range(2)]
        rden = [sb(f"rden{i}", [P, NB, 4]) for i in range(2)]
        zero, vq_zero = sem("zero"), sem("vq_zero")
        stacks_in = [sem("stacks_in0"), sem("stacks_in1")]
        s_part, max_ready, high_ready, shift_ready = sem("s_part"), sem("max_ready"), sem("high_ready"), sem("shift_ready")
        rowsT_done, rows_ready, sT_part, e_part = sem("rowsT_done"), sem("rows_ready"), sem("sT_part"), sem("e_part")
        vq_ready, oT_done, oT_ready, o_done = sem("vq_ready"), sem("oT_done"), sem("oT_ready"), sem("o_done")
        rden_ready, o_ready = sem("rden_ready"), sem("o_ready")
        block = ctx.enter_context(nc.Block())

        def heads(eng, round_):
            round_(0, True, False)
            with eng.Fori(1, rounds - 1) as i:
                round_(i, False, False)
            round_(rounds - 1, False, True)

        @block.sync
        def _(sp):
            def load(b, slot):
                for dst, i, groups in ((qs, 0, GROUPS_Q), (ks, 1, GROUPS_K)):
                    for r, part in enumerate(groups):
                        sp.dma_start(dst[r * D0:(r + 1) * D0, slot, :, :],
                                     d["parts"][i, b, part, :, :].rearrange("(h e) s -> e h s", e=D0))\
                            .then_inc(stacks_in[slot], 16)
            sp.wait_ge(zero, 2)
            load(0, 0)
            load(1, 1)
            with sp.Fori(1, B // 2) as i:
                for slot in range(2):
                    b = 2 * i + slot
                    sp.wait_ge(sT_part, 3 * H0 * (b - 1))
                    load(b, slot)

        @block.gpsimd
        def _(gp):
            nc.gpsimd.memset(qs[:, :, :, :], 0.0).then_inc(zero, 1)
            for s in range(2):
                last = nc.gpsimd.memset(vq[s][:, :, :, :], 0.0)
            last.then_inc(vq_zero, 1)
            gp.wait_ge(vq_zero, 1)

            def copy_v(q, s):
                after(gp, oT_done, q - 1)
                b, h = q // 4, (q % 4) * 4
                nc.gpsimd.tensor_copy(vq[s][:, :, :, 0:D0 + 1], st["v0"][:, bass.ds(b * NB, NB), bass.ds(h, 4), :])\
                    .then_inc(vq_ready, 1)

            for q in range(2):
                copy_v(q, q)
            with gp.Fori(1, n_quads // 2) as i:
                for s in range(2):
                    copy_v(2 * i + s, s)

        @block.tensor
        def _(pe):
            def scores(n, r):
                b, h = n // H0, n % H0
                for part, blocks in enumerate(((3,), (2, 0), (1,))):
                    after(pe, e_part, 3 * (n - 2) + (part + 1))
                    for i in blocks:
                        out = rg.scores(r, i)
                        nc.tensor.matmul(out, qs[:, b % 2, h, i * P:(i + 1) * P], ks[:, b % 2, h, 0:(i + 1) * P],
                                         start=True, stop=False)
                        last = nc.tensor.matmul(out[:, i * P:(i + 1) * P], st["identb"][:, :], st["maskb"][:, 0, :],
                                                start=False, stop=True)
                    last.then_inc(s_part, 1)

            def shift_rows(n, r):
                pe.wait_ge(shift_ready, n + 1)
                for i in range(NB):
                    last = nc.tensor.transpose(rg.shift_rows(r)[:, i * P:(i + 1) * P], shift2[r][:, i, :],
                                               st["identb"][:, :])
                last.then_inc(rowsT_done, 1)

            def transposed(n, r):
                b, h = n // H0, n % H0
                pe.wait_ge(rows_ready, n + 1)
                for blocks in ((0,), (1, 3), (2,)):
                    for j in blocks:
                        out = rg.scores(r, NB - 1 - j)
                        nc.tensor.matmul(out, ks[:, b % 2, h, j * P:(j + 1) * P], qs[:, b % 2, h, j * P:S],
                                         start=True, stop=False)
                        nc.tensor.matmul(out[:, 0:P], st["identb"][:, :], st["maskb"][:, 1, :], start=False, stop=False)
                        last = nc.tensor.matmul(out, st["selb"][0:2, 0, :], rows[r][:, j * P:S], start=False, stop=True)
                    last.then_inc(sT_part, 1)

            def values(q, s):
                pe.wait_ge(e_part, 12 * q + 12)
                pe.wait_ge(vq_ready, q + 1)
                after(pe, oT_ready, q)
                for j in range(NB):
                    for k in range(4):
                        last = nc.tensor.matmul(oT_ps[32 * k:32 * k + 32, j * P:S], vq[s][:, j, k, :],
                                                e[4 * s + k][:, E_AT[j]:E_AT[j] + S - j * P],
                                                start=(j == 0), stop=(j == NB - 1), skip_group_check=True)
                last.then_inc(oT_done, 1)

            def by_token(q, s):
                pe.wait_ge(oT_ready, q + 1)
                after(pe, o_ready, q)
                for t in range(NB):
                    last = nc.tensor.transpose(o_ps[:, t * P:(t + 1) * P], oT[s][:, t * P:(t + 1) * P], st["ident"][:, :])
                last.then_inc(o_done, 1)

            def round_(i, first, last):
                for k in range(per):
                    n, r, q, s = i * per + k, k % 2, 2 * i + k // 4, k // 4
                    shift_rows(n, r)
                    if k == per - 1 and not last:
                        b = (n + 1) // H0
                        pe.wait_ge(stacks_in[0], ((b // 2) + 1) * (12 * 16))
                        pe.wait_ge(stacks_in[1], ((b + 1) // 2) * (12 * 16))
                    if not (k == per - 1 and last):
                        scores(n + 1, 1 - r)
                    transposed(n, r)
                    if k % 4 == 1 and not (first and s == 0):
                        values(q - 1, 1 - s)
                    if k % 4 == 3 and not (first and s == 0):
                        by_token(q - 1, 1 - s)

            pe.wait_ge(stacks_in[0], 12 * 16)
            scores(0, 0)
            heads(pe, round_)
            values(n_quads - 1, 1)
            by_token(n_quads - 1, 1)

        @block.vector
        def _(v):
            def maxima(n, r):
                after(v, rowsT_done, n - 1)
                for part, blocks in enumerate(((3,), (2, 0), (1,))):
                    v.wait_ge(s_part, 3 * n + (part + 1))
                    for i in blocks:
                        last = nc.vector.tensor_reduce(shift[r][:, i:i + 1], rg.scores(r, i), AX.X, ALU.max, negate=True)
                last.then_inc(max_ready, 1)
                v.wait_ge(max_ready, n + 1)
                nc.vector.tensor_copy(shift2[r][:, :, 0], shift[r][:, :]).then_inc(high_ready, 1)
                v.wait_ge(high_ready, n + 1)
                nc.vector.tensor_tensor(shift2[r][:, :, 1], shift[r][:, :], shift2[r][:, :, 0], ALU.subtract)\
                    .then_inc(shift_ready, 1)

            def normed(q, s):
                v.wait_ge(o_done, q + 1)
                b, h = q // 4, (q % 4) * 4
                o = o_ps[:, :].rearrange("p (t h e) -> p t h e", t=NB, h=4)
                nc.vector.reciprocal(rden[s][:, :, :], o[:, :, :, D0]).then_inc(rden_ready, 1)
                v.wait_ge(rden_ready, q + 1)
                out = st["ctx0"][:, bass.ds(b * NB, NB), bass.ds(h * D0, 4 * D0)].rearrange("p t (h e) -> p t h e", h=4)
                nc.vector.tensor_tensor(out, o[:, :, :, 0:D0], bc(rden[s][:, :, :], D0, 3), ALU.mult).then_inc(o_ready, 1)

            def round_(i, first, last):
                for k in range(per):
                    n, r, q, s = i * per + k, k % 2, 2 * i + k // 4, k // 4
                    if not (k == per - 1 and last):
                        maxima(n + 1, 1 - r)
                    if k % 4 == 3 and not (first and s == 0):
                        normed(q - 1, 1 - s)

            nc.vector.memset(ks[:, :, :, :], 0.0).then_inc(zero, 1)
            maxima(0, 0)
            heads(v, round_)
            normed(n_quads - 1, 1)

        @block.scalar
        def _(a):
            def copy_rows(n, r):
                a.wait_ge(rowsT_done, n + 1)
                after(a, sT_part, 3 * (n - 1))
                nc.scalar.copy(rows[r][:, :], rg.shift_rows(r)).then_inc(rows_ready, 1)

            def exps(n, r, k):
                at = 0
                for part, piece in enumerate(rg.whole(r)):
                    a.wait_ge(sT_part, 3 * n + (part + 1))
                    nc.scalar.activation(e[k][:, at:at + piece.shape[1]], piece, ACT.Exp, scale=scale).then_inc(e_part, 1)
                    at += piece.shape[1]

            def copy_values(q, s):
                a.wait_ge(oT_done, q + 1)
                after(a, o_done, q - 1)
                nc.scalar.copy(oT[s][:, :], oT_ps[:, :]).then_inc(oT_ready, 1)

            def round_(i, first, last):
                for k in range(per):
                    n, r, q, s = i * per + k, k % 2, 2 * i + k // 4, k // 4
                    copy_rows(n, r)
                    if k % 4 == 0:
                        after(a, oT_done, q - 1)
                    exps(n, r, k)
                    if k % 4 == 2 and not (first and s == 0):
                        copy_values(q - 1, 1 - s)

            heads(a, round_)
            copy_values(n_quads - 1, 1)


def state(nc, ctx):
    sb = lambda name, shape, dt=F32: ctx.enter_context(nc.sbuf_tensor(name, shape, dt))
    return {
        "ident": sb("ident", [P, P]), "identb": sb("identb", [P, P], BF16),
        "maskf": sb("maskf", [P, 2, P]), "maskb": sb("maskb", [P, 2, P], BF16),
        "self": sb("self", [4, 2, P]), "selb": sb("selb", [4, 2, P], BF16),
        "sin1": sb("sin1", [P, S]), "cos1": sb("cos1", [P, S]),
    }



def attn1(nc, d, st):
    n_pairs = NPAIR * B
    scale = float(1.0 / np.sqrt(D1))
    with ExitStack() as ctx:
        sb = lambda name, shape, dt=F32: ctx.enter_context(nc.sbuf_tensor("a1_" + name, shape, dt))
        sem = Signals(nc, ctx, "a1_")
        two = lambda name, shape, dt=F32: [sb(f"{name}{i}", shape, dt) for i in range(2)]
        rg = Regions(nc, ctx, "a1_ps")
        X, Y = rg.banks[6], rg.banks[7]
        w = two("w", [P, WCOLS])
        wo = two("wo", [P, P + 1])
        xT = two("xT", [P, S])
        qT = two("qT", [P, S])
        kT = [[sb(f"kT{i}{h}", [P, S]) for h in range(2)] for i in range(2)]
        t1 = two("t1", [P, S])
        t2 = two("t2", [P, S])
        v_ = two("v", [P, NB, P])
        shift = two("shift", [P, NB])
        shift2 = two("shift2", [P, NB, 2], BF16)
        rows = two("rows", [2, S], BF16)
        e = two("e", [P, 1280])
        es = two("es", [P, S])
        rden, cx = sb("rden", [P, S]), sb("cx", [P, S])
        cxT = two("cxT", [P, S])
        ones = sb("ones", [P, D1])
        ones_ready, zero = sem("ones_ready"), sem("zero")
        pair_in = sem("in0"), sem("in1")
        wo_in = sem("wo0"), sem("wo1")
        qk_done, v_done = sem("qk_done"), sem("v_done")
        prod_ready, rot_ready, v_ready = sem("prod_ready"), sem("rot_ready"), sem("v_ready")
        s_part, max_ready, high_ready, shift_ready = sem("s_part"), sem("max_ready"), sem("high_ready"), sem("shift_ready")
        rowsT_done, rows_ready, sT_part, e_part = sem("rowsT_done"), sem("rows_ready"), sem("sT_part"), sem("e_part")
        o_done, es_part, es_ready = sem("o_done"), sem("es_part"), sem("es_ready")
        rden_ready, cx_ready, cxT_ready = sem("rden_ready"), sem("cx_ready"), sem("cxT_ready")
        y_done, acc_ready = sem("y_done"), sem("acc_ready")
        block = ctx.enter_context(nc.Block())

        def pairs(eng, pair):
            for n in range(3):
                pair(n, n % 2, n == 0, False)
            with eng.Fori(0, (n_pairs - 4) // 2) as i:
                for j in range(2):
                    pair(2 * i + 3 + j, (1 + j) % 2, False, False)
            pair(n_pairs - 1, 1, False, True)

        @block.sync
        def _(sp):
            def load(n, s):
                if not isinstance(n, int):
                    sp.wait_ge(s_part, 6 * n - 11)
                sp.dma_start(w[s][:, :], d["w1"][n // B, :, :]).then_inc(pair_in[s], 16)
                sp.dma_start(xT[s][:, :], d["xfT"][n % B, :, :]).then_inc(pair_in[s], 16)

            def load_out(n, s):
                after(sp, y_done, n - 1)
                sp.dma_start(wo[s][:, :], d["wo1"][n // B, :, :]).then_inc(wo_in[s], 16)

            load(0, 0)
            load(1, 1)
            load_out(0, 0)
            with sp.Fori(1, n_pairs // 2) as i:
                for s in range(2):
                    load(2 * i + s, s)
                    load_out(2 * i + s - 1, 1 - s)
            load_out(n_pairs - 1, 1)

        @block.tensor
        def _(pe):
            def project(n, s):
                pe.wait_ge(pair_in[s], ((n // 2) + 1) * 32)
                for c, out in enumerate((X, Y, X, Y)):
                    if c == 0:
                        after(pe, rden_ready, n - 1)
                    elif c == 1:
                        after(pe, acc_ready, n - 1)
                    else:
                        pe.wait_ge(prod_ready, 4 * n + (c - 1))
                    nc.tensor.matmul(out[:, :], w[s][:, c * P:(c + 1) * P], xT[s][:, :], start=True, stop=True)\
                        .then_inc(qk_done, 1)
                pe.wait_ge(prod_ready, 4 * n + 3)
                for t in range(NB):
                    last = nc.tensor.matmul(X[:, t * P:(t + 1) * P], xT[s][:, t * P:(t + 1) * P], w[s][:, 4 * P:5 * P],
                                            start=True, stop=True)
                last.then_inc(v_done, 1)

            def scores(g, n, s, h):
                pe.wait_ge(rot_ready, 2 * n + 2)
                for part, blocks in enumerate(((3,), (2, 0), (1,))):
                    after(pe, e_part, 3 * (g - 2) + (part + 1))
                    for i in blocks:
                        out = rg.scores(h, i)
                        nc.tensor.matmul(out, qT[s][:, i * P:(i + 1) * P], kT[s][h][:, 0:(i + 1) * P],
                                         start=True, stop=False)
                        last = nc.tensor.matmul(out[:, i * P:(i + 1) * P], st["identb"][:, :], st["maskb"][:, 0, :],
                                                start=False, stop=True)
                    last.then_inc(s_part, 1)

            def shift_rows(g, h):
                pe.wait_ge(shift_ready, g + 1)
                for i in range(NB):
                    last = nc.tensor.transpose(rg.shift_rows(h)[:, i * P:(i + 1) * P], shift2[h][:, i, :],
                                               st["identb"][:, :])
                last.then_inc(rowsT_done, 1)

            def transposed(g, s, h):
                pe.wait_ge(rows_ready, g + 1)
                for blocks in ((0,), (1, 3), (2,)):
                    for j in blocks:
                        out = rg.scores(h, NB - 1 - j)
                        nc.tensor.matmul(out, kT[s][h][:, j * P:(j + 1) * P], qT[s][:, j * P:S], start=True, stop=False)
                        nc.tensor.matmul(out[:, 0:P], st["identb"][:, :], st["maskb"][:, 1, :], start=False, stop=False)
                        last = nc.tensor.matmul(out, st["selb"][0:2, 0, :], rows[h][:, j * P:S], start=False, stop=True)
                    last.then_inc(sT_part, 1)

            def values(n, s, last):
                pe.wait_ge(e_part, 6 * n + 6)
                if last:
                    pe.wait_ge(acc_ready, n)
                else:
                    pe.wait_ge(prod_ready, 4 * n + 8)
                pe.wait_ge(v_ready, n + 1 if last else n + 2)
                halves = [slice(h * D1, (h + 1) * D1) for h in range(2)]
                for j in range(NB):
                    for h, hh in enumerate(halves):
                        nc.tensor.matmul(Y[hh, j * P:S], v_[s][:, j, hh], e[h][:, E_AT[j]:E_AT[j] + S - j * P],
                                         start=(j == 0), stop=(j == NB - 1), skip_group_check=True)
                for h, hh in enumerate(halves):
                    nc.tensor.matmul(X[hh, 0:P], ones[:, :], e[h][:, 0:P], start=True, stop=True)
                pe.wait_ge(es_ready, 2 * n + 2)
                for h, hh in enumerate(halves):
                    last = nc.tensor.matmul(X[hh, P:S], ones[:, :], es[h][:, P:S], start=True, stop=True)
                last.then_inc(o_done, 1)

            def output(n, s):
                pe.wait_ge(cxT_ready, n + 1)
                pe.wait_ge(wo_in[s], ((n // 2) + 1) * 16)
                for t in range(NB):
                    last = nc.tensor.matmul(Y[:, t * P:(t + 1) * P], cxT[s][:, t * P:(t + 1) * P],
                                            wo[s][:, 0:P], start=True, stop=True)
                last.then_inc(y_done, 1)

            pe.wait_ge(ones_ready, 1)
            project(0, 0)
            scores(0, 0, 0, 0)

            def pair(n, s, first, last):
                g = 2 * n
                shift_rows(g, 0)
                scores(g + 1, n, s, 1)
                transposed(g, s, 0)
                if not first:
                    output(n - 1, 1 - s)
                shift_rows(g + 1, 1)
                if not last:
                    project(n + 1, 1 - s)
                transposed(g + 1, s, 1)
                if not last:
                    scores(g + 2, n + 1, 1 - s, 0)
                values(n, s, last)

            pairs(pe, pair)
            output(n_pairs - 1, 1)

        @block.vector
        def _(v):
            def rotate(n, s):
                for c, (src, dst, table) in enumerate(((X, t1[0], "cos1"), (Y, t2[0], "sin1"),
                                                       (X, t1[1], "cos1"), (Y, t2[1], "sin1"))):
                    v.wait_ge(qk_done, 4 * n + (c + 1))
                    after(v, rot_ready, 2 * n + (c // 2) - 1)
                    nc.vector.scalar_tensor_tensor(out=dst[:, :], in0=src[:, :], scalar=w[s][:, 5 * P + c:5 * P + c + 1],
                                                   in1=st[table][:, :], op0=ALU.add, op1=ALU.mult).then_inc(prod_ready, 1)

            def maxima(g, h):
                after(v, rowsT_done, g - 1)
                for part, blocks in enumerate(((3,), (2, 0), (1,))):
                    v.wait_ge(s_part, 3 * g + (part + 1))
                    for i in blocks:
                        last = nc.vector.tensor_reduce(shift[h][:, i:i + 1], rg.scores(h, i), AX.X, ALU.max, negate=True)
                last.then_inc(max_ready, 1)
                v.wait_ge(max_ready, g + 1)
                nc.vector.tensor_copy(shift2[h][:, :, 0], shift[h][:, :]).then_inc(high_ready, 1)
                v.wait_ge(high_ready, g + 1)
                nc.vector.tensor_tensor(shift2[h][:, :, 1], shift[h][:, :], shift2[h][:, :, 0], ALU.subtract)\
                    .then_inc(shift_ready, 1)

            def normed(n, s):
                v.wait_ge(o_done, n + 1)
                v.wait_ge(cxT_ready, n)
                nc.vector.reciprocal(rden[:, :], X[:, :]).then_inc(rden_ready, 1)
                v.wait_ge(rden_ready, n + 1)
                nc.vector.tensor_tensor(cx[:, :], Y[:, :], rden[:, :], ALU.mult).then_inc(cx_ready, 1)
                v.wait_ge(cx_ready, n + 1)
                v.wait_ge(wo_in[s], ((n // 2) + 1) * 16)
                after(v, y_done, n - 1)
                nc.vector.tensor_scalar(cxT[s][:, :], cx[:, :], wo[s][:, P:P + 1], None, ALU.add).then_inc(cxT_ready, 1)

            def add(n):
                v.wait_ge(y_done, n + 1)
                b = n % B
                at = st["acc"][:, bass.ds(b * NB, NB), :]
                nc.vector.tensor_tensor(at, at, Y[:, :].rearrange("p (t d) -> p t d", d=P), ALU.add).then_inc(acc_ready, 1)

            nc.vector.memset(ones[:, :], 1.0).then_inc(ones_ready, 1)
            rotate(0, 0)
            maxima(0, 0)

            def pair(n, s, first, last):
                g = 2 * n
                maxima(g + 1, 1)
                if not first:
                    add(n - 1)
                if not last:
                    rotate(n + 1, 1 - s)
                if not last:
                    maxima(g + 2, 0)
                normed(n, s)

            pairs(v, pair)
            add(n_pairs - 1)

        @block.gpsimd
        def _(gp):
            def rotated(n, s):
                gp.wait_ge(prod_ready, 4 * n + 2)
                after(gp, sT_part, 6 * (n - 1))
                nc.gpsimd.tensor_tensor(qT[s][:, :], t1[0][:, :], t2[0][:, :], ALU.add).then_inc(rot_ready, 1)
                gp.wait_ge(rot_ready, 2 * n + 1)
                gp.wait_ge(prod_ready, 4 * n + 4)
                for h in range(2):
                    hh = slice(h * D1, (h + 1) * D1)
                    last = nc.gpsimd.tensor_tensor(kT[s][h][hh, :], t1[1][hh, :], t2[1][hh, :], ALU.add)
                last.then_inc(rot_ready, 1)

            def sums(g, n, h):
                gp.wait_ge(e_part, 3 * g + 3)
                after(gp, o_done, n)
                block = lambda j: e[h][:, E_AT[j]:E_AT[j] + S - j * P]
                nc.gpsimd.tensor_tensor(es[h][:, P:S], block(0)[:, P:S], block(1), ALU.add).then_inc(es_part, 1)
                gp.wait_ge(es_part, 2 * g + 1)
                nc.gpsimd.tensor_tensor(es[h][:, 2 * P:S], es[h][:, 2 * P:S], block(2), ALU.add).then_inc(es_part, 1)
                gp.wait_ge(es_part, 2 * g + 2)
                nc.gpsimd.tensor_tensor(es[h][:, 3 * P:S], es[h][:, 3 * P:S], block(3), ALU.add).then_inc(es_ready, 1)
                gp.wait_ge(es_ready, g + 1)

            def pair(n, s, first, last):
                sums(2 * n, n, 0)
                if not last:
                    rotated(n + 1, 1 - s)
                    gp.wait_ge(rot_ready, 2 * n + 4)
                sums(2 * n + 1, n, 1)

            for s in range(2):
                for h in range(2):
                    last = nc.gpsimd.memset(kT[s][h][:, :], 0.0)
            last.then_inc(zero, 1)
            gp.wait_ge(zero, 1)
            rotated(0, 0)
            gp.wait_ge(rot_ready, 2)

            pairs(gp, pair)

        @block.scalar
        def _(a):
            def copy_rows(g, h):
                a.wait_ge(rowsT_done, g + 1)
                after(a, sT_part, 3 * (g - 1))
                nc.scalar.copy(rows[h][:, :], rg.shift_rows(h)).then_inc(rows_ready, 1)

            def exps(g, n, h):
                after(a, o_done, n)
                at = 0
                for part, piece in enumerate(rg.whole(h)):
                    a.wait_ge(sT_part, 3 * g + (part + 1))
                    nc.scalar.activation(e[h][:, at:at + piece.shape[1]], piece, ACT.Exp, scale=scale).then_inc(e_part, 1)
                    at += piece.shape[1]

            def copy_v(n, s):
                a.wait_ge(v_done, n + 1)
                after(a, o_done, n - 1)
                nc.scalar.copy(v_[s][:, :, :], X[:, :].rearrange("p (t c) -> p t c", c=P)).then_inc(v_ready, 1)

            copy_v(0, 0)

            def pair(n, s, first, last):
                g = 2 * n
                copy_rows(g, 0)
                exps(g, n, 0)
                copy_rows(g + 1, 1)
                if not last:
                    copy_v(n + 1, 1 - s)
                exps(g + 1, n, 1)

            pairs(a, pair)



def route(nc, d, st):
    G = 2 * NB
    rounds = NT // G
    with ExitStack() as ctx:
        sb = lambda name, shape, dt=F32: ctx.enter_context(nc.sbuf_tensor("r_" + name, shape, dt))
        sem = Signals(nc, ctx, "r_")
        psb = lambda name: ctx.enter_context(nc.psum_tensor("r_" + name, [P, 512], F32))
        anT_ps, gT_ps = [psb("anT_ps0"), psb("anT_ps1")], [psb("gT_ps0"), psb("gT_ps1")]
        lg_ps, g3_ps = psb("lg_ps"), psb("g3_ps")
        bank = lambda banks, t: banks[t // NB][:, t % NB * P:(t % NB + 1) * P]
        sq = sb("sq", [P, G, P])
        ssq, ms, rms, rr = (sb(n, [P, G]) for n in ("ssq", "ms", "rms", "rr"))
        an = sb("an", [P, G, P])
        anT = sb("anT", [P, 2, S])
        gamma = sb("gamma", [P, P])
        wr = sb("wr", [P, NE])
        rb = sb("rb", [P, NE])
        down = sb("down", [P, NE])
        top, den, rden, vmax, kmax = (sb(n, [P, G]) for n in ("top", "den", "rden", "vmax", "kmax"))
        lg, ex, rem, eq, key, hot, gk, gates, rest = (sb(n, [P, G, NE]) for n in
                                                           ("lg", "ex", "rem", "eq", "key", "hot", "gk", "gates", "rest"))
        g3 = sb("g3", [P, G, 3 * NE], BF16)
        g3T = sb("g3T", [3 * NE, 2, S], BF16)
        gT = sb("gT", [NE, 2, S])
        consts_in, stores, dve = sem("consts_in"), sem("stores"), sem("dve_steps")
        ssq_ready, ms_ready, rms_ready, an_ready = sem("ssq_ready"), sem("ms_ready"), sem("rms_ready"), sem("an_ready")
        anT_done, anT_ready, lg_done, lg_ready = sem("anT_done"), sem("anT_ready"), sem("lg_done"), sem("lg_ready")
        ex_ready, gates_ready, gT_done, gT_ready = sem("ex_ready"), sem("gates_ready"), sem("gT_done"), sem("gT_ready")
        block = ctx.enter_context(nc.Block())

        @block.sync
        def _(sp):
            for dst, src in ((gamma[:, :], d["gamma2"].partition_broadcast(P)), (wr[:, :], d["router_w"]),
                             (rb[:, :], d["router_b"].partition_broadcast(P)), (down[:, :], d["down"].partition_broadcast(P))):
                sp.dma_start(dst, src).then_inc(consts_in, 16)
            with sp.Fori(0, rounds) as b:
                sp.wait_ge(anT_ready, b + 1)
                pair = lambda name: d[name][bass.ds(b * 2, 2), :, :].rearrange("b p s -> p b s")
                sp.dma_start(pair("anT"), anT[:, :, :]).then_inc(stores, 16)
                sp.wait_ge(gT_ready, b + 1)
                sp.dma_start(pair("g3T"), g3T[:, :, :]).then_inc(stores, 16)
                sp.dma_start(pair("gT"), gT[:, :, :]).then_inc(stores, 16)
            sp.wait_ge(stores, 48 * rounds)

        @block.vector
        def _(v):
            step = Chain(v, dve)
            v.wait_ge(consts_in, 64)
            with v.Fori(0, rounds) as b:
                step.restart()
                at = st["acc"][:, bass.ds(b * G, G), :]
                v.wait_ge(ssq_ready, b + 1)
                nc.vector.tensor_scalar(ms[:, :], ssq[:, :], 1.0 / P, LN_EPS, ALU.mult, ALU.add).then_inc(ms_ready, 1)
                v.wait_ge(rms_ready, b + 1)
                step(nc.vector.reciprocal(rr[:, :], rms[:, :]))
                v.wait_ge(anT_done, b)
                for t in range(G):
                    last = nc.vector.scalar_tensor_tensor(out=an[:, t, :], in0=st["acc"][:, b * G + t, :],
                                                          scalar=rr[:, t:t + 1], in1=gamma[:, :],
                                                          op0=ALU.mult, op1=ALU.mult)
                last.then_inc(an_ready, 1)
                v.wait_ge(an_ready, b + 1)
                nc.vector.tensor_tensor(at, at, an[:, :, :], ALU.add)
                v.wait_ge(lg_done, b + 1)
                z = lg_ps[:, 0:G * NE].rearrange("p (t e) -> p t e", e=NE)
                v.wait_ge(ex_ready, b)
                step(nc.vector.tensor_tensor(lg[:, :, :], z, bc(rb[:, :], G), ALU.add))
                step(nc.vector.tensor_reduce(top[:, :], lg[:, :, :], AX.X, ALU.max))
                nc.vector.tensor_tensor(lg[:, :, :], lg[:, :, :], bc(top[:, :], NE, 2), ALU.subtract).then_inc(lg_ready, 1)
                v.wait_ge(ex_ready, b + 1)
                step(nc.vector.tensor_reduce(den[:, :], ex[:, :, :], AX.X, ALU.add))
                step(nc.vector.reciprocal(rden[:, :], den[:, :]))
                step(nc.vector.tensor_tensor(rem[:, :, :], ex[:, :, :], bc(rden[:, :], NE, 2), ALU.mult))
                for k in range(TOPK):
                    step(nc.vector.tensor_reduce(vmax[:, :], rem[:, :, :], AX.X, ALU.max))
                    step(nc.vector.tensor_tensor(eq[:, :, :], rem[:, :, :], bc(vmax[:, :], NE, 2), ALU.is_equal))
                    step(nc.vector.tensor_tensor(key[:, :, :], eq[:, :, :], bc(down[:, :], G), ALU.mult))
                    step(nc.vector.tensor_reduce(kmax[:, :], key[:, :, :], AX.X, ALU.max))
                    step(nc.vector.tensor_tensor(hot[:, :, :], key[:, :, :], bc(kmax[:, :], NE, 2), ALU.is_equal))
                    if k == 0:
                        v.wait_ge(gT_done, b)
                        step(nc.vector.tensor_tensor(gates[:, :, :], hot[:, :, :], bc(vmax[:, :], NE, 2), ALU.mult))
                    else:
                        step(nc.vector.tensor_tensor(gk[:, :, :], hot[:, :, :], bc(vmax[:, :], NE, 2), ALU.mult))
                        step(nc.vector.tensor_tensor(gates[:, :, :], gates[:, :, :], gk[:, :, :], ALU.add))
                    if k < TOPK - 1:
                        step(nc.vector.scalar_tensor_tensor(out=rem[:, :, :], in0=hot[:, :, :], scalar=-4.0,
                                                            in1=rem[:, :, :], op0=ALU.mult, op1=ALU.add))
                hi, mid, lo = (g3[:, :, i * NE:(i + 1) * NE] for i in range(3))
                step(nc.vector.tensor_copy(hi, gates[:, :, :]))
                step(nc.vector.tensor_tensor(rest[:, :, :], gates[:, :, :], hi, ALU.subtract))
                step(nc.vector.tensor_copy(mid, rest[:, :, :]))
                nc.vector.tensor_tensor(lo, rest[:, :, :], mid, ALU.subtract).then_inc(gates_ready, 1)

        @block.scalar
        def _(a):
            with a.Fori(0, rounds) as b:
                for t in range(G):
                    last = nc.scalar.activation(sq[:, t, :], st["acc"][:, b * G + t, :], ACT.Square,
                                                accum_out=ssq[:, t:t + 1])
                last.then_inc(ssq_ready, 1)
                a.wait_ge(ms_ready, b + 1)
                nc.scalar.activation(rms[:, :], ms[:, :], ACT.Sqrt).then_inc(rms_ready, 1)
                a.wait_ge(anT_done, b + 1)
                a.wait_ge(lg_done, b)
                a.wait_ge(stores, 48 * b)
                for i in range(2):
                    last = nc.scalar.copy(anT[:, i, :], anT_ps[i][:, :])
                last.then_inc(anT_ready, 1)
                a.wait_ge(lg_ready, b + 1)
                nc.scalar.activation(ex[:, :, :], lg[:, :, :], ACT.Exp).then_inc(ex_ready, 1)
                a.wait_ge(gT_done, b + 1)
                nc.scalar.copy(g3T[:, :, :], g3_ps[0:3 * NE, 0:S].bitcast(BF16).rearrange("p (i s) -> p i s", s=S))
                for i in range(2):
                    last = nc.scalar.copy(gT[:, i, :], gT_ps[i][0:NE, :])
                last.then_inc(gT_ready, 1)

        @block.tensor
        def _(pe):
            pe.wait_ge(consts_in, 64)
            with pe.Fori(0, rounds) as b:
                pe.wait_ge(an_ready, b + 1)
                pe.wait_ge(anT_ready, b)
                for t in range(G):
                    last = nc.tensor.transpose(bank(anT_ps, t), an[:, t, :], st["ident"][:, :])
                last.then_inc(anT_done, 1)
                pe.wait_ge(anT_ready, b + 1)
                pe.wait_ge(lg_ready, b)
                for t in range(G):
                    tokens = anT[:, t // NB, t % NB * P:(t % NB + 1) * P]
                    last = nc.tensor.matmul(lg_ps[:, t * NE:(t + 1) * NE], tokens, wr[:, :], start=True, stop=True)
                last.then_inc(lg_done, 1)
                pe.wait_ge(gates_ready, b + 1)
                pe.wait_ge(gT_ready, b)
                for t in range(G):
                    nc.tensor.transpose(g3_ps[0:3 * NE, 64 * t:64 * t + 64].bitcast(BF16), g3[:, t, :], st["identb"][:, :])
                    last = nc.tensor.transpose(bank(gT_ps, t)[0:NE, :], gates[:, t, :], st["ident"][:, :])
                last.then_inc(gT_done, 1)


def experts(nc, d, st):
    n_exp = NE + 1
    per = 2 * n_exp
    SLOTS = 4
    with ExitStack() as ctx:
        sb = lambda name, shape, dt=F32: ctx.enter_context(nc.sbuf_tensor("x_" + name, shape, dt))
        sem = Signals(nc, ctx, "x_")
        psb = lambda name: ctx.enter_context(nc.psum_tensor("x_" + name, [P, 512], F32))
        two = lambda name, shape, dt=F32: [sb(f"{name}{i}", shape, dt) for i in range(2)]
        h_ps, g_ps, y_ps = ([psb(f"{n}{i}") for i in range(2)] for n in ("h_ps", "g_ps", "y_ps"))
        w = [sb(f"w{c}", [P, 2 * P + 1]) for c in range(SLOTS)]
        b2 = sb("b2", [NE, P])
        sh_b2 = sb("sh_b2", [P, 1])
        sel = sb("sel", [3 * NE, NE, P], BF16)
        self_ = sb("self", [3 * NE, NE, P])
        sel_ready = sem("sel_ready")
        anT = two("anT", [P, S])
        g3T = two("g3T", [3 * NE, S], BF16)
        gT = two("gT", [NE, S])
        h = two("h", [P, S])
        hg = two("hg", [P, S])
        y = two("y", [P, S])
        consts_in, stores = sem("consts_in"), sem("stores")
        seq_in = [sem(f"seq_in{i}") for i in range(2)]
        w_in = [sem(f"w_in{c}") for c in range(SLOTS)]
        h_done, h_ready, hg_ready = sem("h_done"), sem("h_ready"), sem("hg_ready")
        used = [sem(f"used{c}") for c in range(SLOTS)]
        y_done, y_ready = sem("y_done"), sem("y_ready")
        block = ctx.enter_context(nc.Block())
        turns = n_exp // SLOTS

        number = lambda r, i, c, q: r * per + i * (2 * SLOTS) + (2 * c + q)
        routed = lambda r, i, c, q: r * (per - 2) + i * (2 * SLOTS) + (2 * c + q - 2)
        is_expert = lambda i, c, e: isinstance(i, int) and c == e

        def rounds(eng, unit, head=None, tail=None):
            with eng.Fori(0, B // 2) as r:
                if head:
                    head(r)
                for c in range(SLOTS):
                    for q in range(2):
                        unit(r, 0, c, q)
                with eng.Fori(1, turns) as i:
                    for c in range(SLOTS):
                        for q in range(2):
                            unit(r, i, c, q)
                if tail:
                    tail(r)

        def wait_used_before(eng, r, i, c, q):
            if c:
                eng.wait_ge(used[c - 1], r * (2 * turns) + i * 2 + (q + 1))
            else:
                eng.wait_ge(used[SLOTS - 1], r * (2 * turns) + i * 2 + (q - 1))

        @block.sync
        def _(sp):
            for dst, src in ((b2[:, :], d["b2"]), (sh_b2[:, :], d["sh_b2"]),
                             (self_[:, :, :], d["sel_e"])):
                sp.dma_start(dst, src).then_inc(consts_in, 16)
            with sp.Fori(0, B // 2) as r:
                sp.wait_ge(y_ready, r * 2)
                for q in range(2):
                    for dst, name in ((anT, "anT"), (g3T, "g3T"), (gT, "gT")):
                        sp.dma_start(dst[q][:, :], d[name][r * 2 + q, :, :]).then_inc(seq_in[q], 16)
                with sp.Fori(0, turns) as i:
                    for c in range(SLOTS):
                        sp.wait_ge(used[c], r * (2 * turns) + i * 2)
                        sp.dma_start(w[c][:, :], d["w2"][i * SLOTS + c, :, :]).then_inc(w_in[c], 16)
                for q in range(2):
                    sp.wait_ge(y_ready, r * 2 + (q + 1))
                    sp.dma_start(d["yT"][r * 2 + q, :, :], y[q][:, :]).then_inc(stores, 16)
            sp.wait_ge(stores, 16 * B)

        @block.tensor
        def _(pe):
            pe.wait_ge(consts_in, 48)
            pe.wait_ge(sel_ready, 1)

            def first_product(r, i, c, q):
                if q == 0:
                    pe.wait_ge(w_in[c], r * (16 * turns) + i * 16 + 16)
                pe.wait_ge(h_ready, r * per if is_expert(i, c, 0) else number(r, i, c, q) - 1)
                last = nc.tensor.matmul(h_ps[q][:, :], w[c][:, 0:P], anT[q][:, :], start=True, stop=True)
                if not is_expert(i, c, 0):
                    pe.wait_ge(hg_ready, r * (per - 2) if is_expert(i, c, 1) else routed(r, i, c, q) - 1)
                    last = nc.tensor.matmul(g_ps[q][:, :], sel[:, i * SLOTS + (c - 1), :], g3T[q][:, :], start=True, stop=True)
                last.then_inc(h_done, 1)

            def second_product(slot, q, src, first):
                nc.tensor.matmul(y_ps[q][:, :], w[slot][:, P:2 * P], src[q][:, :], start=first, stop=False)\
                    .then_inc(used[slot], 1)

            def head(r):
                for q in range(2):
                    pe.wait_ge(seq_in[q], r * 48 + 48)
                pe.wait_ge(y_ready, r * 2)

            def unit(r, i, c, q):
                first_product(r, i, c, q)
                if is_expert(i, c, 1):
                    pe.wait_ge(h_ready, r * per + (q + 1))
                    second_product(0, q, h, True)
                elif not is_expert(i, c, 0):
                    pe.wait_ge(hg_ready, routed(r, i, c, q) - 1)
                    second_product((c - 1) % SLOTS, q, hg, False)

            def tail(r):
                for q in range(2):
                    pe.wait_ge(hg_ready, r * (per - 2) + (per - 4 + q + 1))
                    second_product(SLOTS - 1, q, hg, False)
                for q in range(2):
                    last = nc.tensor.matmul(y_ps[q][:, :], b2[:, :], gT[q][:, :], start=False, stop=True)
                last.then_inc(y_done, 1)

            rounds(pe, unit, head, tail)

        @block.scalar
        def _(a):
            a.wait_ge(consts_in, 48)

            def unit(r, i, c, q):
                a.wait_ge(h_done, number(r, i, c, q) + 1)
                if is_expert(i, c, 0):
                    a.wait_ge(hg_ready, r * (per - 2))
                elif is_expert(i, c, 1):
                    a.wait_ge(used[0], r * (2 * turns) + (q + 1))
                else:
                    a.wait_ge(hg_ready, routed(r, i, c, q) - 1)
                nc.scalar.activation(h[q][:, :], h_ps[q][:, :], ACT.Gelu, bias=w[c][:, 2 * P:2 * P + 1])\
                    .then_inc(h_ready, 1)

            rounds(a, unit)

        @block.vector
        def _(v):
            v.wait_ge(consts_in, 48)
            nc.vector.tensor_copy(sel[:, :, :], self_[:, :, :]).then_inc(sel_ready, 1)

            def unit(r, i, c, q):
                if is_expert(i, c, 0):
                    return
                v.wait_ge(h_ready, number(r, i, c, q) + 1)
                wait_used_before(v, r, i, c, q)
                nc.vector.tensor_tensor(hg[q][:, :], h[q][:, :], g_ps[q][:, :], ALU.mult).then_inc(hg_ready, 1)

            def tail(r):
                v.wait_ge(y_done, r + 1)
                v.wait_ge(stores, r * 32)
                for q in range(2):
                    nc.vector.tensor_scalar(y[q][:, :], y_ps[q][:, :], sh_b2[:, 0:1], None, ALU.add).then_inc(y_ready, 1)

            rounds(v, unit, None, tail)



def join0(nc, d, st):
    with ExitStack() as ctx:
        sb = lambda name, shape, dt=F32: ctx.enter_context(nc.sbuf_tensor("j_" + name, shape, dt))
        sem = Signals(nc, ctx, "j_")
        psb = lambda name: ctx.enter_context(nc.psum_tensor("j_" + name, [P, 512], F32))
        y_ps, cT_ps, s_ps, hT_ps = psb("y_ps"), psb("cT_ps"), psb("s_ps"), psb("hT_ps")
        wo = sb("wo", [P, P])
        yT = sb("yT", [P, S])
        xs, cs, f, g, t, hs, x1 = (sb(n, [P, NB, P]) for n in ("xs", "cs", "f", "g", "t", "hs", "x1"))
        cT = sb("cT", [P, S])
        stats = sb("stats", [P, NB, 6])
        mv = sb("mv", [P, NB, 2])
        var, sd, rstd = (sb(n, [P, NB]) for n in ("var", "sd", "rstd"))
        w_in, tile_in = sem("w_in"), sem("tile_in")
        y_done, cT_done, s_done, hT_done = sem("y_done"), sem("cT_done"), sem("s_done"), sem("hT_done")
        cs_ready, cT_ready, f_ready, g_ready = sem("cs_ready"), sem("cT_ready"), sem("f_ready"), sem("g_ready")
        x_ready, var_ready, sd_ready, hs_ready, hT_ready = (sem(n) for n in
                                                            ("x_ready", "var_ready", "sd_ready", "hs_ready", "hT_ready"))
        dve, kept = sem("dve_steps"), sem("kept")
        block = ctx.enter_context(nc.Block())

        @block.sync
        def _(sp):
            sp.dma_start(wo[:, :], d["w0"][:, 5 * P:6 * P]).then_inc(w_in, 16)
            with sp.Fori(0, B) as b:
                sp.wait_ge(x_ready, b)
                sp.dma_start(yT[:, :], d["yT"][b, :, :]).then_inc(tile_in, 16)
                sp.dma_start(xs[:, :, :], d["x"][b, :, :].rearrange("(t p) d -> p t d", p=P)).then_inc(tile_in, 16)

        @block.gpsimd
        def _(gp):
            with gp.Fori(0, B) as b:
                gp.wait_ge(cT_done, b)
                nc.gpsimd.tensor_copy(cs[:, :, :], st["ctx0"][:, bass.ds(b * NB, NB), :]).then_inc(cs_ready, 1)

        @block.tensor
        def _(pe):
            pe.wait_ge(w_in, 16)
            with pe.Fori(0, B) as b:
                pe.wait_ge(tile_in, b * 32 + 32)
                pe.wait_ge(f_ready, b)
                for k in range(NB):
                    last = nc.tensor.transpose(y_ps[:, k * P:(k + 1) * P], yT[:, k * P:(k + 1) * P], st["ident"][:, :])
                last.then_inc(y_done, 1)
                pe.wait_ge(cs_ready, b + 1)
                pe.wait_ge(cT_ready, b)
                for k in range(NB):
                    last = nc.tensor.transpose(cT_ps[:, k * P:(k + 1) * P], cs[:, k, :], st["ident"][:, :])
                last.then_inc(cT_done, 1)
                pe.wait_ge(cT_ready, b + 1)
                pe.wait_ge(x_ready, b)
                for k in range(NB):
                    last = nc.tensor.matmul(s_ps[:, k * P:(k + 1) * P], cT[:, k * P:(k + 1) * P], wo[:, :],
                                            start=True, stop=True)
                last.then_inc(s_done, 1)
                pe.wait_ge(hs_ready, b + 1)
                pe.wait_ge(hT_ready, b)
                for k in range(NB):
                    last = nc.tensor.transpose(hT_ps[:, k * P:(k + 1) * P], hs[:, k, :], st["ident"][:, :])
                last.then_inc(hT_done, 1)

        @block.vector
        def _(v):
            step = Chain(v, dve)
            with v.Fori(0, B) as b:
                step.restart()
                at = st["acc"][:, bass.ds(b * NB, NB), :]
                tiles = lambda ap: ap.rearrange("p (t d) -> p t d", d=P)
                v.wait_ge(y_done, b + 1)
                v.wait_ge(g_ready, b)
                nc.vector.tensor_tensor(f[:, :, :], tiles(y_ps[:, :]), at, ALU.add).then_inc(f_ready, 1)
                v.wait_ge(g_ready, b + 1)
                v.wait_ge(s_done, b + 1)
                step(nc.vector.tensor_tensor(t[:, :, :], tiles(s_ps[:, :]), g[:, :, :], ALU.mult))
                v.wait_ge(tile_in, b * 32 + 32)
                v.wait_ge(kept, b)
                nc.vector.tensor_tensor(x1[:, :, :], t[:, :, :], xs[:, :, :], ALU.add).then_inc(x_ready, 1)
                v.wait_ge(x_ready, b + 1)
                for k in range(NB):
                    last = nc.vector.bn_stats(stats[:, k, :], x1[:, k, :])
                step(last)
                for k in range(NB):
                    last = nc.vector.bn_aggr(mv[:, k, :], stats[:, k, :])
                step(last)
                nc.vector.tensor_scalar(var[:, :], mv[:, :, 1], LN_EPS, None, ALU.add).then_inc(var_ready, 1)
                v.wait_ge(sd_ready, b + 1)
                step(nc.vector.reciprocal(rstd[:, :], sd[:, :]))
                v.wait_ge(hT_done, b)
                for k in range(NB):
                    last = nc.vector.tensor_scalar(hs[:, k, :], x1[:, k, :], mv[:, k, 0:1],
                                                   rstd[:, k:k + 1], ALU.subtract, ALU.mult)
                last.then_inc(hs_ready, 1)

        @block.scalar
        def _(a):
            with a.Fori(0, B) as b:
                a.wait_ge(cT_done, b + 1)
                a.wait_ge(s_done, b)
                nc.scalar.copy(cT[:, :], cT_ps[:, :]).then_inc(cT_ready, 1)
                a.wait_ge(f_ready, b + 1)
                a.wait_ge(x_ready, b)
                nc.scalar.activation(g[:, :, :], f[:, :, :], ACT.Silu).then_inc(g_ready, 1)
                a.wait_ge(x_ready, b + 1)
                nc.scalar.copy(st["acc"][:, bass.ds(b * NB, NB), :], x1[:, :, :]).then_inc(kept, 1)
                a.wait_ge(var_ready, b + 1)
                nc.scalar.activation(sd[:, :], var[:, :], ACT.Sqrt).then_inc(sd_ready, 1)
                a.wait_ge(hT_done, b + 1)
                nc.scalar.copy(st["hsT"][:, bass.ds(b * S, S)], hT_ps[:, :]).then_inc(hT_ready, 1)


def project1(nc, d, st):
    with ExitStack() as ctx:
        sb = lambda name, shape, dt=F32: ctx.enter_context(nc.sbuf_tensor("q_" + name, shape, dt))
        sem = Signals(nc, ctx, "q_")
        ps = [ctx.enter_context(nc.psum_tensor(f"q_ps{i}", [P, 512], F32)) for i in range(8)]
        w = sb("w", [P, 3 * P + HL])
        cw = sb("cw", [P, 3, KC])
        fw = sb("fw", [P, KF])
        lead = 16
        pre = [sb(f"pre{i}", [P, lead + S]) for i in range(3)]
        conv = [sb(f"conv{i}", [P, S]) for i in range(3)]
        hT = sb("hT", [P, S])
        qT, kT = sb("qT", [P, S]), sb("kT", [P, S])
        vT = sb("vT", [P, lead + S])
        shT = sb("shT", [P, S])
        sq = sb("sq", [P, 2, S])
        beta = sb("beta", [P, NB, HL])
        ss, rt, rn = (sb(n, [P, 2, NB * HL]) for n in ("ss", "rt", "rn"))
        qn, kn, kb, vb = (sb(n, [P, NB, P]) for n in ("qn", "kn", "kb", "vb"))
        nT = [sb(f"nT{i}", [P, S]) for i in range(3)]
        m = sb("m", [P, HL, NB, P])
        mask = sb("mask", [P, P])
        consts_in, stores, dve = sem("consts_in"), sem("stores"), sem("dve_steps")
        hT_ready, proj_done, pre_ready, conv_ready, silu_ready = (sem(n) for n in
            ("hT_ready", "proj_done", "pre_ready", "conv_ready", "silu_ready"))
        short_ready, tok_done, sq_ready, ss_ready, rt_ready = (sem(n) for n in
            ("short_ready", "tok_done", "sq_ready", "ss_ready", "rt_ready"))
        beta_done, norm_ready, nT_done, nT_ready = (sem(n) for n in
            ("beta_done", "norm_ready", "nT_done", "nT_ready"))
        m_done, m_ready, sh_done, vd_ready = sem("m_done"), sem("m_ready"), sem("sh_done"), sem("vd_ready")
        sg_ready, zero = sem("sg_ready"), sem("zero")
        block = ctx.enter_context(nc.Block())
        n_stores = 5 + NB * HL

        @block.sync
        def _(sp):
            for dst, src in ((w[:, :], d["w3"]), (cw[:, :, :], d["cw"]), (fw[:, :], d["fir_short"]),
                             (mask[:, :], d["mask_m"])):
                sp.dma_start(dst, src).then_inc(consts_in, 16)
            with sp.Fori(0, B) as b:
                sp.wait_ge(norm_ready, b + 1)
                for i, src in enumerate((kn, kb, vb)):
                    sp.dma_start(d["tok"][i, b, :, :, :].rearrange("t p c -> p t c"), src[:, :, :]).then_inc(stores, 16)
                sp.wait_ge(nT_ready, b + 1)
                for i in range(2):
                    sp.dma_start(d["chan"][i, b, :, :], nT[i][:, :]).then_inc(stores, 16)
                sp.wait_ge(m_ready, b + 1)
                for h in range(HL):
                    for c in range(NB):
                        cc = slice(c * CH, (c + 1) * CH)
                        sp.dma_start(d["m"][b, h, :, c, :, :].rearrange("t i j -> i t j"), m[cc, h, :, cc])\
                            .then_inc(stores, 16)
            sp.wait_ge(stores, 16 * n_stores * B)

        @block.gpsimd
        def _(gp):
            for t in pre + [vT]:
                nc.gpsimd.memset(t[:, 0:lead], 0.0)
            for b in range(B):
                last = nc.gpsimd.memset(st["vd"][:, b * (NB + 1), :], 0.0)
            last.then_inc(zero, 1)
            with gp.Fori(0, B) as b:
                gp.wait_ge(beta_done, b)
                nc.gpsimd.tensor_copy(hT[:, :], st["hsT"][:, bass.ds(b * S, S)]).then_inc(hT_ready, 1)

        @block.tensor
        def _(pe):
            pe.wait_ge(consts_in, 64)
            with pe.Fori(0, B) as b:
                pe.wait_ge(hT_ready, b + 1)
                pe.wait_ge(m_ready, b)
                for i in range(3):
                    nc.tensor.matmul(ps[i][:, :], w[:, i * P:(i + 1) * P], hT[:, :], start=True, stop=True)\
                        .then_inc(proj_done, 1)
                for t in range(NB):
                    last = nc.tensor.matmul(ps[3][:, t * HL:(t + 1) * HL], hT[:, t * P:(t + 1) * P],
                                            w[:, 3 * P:3 * P + HL], start=True, stop=True)
                last.then_inc(beta_done, 1)
                pe.wait_ge(nT_ready, b)
                for i, src in enumerate((qT[:, :], kT[:, :], vT[:, lead:lead + S])):
                    pe.wait_ge(silu_ready, b * 3 + (i + 1))
                    for t in range(NB):
                        last = nc.tensor.transpose(ps[4 + i][:, t * P:(t + 1) * P], src[:, t * P:(t + 1) * P],
                                                   st["ident"][:, :])
                last.then_inc(tok_done, 1)
                pe.wait_ge(short_ready, b + 1)
                pe.wait_ge(vd_ready, b)
                for t in range(NB):
                    last = nc.tensor.transpose(ps[7][:, t * P:(t + 1) * P], shT[:, t * P:(t + 1) * P], st["ident"][:, :])
                last.then_inc(sh_done, 1)
                pe.wait_ge(norm_ready, b + 1)
                pe.wait_ge(vd_ready, b + 1)
                for i, src in enumerate((qn, kn, kb)):
                    for t in range(NB):
                        last = nc.tensor.transpose(ps[4 + i][:, t * P:(t + 1) * P], src[:, t, :], st["ident"][:, :])
                last.then_inc(nT_done, 1)
                pe.wait_ge(nT_ready, b + 1)
                pe.wait_ge(sg_ready, b + 1)
                for h in range(HL):
                    hh = slice(h * CH, (h + 1) * CH)
                    for t in range(NB):
                        tt = slice(t * P, (t + 1) * P)
                        last = nc.tensor.matmul(ps[h][:, tt], nT[2][hh, tt], nT[1][hh, tt], start=True, stop=True)
                last.then_inc(m_done, 1)

        @block.vector
        def _(v):
            step = Chain(v, dve)
            v.wait_ge(consts_in, 64)
            v.wait_ge(zero, 1)
            with v.Fori(0, B) as b:
                step.restart()
                for i in range(3):
                    v.wait_ge(pre_ready, b * 3 + (i + 1))
                    v.wait_ge(silu_ready, b * 3)
                    x = lambda j: pre[i][:, lead - KC + 1 + j:lead - KC + 1 + j + S]
                    step(nc.vector.tensor_scalar(conv[i][:, :], x(0), cw[:, i, 0:1], None, ALU.mult))
                    for j in range(1, KC):
                        op = nc.vector.scalar_tensor_tensor(out=conv[i][:, :], in0=x(j), scalar=cw[:, i, j:j + 1],
                                                            in1=conv[i][:, :], op0=ALU.mult, op1=ALU.add)
                        if j < KC - 1:
                            step(op)
                        else:
                            op.then_inc(conv_ready, 1)
                v.wait_ge(silu_ready, b * 3 + 3)
                v.wait_ge(sh_done, b)
                x = lambda j: vT[:, lead - KF + 1 + j:lead - KF + 1 + j + S]
                step(nc.vector.tensor_scalar(shT[:, :], x(0), fw[:, 0:1], None, ALU.mult))
                for j in range(1, KF):
                    op = nc.vector.scalar_tensor_tensor(out=shT[:, :], in0=x(j), scalar=fw[:, j:j + 1],
                                                        in1=shT[:, :], op0=ALU.mult, op1=ALU.add)
                    if j < KF - 1:
                        step(op)
                    else:
                        op.then_inc(short_ready, 1)
                v.wait_ge(sq_ready, b + 1)
                step(nc.vector.tensor_reduce(ss[:, :, :], sq[:, :, :].rearrange("p i (g e) -> p i g e", e=CH),
                                             AX.X, ALU.add))
                nc.vector.tensor_scalar(ss[:, :, :], ss[:, :, :], 1e-6, None, ALU.add).then_inc(ss_ready, 1)
                v.wait_ge(rt_ready, b + 1)
                step(nc.vector.reciprocal(rn[:, :, :], rt[:, :, :]))
                v.wait_ge(sg_ready, b + 1)
                step(nc.vector.tensor_scalar(beta[:, :, :], beta[:, :, :], 1e-6, None, ALU.max))
                v.wait_ge(nT_done, b)
                v.wait_ge(stores, b * (16 * n_stores))
                heads = lambda ap: ap.rearrange("p (g e) -> p g e", e=CH)
                flat = lambda ap: ap.rearrange("p t (h e) -> p (t h) e", e=CH)
                betas = bc(beta[:, :, :].rearrange("p t h -> p (t h)"), CH, 2)
                nc.vector.tensor_tensor(flat(qn[:, :, :]), heads(ps[4][:, :]), bc(rn[:, 0, :], CH, 2), ALU.mult)
                nc.vector.tensor_tensor(flat(vb[:, :, :]), heads(ps[6][:, :]), betas, ALU.mult)
                step(nc.vector.tensor_tensor(flat(kn[:, :, :]), heads(ps[5][:, :]), bc(rn[:, 1, :], CH, 2), ALU.mult))
                nc.vector.tensor_tensor(flat(kb[:, :, :]), flat(kn[:, :, :]), betas, ALU.mult).then_inc(norm_ready, 1)
                v.wait_ge(m_done, b + 1)
                for h in range(HL):
                    last = nc.vector.tensor_tensor(m[:, h, :, :], ps[h][:, :].rearrange("p (t j) -> p t j", j=P),
                                                   bc(mask[:, :], NB), ALU.mult)
                last.then_inc(m_ready, 1)

        @block.scalar
        def _(a):
            with a.Fori(0, B) as b:
                for i in range(3):
                    a.wait_ge(proj_done, b * 3 + (i + 1))
                    a.wait_ge(conv_ready, b * 3)
                    nc.scalar.copy(pre[i][:, lead:], ps[i][:, :]).then_inc(pre_ready, 1)
                a.wait_ge(beta_done, b + 1)
                nc.scalar.activation(beta[:, :, :], ps[3][:, 0:NB * HL].rearrange("p (t h) -> p t h", h=HL), ACT.Sigmoid)\
                    .then_inc(sg_ready, 1)
                for i, dst in enumerate((qT[:, :], kT[:, :], vT[:, lead:lead + S])):
                    a.wait_ge(conv_ready, b * 3 + (i + 1))
                    a.wait_ge(tok_done, b)
                    a.wait_ge(short_ready, b)
                    nc.scalar.activation(dst, conv[i][:, :], ACT.Silu).then_inc(silu_ready, 1)
                a.wait_ge(tok_done, b + 1)
                for i in range(2):
                    last = nc.scalar.activation(sq[:, i, :], ps[4 + i][:, :], ACT.Square)
                last.then_inc(sq_ready, 1)
                a.wait_ge(ss_ready, b + 1)
                nc.scalar.activation(rt[:, :, :], ss[:, :, :], ACT.Sqrt).then_inc(rt_ready, 1)
                a.wait_ge(norm_ready, b + 1)
                tiles = lambda ap: ap.rearrange("p (t c) -> p t c", c=P)
                nc.scalar.copy(st["vd"][:, bass.ds(b * 5 + 1, NB), :], tiles(ps[6][:, :]))
                a.wait_ge(sh_done, b + 1)
                nc.scalar.copy(st["short"][:, bass.ds(b * NB, NB), :], tiles(ps[7][:, :])).then_inc(vd_ready, 1)
                a.wait_ge(nT_done, b + 1)
                a.wait_ge(m_done, b)
                a.wait_ge(stores, b * (16 * n_stores))
                for i in range(3):
                    last = nc.scalar.copy(nT[i][:, :], ps[4 + i][:, :])
                last.then_inc(nT_ready, 1)



def filter_and_solve(nc, d, st):
    per = 8
    n = P // per
    with ExitStack() as ctx:
        sb = lambda name, shape, dt=F32: ctx.enter_context(nc.sbuf_tensor("l_" + name, shape, dt))
        sem = Signals(nc, ctx, "l_")
        ps = [ctx.enter_context(nc.psum_tensor(f"l_ps{i}", [P, 512], F32)) for i in range(2)]
        flip = sb("flip", [P, P])
        back = sb("back", [P, B * (NB + 1), P])
        cuts = B * (NB + 1) * P // 512
        piece = lambda ap, i: ap[:, i * 4:(i + 1) * 4, :].rearrange("p t c -> p (t c)")
        band = [sb(f"band{i}", [P, per, P + KL]) for i in range(2)]
        m, inv, prod = (sb(name, [P, NB, CH, CH]) for name in ("m", "inv", "prod"))
        flip_in, back_done, back_ready = sem("flip_in"), sem("back_done"), sem("back_ready")
        band_in = [sem(f"band_in{i}") for i in range(2)]
        done, ready = sem("done"), sem("ready")
        m_in, stored, dve, inv_ready = sem("m_in"), sem("stored"), sem("dve_steps"), sem("inv_ready")
        taps = bass.AP(d["fir_long"].tensor, 0, [[per * 3 * P, n], [1, P], [3 * P, per], [1, P + KL]])
        block = ctx.enter_context(nc.Block())

        @block.sync
        def _(sp):
            sp.dma_start(flip[:, :], d["flip"]).then_inc(flip_in, 16)
            sp.dma_start(m[:, :, :, :], d["m"].rearrange("b h t c i j -> (b h t) c i j")).then_inc(m_in, 16)
            for s in range(2):
                sp.dma_start(band[s][:, :, :], taps[s, :, :, :]).then_inc(band_in[s], 16)
            with sp.Fori(1, n // 2) as i:
                for s in range(2):
                    sp.wait_ge(done, i * 2 + (s - 1))
                    sp.dma_start(band[s][:, :, :], taps[i * 2 + s, :, :, :]).then_inc(band_in[s], 16)
            sp.wait_ge(inv_ready, 1)
            sp.dma_start(d["t"].rearrange("b h t c m j -> (b h t) c m j"), inv[:, :, :, :]).then_inc(stored, 16)
            sp.wait_ge(stored, 16)

        @block.tensor
        def _(pe):
            pe.wait_ge(flip_in, 16)
            for i in range(cuts):
                if i >= 2:
                    pe.wait_ge(back_ready, i - 1)
                nc.tensor.matmul(ps[i % 2][:, :], flip[:, :], piece(st["vd"], i), start=True, stop=True).then_inc(back_done, 1)
            pe.wait_ge(back_ready, cuts)
            tiles = back[:, :, :].rearrange("p (b t) c -> p b t c", t=NB + 1)
            with pe.Fori(0, n // 2) as i:
                for s in range(2):
                    pe.wait_ge(band_in[s], i * 16 + 16)
                    pe.wait_ge(ready, i * 2)
                    for k in range(per):
                        c = i * (2 * per) + (s * per + k)
                        out = ps[s][:, k * NT:(k + 1) * NT]
                        nc.tensor.matmul(out, band[s][:, k, 0:P], tiles[:, :, 1:NB + 1, c], start=True, stop=False,
                                         skip_group_check=True)
                        last = nc.tensor.matmul(out[0:KL, :], band[s][:, k, P:P + KL], tiles[:, :, 0:NB, c],
                                                start=False, stop=True, skip_group_check=True)
                    last.then_inc(done, 1)

        @block.scalar
        def _(a):
            for i in range(cuts):
                a.wait_ge(back_done, i + 1)
                nc.scalar.copy(piece(back, i), ps[i % 2][:, :]).then_inc(back_ready, 1)
            with a.Fori(0, n // 2) as i:
                for s in range(2):
                    a.wait_ge(done, i * 2 + (s + 1))
                    nc.scalar.copy(st["long"][:, :, bass.ds(i * (2 * per) + s * per, per)],
                                   ps[s][:, 0:per * NT].rearrange("p (c t) -> p t c", t=NT)).then_inc(ready, 1)

        @block.vector
        def _(v):
            step = Chain(v, dve)
            step(nc.vector.memset(inv[:, :, :, :], 0.0))
            diag = inv[:, :, :, :].rearrange("p c m j -> p c (m j)")[:, :, 0:CH * CH:CH + 1]
            step(nc.vector.memset(diag, 1.0))
            v.wait_ge(m_in, 16)
            for i in range(1, CH):
                row = bc(m[:, :, i, 0:i], i, 2)
                step(nc.vector.tensor_tensor(prod[:, :, 0:i, 0:i], inv[:, :, 0:i, 0:i], row, ALU.mult))
                last = nc.vector.tensor_reduce(inv[:, :, 0:i, i], prod[:, :, 0:i, 0:i], AX.X, ALU.add)
                if i < CH - 1:
                    step(last)
            last.then_inc(inv_ready, 1)


def scan(nc, d, st):
    with ExitStack() as ctx:
        sb = lambda name, shape, dt=F32: ctx.enter_context(nc.sbuf_tensor("c_" + name, shape, dt))
        sem = Signals(nc, ctx, "c_")
        ps = [ctx.enter_context(nc.psum_tensor(f"c_ps{i}", [P, 512], F32)) for i in range(8)]
        A, WS, DS, OUT = ps[0:2], ps[2:4], ps[4:6], ps[6:8]
        inv = sb("inv", [P, B * HL, P])
        kn, kb, vb = (sb(n, [P, B, P]) for n in ("kn", "kb", "vb"))
        qT, kT = sb("qT", [P, B, P]), sb("kT", [P, B, P])
        u, wT, ua = (sb(n, [P, B, P]) for n in ("u", "wT", "ua"))
        at = sb("at", [P, HL, B, P])
        state_ = sb("state", [P, B, P])
        mask = sb("mask", [P, P])
        hmask = sb("hmask", [P, P])
        zeros = sb("zeros", [1, 512], BF16)
        consts_in, zero = sem("consts_in"), sem("zero")
        uw_in, qk_in = sem("uw_in"), sem("qk_in")
        u_done, u_ready, w_done, w_ready = sem("u_done"), sem("u_ready"), sem("w_done"), sem("w_ready")
        at_done, at_ready, ws_done, ua_ready = sem("at_done"), sem("at_ready"), sem("ws_done"), sem("ua_ready")
        ds_done, state_ready, out_done, out_ready = sem("ds_done"), sem("state_ready"), sem("out_done"), sem("out_ready")
        block = ctx.enter_context(nc.Block())
        half = B // 2

        @block.sync
        def _(sp):
            sp.dma_start(mask[:, :], d["mask_a"]).then_inc(consts_in, 16)
            sp.dma_start(hmask[:, :], d["mask_h"]).then_inc(consts_in, 16)
            sp.wait_ge(zero, 1)
            with sp.Fori(0, NB) as t:
                sp.wait_ge(w_done, t)
                for c in range(NB):
                    cc = slice(c * CH, (c + 1) * CH)
                    sp.dma_start(inv[cc, :, cc], d["t"][:, :, t, c, :, :].rearrange("b h m j -> m (b h) j"))\
                        .then_inc(uw_in, 16)
                for i, dst in ((2, vb), (1, kb)):
                    sp.dma_start(dst[:, :, :], d["tok"][i, :, t, :, :].rearrange("b p c -> p b c")).then_inc(uw_in, 16)
                sp.wait_ge(ds_done, t * NB)
                for i, dst in enumerate((qT, kT)):
                    sp.dma_start(dst[:, :, :], d["chan"][i, :, :, bass.ds(t * P, P)].rearrange("b c s -> c b s"))\
                        .then_inc(qk_in, 16)
                sp.dma_start(kn[:, :, :], d["tok"][0, :, t, :, :].rearrange("b p c -> p b c")).then_inc(qk_in, 16)

        @block.gpsimd
        def _(gp):
            nc.gpsimd.memset(zeros[:, :], 0.0)
            nc.gpsimd.memset(state_[:, :, :], 0.0)
            nc.gpsimd.memset(inv[:, :, :], 0.0).then_inc(zero, 1)

        @block.tensor
        def _(pe):
            pe.wait_ge(zero, 1)

            def clear(banks):
                for bank in banks:
                    nc.tensor.matmul(bank[:, :], zeros[0:1, 0:P], zeros[0:1, :], start=True, stop=False,
                                     skip_group_check=True)

            clear(DS)
            with pe.Fori(0, NB) as t:
                pe.wait_ge(uw_in, t * (6 * 16) + 6 * 16)
                pe.wait_ge(at_ready, t * HL * 2)
                for b in range(B):
                    for h in range(HL):
                        hh = slice(h * CH, (h + 1) * CH)
                        at_ = (b % half) * P
                        last = nc.tensor.matmul(A[b // half][:, at_ + h * CH:at_ + (h + 1) * CH],
                                                inv[:, b * HL + h, :], vb[:, b, hh], start=True, stop=True)
                last.then_inc(u_done, 1)
                pe.wait_ge(u_ready, t + 1)
                for b in range(B):
                    for h in range(HL):
                        hh = slice(h * CH, (h + 1) * CH)
                        at_ = (b % half) * P
                        last = nc.tensor.matmul(A[b // half][hh, at_:at_ + P], kb[:, b, hh], inv[:, b * HL + h, :],
                                                start=True, stop=True)
                last.then_inc(w_done, 1)
                pe.wait_ge(w_ready, t + 1)
                pe.wait_ge(qk_in, t * (3 * 16) + 3 * 16)
                for k in range(HL * 2):
                    h, s = k // 2, k % 2
                    hh = slice(h * CH, (h + 1) * CH)
                    if k >= 2:
                        pe.wait_ge(at_ready, t * (HL * 2) + (k - 1))
                    for i in range(half):
                        last = nc.tensor.matmul(A[s][:, i * P:(i + 1) * P], kT[hh, s * half + i, :],
                                                qT[hh, s * half + i, :], start=True, stop=True)
                    last.then_inc(at_done, 1)
                pe.wait_ge(out_ready, t)
                clear(OUT)
                for c in range(NB):
                    cc = slice(c * CH, (c + 1) * CH)
                    pe.wait_ge(state_ready, t * NB + c)
                    for b in range(B):
                        last = nc.tensor.matmul(WS[b // half][cc, (b % half) * P:(b % half + 1) * P],
                                                wT[:, b, cc], state_[:, b, :], start=True, stop=True)
                    last.then_inc(ws_done, 1)
                    for b in range(B):
                        nc.tensor.matmul(OUT[b // half][cc, (b % half) * P:(b % half + 1) * P],
                                         qT[:, b, cc], state_[:, b, :], start=False, stop=False, skip_group_check=True)
                    pe.wait_ge(ua_ready, t * NB + (c + 1))
                    for b in range(B):
                        last = nc.tensor.matmul(DS[b // half][:, (b % half) * P:(b % half + 1) * P],
                                                kn[cc, b, :], ua[cc, b, :], start=False, stop=False,
                                                skip_group_check=True)
                    last.then_inc(ds_done, 1)
                pe.wait_ge(at_ready, t * (HL * 2) + HL * 2)
                for b in range(B):
                    for h in range(HL):
                        hh = slice(h * CH, (h + 1) * CH)
                        at_ = (b % half) * P
                        last = nc.tensor.matmul(OUT[b // half][:, at_ + h * CH:at_ + (h + 1) * CH], at[:, h, b, :],
                                                ua[:, b, hh], start=False, stop=False, skip_group_check=True)
                last.then_inc(out_done, 1)

        @block.vector
        def _(v):
            v.wait_ge(consts_in, 32)
            v.wait_ge(zero, 1)
            seqs = lambda bank: bank[:, :].rearrange("p (b c) -> p b c", c=P)
            with v.Fori(0, NB) as t:
                v.wait_ge(out_done, t)
                for k in range(HL * 2):
                    h, s = k // 2, k % 2
                    v.wait_ge(at_done, t * (HL * 2) + (k + 1))
                    nc.vector.tensor_tensor(at[:, h, s * half:(s + 1) * half, :], seqs(A[s]), bc(mask[:, :], half), ALU.mult)\
                        .then_inc(at_ready, 1)
                for c in range(NB):
                    cc = slice(c * CH, (c + 1) * CH)
                    v.wait_ge(ws_done, t * NB + (c + 1))
                    v.wait_ge(u_ready, t + 1)
                    for s in range(2):
                        last = nc.vector.tensor_tensor(ua[cc, s * half:(s + 1) * half, :], u[cc, s * half:(s + 1) * half, :],
                                                       seqs(WS[s])[cc, :, :], ALU.subtract)
                    last.then_inc(ua_ready, 1)
                    v.wait_ge(ds_done, t * NB + (c + 1))
                    for s in range(2):
                        last = nc.vector.tensor_tensor(state_[:, s * half:(s + 1) * half, :], seqs(DS[s]),
                                                       bc(hmask[:, :], half), ALU.mult)
                    last.then_inc(state_ready, 1)

        @block.scalar
        def _(a):
            seqs = lambda bank: bank[:, :].rearrange("p (b c) -> p b c", c=P)
            with a.Fori(0, NB) as t:
                a.wait_ge(u_done, t + 1)
                a.wait_ge(ua_ready, t * NB)
                for s in range(2):
                    last = nc.scalar.copy(u[:, s * half:(s + 1) * half, :], seqs(A[s]))
                last.then_inc(u_ready, 1)
                a.wait_ge(w_done, t + 1)
                a.wait_ge(out_done, t)
                for s in range(2):
                    last = nc.scalar.copy(wT[:, s * half:(s + 1) * half, :], seqs(A[s]))
                last.then_inc(w_ready, 1)
                a.wait_ge(out_done, t + 1)
                for s in range(2):
                    tiles = st["delta"][:, :, :].rearrange("p (b t) c -> p b t c", t=NB)
                    last = nc.scalar.copy(tiles[:, s * half:(s + 1) * half, t, :], seqs(OUT[s]))
                last.then_inc(out_ready, 1)



def gate1(nc, d, st):
    G = NB * HL
    with ExitStack() as ctx:
        sb = lambda name, shape, dt=F32: ctx.enter_context(nc.sbuf_tensor("g_" + name, shape, dt))
        sem = Signals(nc, ctx, "g_")
        ps = [ctx.enter_context(nc.psum_tensor(f"g_ps{i}", [P, 512], F32)) for i in range(8)]
        w1 = sb("w1", [P, (1 + HL) * P])
        w2 = sb("w2", [P, 4])
        wo = sb("wo", [P, P])
        b1 = sb("b1", [P, 1])
        b2 = sb("b2", [P, 4])
        nw = sb("nw", [P, CH])
        temp, res = sb("temp", [P, 4]), sb("res", [P, HL])
        xs = [sb(f"x{i}", [P, 4, S]) for i in range(2)]
        hTs = [sb(f"hT{i}", [P, S]) for i in range(2)]
        dev, sq, dsq = (sb(n, [P, 4, S]) for n in ("dev", "sq", "dsq"))
        sums, mean, l2 = (sb(n, [P, 4 * G]) for n in ("sums", "mean", "l2"))
        stat = sb("stat", [P, NB, HL, CH])
        statT = sb("statT", [P, S])
        h1 = [sb(f"h1{i}", [P, S]) for i in range(2)]
        z, ez, pr = (sb(n, [P, G, 4]) for n in ("z", "ez", "pr"))
        top, den, rden, rs = (sb(n, [P, G]) for n in ("top", "den", "rden", "rs"))
        mix, o, on, osq = (sb(n, [P, S]) for n in ("mix", "o", "on", "osq"))
        rt = sb("rt", [P, G])
        oT = sb("oT", [P, S])
        consts_in, zero, dve, act = sem("consts_in"), sem("zero"), sem("dve_steps"), sem("act_steps")
        temp0_ready, temp1_ready, temp2_ready = sem("temp0"), sem("temp1"), sem("temp2")
        x_ready, dev_ready, sq_ready, l2_ready = sem("x_ready"), sem("dev_ready"), sem("sq_ready"), sem("l2_ready")
        sum_ready, stat_ready, statT_done, statT_ready = (sem(n) for n in ("sum_ready", "stat_ready", "statT_done", "statT_ready"))
        h_done, h_ready, z_part, z_ready, ez_ready = (sem(n) for n in ("h_done", "h_ready", "z_part", "z_ready", "ez_ready"))
        o_ready, osq_ready, ms_ready, rt_ready, on_ready = (sem(n) for n in ("o_ready", "osq_ready", "ms_ready", "rt_ready", "on_ready"))
        oT_done, oT_ready, y_done, y_ready = (sem(n) for n in ("oT_done", "oT_ready", "y_done", "y_ready"))
        block = ctx.enter_context(nc.Block())
        groups = lambda ap: ap.rearrange("p (g e) -> p g e", e=CH)

        @block.sync
        def _(sp):
            for dst, src in ((w1[:, :], d["mlp1"]), (w2[:, :], d["mlp2"]), (wo[:, :], d["wo3"]),
                             (b1[:, :], d["mlp1_b"]), (b2[:, :], d["mlp2_b"].partition_broadcast(P)),
                             (nw[:, :], d["norm_w"].partition_broadcast(P)),
                             (temp[:, 0:1], d["temp"].partition_broadcast(P)),
                             (res[:, :], d["res"].partition_broadcast(P))):
                sp.dma_start(dst, src).then_inc(consts_in, 16)

        @block.gpsimd
        def _(gp):
            nc.gpsimd.memset(stat[:, :, :, :], 0.0).then_inc(zero, 1)

            def sequence(b, x, hT):
                after(gp, o_ready, b - 1)
                after(gp, h_done, (b - 1) * HL)
                for dst, src in ((0, "short"), (1, "long"), (2, "delta")):
                    nc.gpsimd.tensor_copy(x[:, dst, :].rearrange("p (t c) -> p t c", c=P),
                                          st[src][:, bass.ds(b * NB, NB), :])
                nc.gpsimd.tensor_copy(x[:, 3, :].rearrange("p (t c) -> p t c", c=P),
                                      st["vd"][:, bass.ds(b * (NB + 1) + 1, NB), :])
                nc.gpsimd.tensor_copy(hT[:, :], st["hsT"][:, bass.ds(b * S, S)]).then_inc(x_ready, 1)

            for s in range(2):
                sequence(s, xs[s], hTs[s])
            with gp.Fori(1, B // 2) as i:
                for s in range(2):
                    sequence(i * 2 + s, xs[s], hTs[s])

        @block.vector
        def _(v):
            step = Chain(v, dve)
            v.wait_ge(consts_in, 8 * 16)
            v.wait_ge(zero, 1)
            step(nc.vector.tensor_scalar(temp[:, 1:2], temp[:, 0:1], -1.0, None, ALU.mult))
            nc.vector.tensor_tensor(temp[:, 1:2], temp[:, 1:2], temp[:, 0:1], ALU.min).then_inc(temp0_ready, 1)
            v.wait_ge(temp1_ready, 1)
            step(nc.vector.tensor_scalar(temp[:, 3:4], temp[:, 0:1], 0.0, None, ALU.max))
            step(nc.vector.tensor_tensor(temp[:, 2:3], temp[:, 2:3], temp[:, 3:4], ALU.add))
            step(nc.vector.reciprocal(temp[:, 3:4], temp[:, 2:3]))

            def sequence(b, x):
                step.restart()
                v.wait_ge(x_ready, b + 1)
                v.wait_ge(statT_done, b)
                v.wait_ge(osq_ready, b)
                every = x[:, :, :].rearrange("p i (g e) -> p (i g) e", e=CH)
                many = lambda ap: ap.rearrange("p i (g e) -> p (i g) e", e=CH)
                out = lambda k: stat[:, :, :, k:4 * 4:4].rearrange("p t h i -> p i (t h)")
                branch = lambda ap: ap.rearrange("p (i g) -> p i g", i=4)
                step(nc.vector.tensor_reduce(sums[:, :], every, AX.X, ALU.add))
                step(nc.vector.tensor_scalar(mean[:, :], sums[:, :], 1.0 / CH, None, ALU.mult))
                nc.vector.tensor_tensor(many(dev[:, :, :]), every, bc(mean[:, :], CH, 2), ALU.subtract)\
                    .then_inc(dev_ready, 1)
                nc.vector.tensor_copy(out(0), branch(mean[:, :]))
                step(nc.vector.tensor_reduce(sums[:, :], every, AX.X, ALU.add, apply_absolute_value=True))
                step(nc.vector.tensor_scalar(out(2), branch(sums[:, :]), 1.0 / CH, None, ALU.mult))
                v.wait_ge(sq_ready, b * 2 + 1)
                nc.vector.tensor_reduce(l2[:, :], many(sq[:, :, :]), AX.X, ALU.add).then_inc(sum_ready, 1)
                v.wait_ge(sq_ready, b * 2 + 2)
                step(nc.vector.tensor_reduce(sums[:, :], many(dsq[:, :, :]), AX.X, ALU.add))
                step(nc.vector.tensor_scalar(out(1), branch(sums[:, :]), 1.0 / CH, None, ALU.mult))
                v.wait_ge(l2_ready, b + 1)
                nc.vector.tensor_copy(out(3), branch(l2[:, :])).then_inc(stat_ready, 1)
                v.wait_ge(z_part, b * HL + HL)
                zp = ps[4][:, 0:4 * G].rearrange("p (t h k) -> p (t h) k", h=HL, k=4)
                step(nc.vector.tensor_tensor(z[:, :, :], zp, bc(b2[:, :], G), ALU.add))
                step(nc.vector.tensor_scalar(z[:, :, :], z[:, :, :], temp[:, 3:4], None, ALU.mult))
                step(nc.vector.tensor_reduce(top[:, :], z[:, :, :], AX.X, ALU.max))
                nc.vector.tensor_tensor(z[:, :, :], z[:, :, :], bc(top[:, :], 4, 2), ALU.subtract).then_inc(z_ready, 1)
                v.wait_ge(ez_ready, b + 1)
                step(nc.vector.tensor_reduce(den[:, :], ez[:, :, :], AX.X, ALU.add))
                step(nc.vector.reciprocal(rden[:, :], den[:, :]))
                step(nc.vector.tensor_tensor(pr[:, :, :], ez[:, :, :], bc(rden[:, :], 4, 2), ALU.mult))
                step(nc.vector.tensor_scalar(pr[:, :, :], pr[:, :, :], 0.02, None, ALU.max))
                step(nc.vector.tensor_reduce(den[:, :], pr[:, :, :], AX.X, ALU.add))
                step(nc.vector.reciprocal(rden[:, :], den[:, :]))
                step(nc.vector.tensor_tensor(pr[:, :, :], pr[:, :, :], bc(rden[:, :], 4, 2), ALU.mult))
                p0 = pr[:, :, 0].rearrange("p (t h) -> p t h", h=HL)
                v.wait_ge(temp2_ready, 1)
                step(nc.vector.tensor_tensor(p0, p0, bc(res[:, :], NB), ALU.add))
                v.wait_ge(osq_ready, b)
                for i in range(4):
                    dst = o if i == 0 else mix
                    step(nc.vector.tensor_tensor(groups(dst[:, :]), groups(x[:, i, :]), bc(pr[:, :, i], CH, 2), ALU.mult))
                    if i:
                        last = nc.vector.tensor_tensor(o[:, :], o[:, :], mix[:, :], ALU.add)
                        if i < 3:
                            step(last)
                last.then_inc(o_ready, 1)
                v.wait_ge(osq_ready, b + 1)
                step(nc.vector.tensor_reduce(rs[:, :], groups(osq[:, :]), AX.X, ALU.add))
                nc.vector.tensor_scalar(rs[:, :], rs[:, :], 1.0 / CH, LN_EPS, ALU.mult, ALU.add).then_inc(ms_ready, 1)
                v.wait_ge(rt_ready, b + 1)
                step(nc.vector.reciprocal(rden[:, :], rt[:, :]))
                v.wait_ge(oT_done, b)
                step(nc.vector.tensor_tensor(groups(on[:, :]), groups(o[:, :]), bc(rden[:, :], CH, 2), ALU.mult))
                nc.vector.tensor_tensor(groups(on[:, :]), groups(on[:, :]), bc(nw[:, :], G), ALU.mult).then_inc(on_ready, 1)

            with v.Fori(0, B // 2) as i:
                for s in range(2):
                    sequence(i * 2 + s, xs[s])

        @block.scalar
        def _(a):
            a.wait_ge(temp0_ready, 1)
            nc.scalar.activation(temp[:, 2:3], temp[:, 1:2], ACT.Exp).then_inc(act, 1)
            a.wait_ge(act, 1)
            nc.scalar.activation(temp[:, 2:3], temp[:, 2:3], ACT.Ln, bias=1.0).then_inc(temp1_ready, 1)
            nc.scalar.activation(res[:, :], res[:, :], ACT.Sigmoid).then_inc(temp2_ready, 1)

            def sequence(b, x):
                a.wait_ge(x_ready, b + 1)
                nc.scalar.activation(sq[:, :, :], x[:, :, :], ACT.Square).then_inc(sq_ready, 1)
                a.wait_ge(dev_ready, b + 1)
                nc.scalar.activation(dsq[:, :, :], dev[:, :, :], ACT.Square).then_inc(sq_ready, 1)
                a.wait_ge(sum_ready, b + 1)
                nc.scalar.activation(l2[:, :], l2[:, :], ACT.Sqrt).then_inc(l2_ready, 1)
                a.wait_ge(statT_done, b + 1)
                a.wait_ge(h_done, b * HL)
                nc.scalar.copy(statT[:, :], ps[0][:, :]).then_inc(statT_ready, 1)
                for h in range(HL):
                    a.wait_ge(h_done, b * HL + (h + 1))
                    if h >= 2:
                        a.wait_ge(z_part, b * HL + (h - 1))
                    else:
                        a.wait_ge(z_part, b * HL)
                    nc.scalar.activation(h1[h % 2][:, :], ps[1 + h % 2][:, :], ACT.Gelu_apprx_tanh, bias=b1[:, 0:1])\
                        .then_inc(h_ready, 1)
                a.wait_ge(z_ready, b + 1)
                nc.scalar.activation(ez[:, :, :], z[:, :, :], ACT.Exp).then_inc(ez_ready, 1)
                a.wait_ge(o_ready, b + 1)
                a.wait_ge(ms_ready, b)
                nc.scalar.activation(osq[:, :], o[:, :], ACT.Square).then_inc(osq_ready, 1)
                a.wait_ge(ms_ready, b + 1)
                nc.scalar.activation(rt[:, :], rs[:, :], ACT.Sqrt).then_inc(rt_ready, 1)
                a.wait_ge(oT_done, b + 1)
                a.wait_ge(y_done, b)
                nc.scalar.copy(oT[:, :], ps[5][:, :]).then_inc(oT_ready, 1)
                a.wait_ge(y_done, b + 1)
                nc.scalar.copy(st["s1"][:, bass.ds(b * NB, NB), :], ps[6][:, :].rearrange("p (t d) -> p t d", d=P))\
                    .then_inc(y_ready, 1)

            with a.Fori(0, B // 2) as i:
                for s in range(2):
                    sequence(i * 2 + s, xs[s])

        @block.tensor
        def _(pe):
            pe.wait_ge(consts_in, 8 * 16)
            pe.wait_ge(zero, 1)

            def sequence(b, hT):
                pe.wait_ge(stat_ready, b + 1)
                pe.wait_ge(statT_ready, b)
                for t in range(NB):
                    last = nc.tensor.transpose(ps[0][:, t * P:(t + 1) * P], stat[:, t, :, :].rearrange("p h k -> p (h k)"),
                                               st["ident"][:, :])
                last.then_inc(statT_done, 1)
                pe.wait_ge(statT_ready, b + 1)

                def logits(h):
                    pe.wait_ge(h_ready, b * HL + (h + 1))
                    if h == 0:
                        pe.wait_ge(z_ready, b)
                    for t in range(NB):
                        out = ps[4][:, (t * HL + h) * 4:(t * HL + h) * 4 + 4]
                        last = nc.tensor.matmul(out, h1[h % 2][:, t * P:(t + 1) * P], w2[:, :], start=True, stop=True)
                    last.then_inc(z_part, 1)

                for h in range(HL):
                    if h >= 2:
                        pe.wait_ge(h_ready, b * HL + (h - 1))
                    else:
                        pe.wait_ge(h_ready, b * HL)
                    out = ps[1 + h % 2]
                    nc.tensor.matmul(out[:, :], w1[:, 0:P], hT[:, :], start=True, stop=False)
                    nc.tensor.matmul(out[:, :], w1[:, (1 + h) * P:(2 + h) * P], statT[:, :], start=False, stop=True)\
                        .then_inc(h_done, 1)
                    if h:
                        logits(h - 1)
                logits(HL - 1)
                pe.wait_ge(on_ready, b + 1)
                pe.wait_ge(oT_ready, b)
                for t in range(NB):
                    last = nc.tensor.transpose(ps[5][:, t * P:(t + 1) * P], on[:, t * P:(t + 1) * P], st["ident"][:, :])
                last.then_inc(oT_done, 1)
                pe.wait_ge(oT_ready, b + 1)
                pe.wait_ge(y_ready, b)
                for t in range(NB):
                    last = nc.tensor.matmul(ps[6][:, t * P:(t + 1) * P], oT[:, t * P:(t + 1) * P], wo[:, :],
                                            start=True, stop=True)
                last.then_inc(y_done, 1)

            with pe.Fori(0, B // 2) as i:
                for s in range(2):
                    sequence(i * 2 + s, hTs[s])


def sinkhorn(nc, d, st):
    FOLD = 5
    with ExitStack() as ctx:
        sb = lambda name, shape, dt=F32: ctx.enter_context(nc.sbuf_tensor("k_" + name, shape, dt))
        sem = Signals(nc, ctx, "k_")
        lg_ps, t_ps, m_ps, s_ps = (ctx.enter_context(nc.psum_tensor("k_" + n, [P, 512], F32))
                                   for n in ("lg_ps", "t_ps", "m_ps", "s_ps"))
        w = sb("w", [P, NE2])
        down = sb("down", [P, NE2])
        ones = sb("ones", [P, P])
        c, z, zc, ez, key, hot = (sb(n, [P, NT, NE2]) for n in ("c", "z", "zc", "ez", "key", "hot"))
        weight = sb("weight", [P, NT, TOPK2])
        rm, rsum, rrec, rlog, vmax, kmax = (sb(n, [P, NT]) for n in ("rm", "rsum", "rrec", "rlog", "vmax", "kmax"))
        cm, cmb, cpart, csum, crec, clog = (sb(n, [P, NE2]) for n in ("cm", "cmb", "cpart", "csum", "crec", "clog"))
        top = sb("top", [NE2, 1])
        topb = sb("topb", [NE2, P])
        one8 = sb("one8", [NE2, P])
        consts_in, lg_done, zero, dve = sem("consts_in"), sem("lg_done"), sem("zero"), sem("dve_steps")
        row_ready, row_exp, sums_ready, logs_ready = (sem(n) for n in ("row_ready", "row_exp", "sums_ready", "logs_ready"))
        cm_ready, cmT_done, topb_ready, cmb_done = (sem(n) for n in ("cm_ready", "cmT_done", "topb_ready", "cmb_done"))
        col_ready, col_exp, cpart_ready, csum_done = (sem(n) for n in ("col_ready", "col_exp", "cpart_ready", "csum_done"))
        last_ready, last_exp = sem("last_ready"), sem("last_exp")
        block = ctx.enter_context(nc.Block())

        @block.sync
        def _(sp):
            sp.dma_start(w[:, :], d["gate_w"]).then_inc(consts_in, 16)
            sp.dma_start(down[:, :], d["down2"].partition_broadcast(P)).then_inc(consts_in, 16)

        @block.tensor
        def _(pe):
            pe.wait_ge(consts_in, 32)
            for t in range(NT):
                last = nc.tensor.matmul(lg_ps[:, t * NE2:(t + 1) * NE2], st["hsT"][:, t * P:(t + 1) * P], w[:, :],
                                        start=True, stop=True)
            last.then_inc(lg_done, 1)
            pe.wait_ge(zero, 1)
            with pe.Fori(0, SINKHORN) as i:
                pe.wait_ge(cm_ready, i + 1)
                nc.tensor.transpose(t_ps[0:NE2, 0:P], cm[:, :], st["ident"][:, :]).then_inc(cmT_done, 1)
                pe.wait_ge(topb_ready, i + 1)
                nc.tensor.matmul(m_ps[:, 0:NE2], topb[:, :], st["ident"][0:NE2, 0:NE2], start=True, stop=True)\
                    .then_inc(cmb_done, 1)
                pe.wait_ge(cpart_ready, i + 1)
                nc.tensor.matmul(s_ps[:, 0:NE2], ones[:, :], cpart[:, :], start=True, stop=True).then_inc(csum_done, 1)

        @block.vector
        def _(v):
            step = Chain(v, dve)
            by_expert = lambda ap: ap.rearrange("p t e -> p e t")
            step(nc.vector.memset(ones[:, :], 1.0))
            step(nc.vector.memset(one8[:, :], 1.0))
            step(nc.vector.memset(cmb[:, :], 0.0))
            nc.vector.memset(crec[:, :], 1.0).then_inc(zero, 1)
            v.wait_ge(zero, 1)
            v.wait_ge(consts_in, 32)
            v.wait_ge(lg_done, 1)
            step(nc.vector.tensor_scalar(c[:, :, :], lg_ps[:, 0:NT * NE2].rearrange("p (t e) -> p t e", e=NE2),
                                         float(-1.0 / SK_EPS), None, ALU.mult))
            with v.Fori(0, SINKHORN // FOLD) as fold:
                with v.Fori(0, FOLD) as at:
                    i = fold * FOLD + at
                    step.restart()
                    step(nc.vector.tensor_tensor(z[:, :, :], c[:, :, :], bc(cmb[:, :], NT), ALU.subtract))
                    step(nc.vector.tensor_reduce(rm[:, :], z[:, :, :], AX.X, ALU.max))
                    nc.vector.tensor_tensor(z[:, :, :], z[:, :, :], bc(rm[:, :], NE2, 2), ALU.subtract).then_inc(row_ready, 1)
                    step(nc.vector.tensor_tensor(zc[:, :, :], c[:, :, :], bc(rm[:, :], NE2, 2), ALU.subtract))
                    nc.vector.tensor_reduce(cm[:, :], by_expert(zc[:, :, :]), AX.X, ALU.max).then_inc(cm_ready, 1)
                    v.wait_ge(row_exp, i + 1)
                    step(nc.vector.tensor_tensor(ez[:, :, :], ez[:, :, :], bc(crec[:, :], NT), ALU.mult))
                    step(nc.vector.tensor_reduce(rsum[:, :], ez[:, :, :], AX.X, ALU.add))
                    step(nc.vector.reciprocal(rrec[:, :], rsum[:, :]))
                    v.wait_ge(cmT_done, i + 1)
                    step(nc.vector.tensor_reduce(top[:, :], t_ps[0:NE2, 0:P], AX.X, ALU.max))
                    nc.vector.tensor_scalar(topb[:, :], one8[:, :], top[:, 0:1], None, ALU.mult).then_inc(topb_ready, 1)
                    v.wait_ge(cmb_done, i + 1)
                    step(nc.vector.tensor_copy(cmb[:, :], m_ps[:, 0:NE2]))
                    nc.vector.tensor_tensor(zc[:, :, :], zc[:, :, :], bc(cmb[:, :], NT), ALU.subtract).then_inc(col_ready, 1)
                    v.wait_ge(col_exp, i + 1)
                    step(nc.vector.tensor_tensor(ez[:, :, :], ez[:, :, :], bc(rrec[:, :], NE2, 2), ALU.mult))
                    nc.vector.tensor_reduce(cpart[:, :], by_expert(ez[:, :, :]), AX.X, ALU.add).then_inc(cpart_ready, 1)
                    v.wait_ge(csum_done, i + 1)
                    step(nc.vector.tensor_copy(csum[:, :], s_ps[:, 0:NE2]))
                    step(nc.vector.reciprocal(crec[:, :], csum[:, :]))
                nc.vector.tensor_copy(rlog[:, :], rsum[:, :])
                nc.vector.tensor_copy(clog[:, :], csum[:, :]).then_inc(sums_ready, 1)
                v.wait_ge(logs_ready, fold + 1)
                step(nc.vector.tensor_tensor(cmb[:, :], cmb[:, :], clog[:, :], ALU.add))
                step(nc.vector.memset(crec[:, :], 1.0))
            step(nc.vector.tensor_tensor(z[:, :, :], zc[:, :, :], bc(rlog[:, :], NE2, 2), ALU.subtract))
            nc.vector.tensor_tensor(z[:, :, :], z[:, :, :], bc(clog[:, :], NT), ALU.subtract).then_inc(last_ready, 1)
            v.wait_ge(last_exp, 1)
            step(nc.vector.tensor_scalar(key[:, :, :], z[:, :, :], float(np.log(np.finfo(np.float32).tiny)), None,
                                         ALU.is_ge))
            step(nc.vector.tensor_tensor(ez[:, :, :], ez[:, :, :], key[:, :, :], ALU.mult))
            gates = st["gates1"]
            step(nc.vector.tensor_copy(weight[:, :, :], ez[:, :, 0:TOPK2]))
            for k in range(TOPK2):
                step(nc.vector.tensor_reduce(vmax[:, :], ez[:, :, :], AX.X, ALU.max))
                step(nc.vector.tensor_tensor(key[:, :, :], ez[:, :, :], bc(vmax[:, :], NE2, 2), ALU.is_equal))
                step(nc.vector.tensor_tensor(key[:, :, :], key[:, :, :], bc(down[:, :], NT), ALU.mult))
                step(nc.vector.tensor_reduce(kmax[:, :], key[:, :, :], AX.X, ALU.max))
                step(nc.vector.tensor_tensor(hot[:, :, :], key[:, :, :], bc(kmax[:, :], NE2, 2), ALU.is_equal))
                dst = gates if k == 0 else key
                step(nc.vector.tensor_tensor(dst[:, :, :], hot[:, :, :], bc(weight[:, :, k], NE2, 2), ALU.mult))
                if k:
                    step(nc.vector.tensor_tensor(gates[:, :, :], gates[:, :, :], key[:, :, :], ALU.add))
                else:
                    step(nc.vector.scalar_tensor_tensor(out=ez[:, :, :], in0=hot[:, :, :], scalar=-4.0,
                                                        in1=ez[:, :, :], op0=ALU.mult, op1=ALU.add))

        @block.scalar
        def _(a):
            with a.Fori(0, SINKHORN // FOLD) as fold:
                with a.Fori(0, FOLD) as at:
                    i = fold * FOLD + at
                    a.wait_ge(row_ready, i + 1)
                    nc.scalar.activation(ez[:, :, :], z[:, :, :], ACT.Exp).then_inc(row_exp, 1)
                    a.wait_ge(col_ready, i + 1)
                    nc.scalar.activation(ez[:, :, :], zc[:, :, :], ACT.Exp).then_inc(col_exp, 1)
                a.wait_ge(sums_ready, fold + 1)
                nc.scalar.activation(rlog[:, :], rlog[:, :], ACT.Ln)
                nc.scalar.activation(clog[:, :], clog[:, :], ACT.Ln).then_inc(logs_ready, 1)
            a.wait_ge(last_ready, 1)
            nc.scalar.activation(ez[:, :, :], z[:, :, :], ACT.Exp).then_inc(last_exp, 1)


def experts1(nc, d, st):
    F = DF // P
    with ExitStack() as ctx:
        sb = lambda name, shape, dt=F32: ctx.enter_context(nc.sbuf_tensor("f_" + name, shape, dt))
        sem = Signals(nc, ctx, "f_")
        bank = lambda n: ctx.enter_context(nc.psum_tensor("f_" + n, [P, 512], F32))
        g_ps, u_ps, y_ps = ([bank(f"{n}{i}") for i in range(2)] for n in ("g", "u", "y"))
        wg, wu, wd = ([sb(f"{n}{i}", [P, DF]) for i in range(2)] for n in ("wg", "wu", "wd"))
        g = [sb(f"silu{i}", [P, S]) for i in range(2)]
        act = [sb(f"act{i}", [P, F, S]) for i in range(2)]
        tail = [sb(f"tail{i}", [P, NB, P]) for i in range(2)]
        gb = [sb(f"gb{i}", [P, NB]) for i in range(2)]
        w_in = [sem(f"w_in{i}") for i in range(2)]
        slot_done = [sem(f"slot_done{i}") for i in range(2)]
        gu_done, g_ready, act_ready, sum_ready, stored = (sem(n) for n in
            ("gu_done", "g_ready", "act_ready", "sum_ready", "stored"))
        gb_ready, silu_ready, mul_ready, out_ready = (sem(n) for n in
            ("gb_ready", "silu_ready", "mul_ready", "out_ready"))
        block = ctx.enter_context(nc.Block())

        def units(eng, ahead, behind):
            with eng.Fori(0, NE2 // 2) as i:
                for k in range(2):
                    unit = lambda b, s: (i, k, b, s, i * (2 * B) + b + k * B)
                    ahead(*unit(0, 0))
                    with eng.Fori(0, B // 2 - 1) as j:
                        for s in range(2):
                            ahead(*unit(j * 2 + (s + 1), 1 - s))
                            behind(*unit(j * 2 + s, s))
                    ahead(*unit(B - 1, 1))
                    behind(*unit(B - 2, 0))
                    behind(*unit(B - 1, 1))

        @block.sync
        def _(sp):
            with sp.Fori(0, NE2 // 2) as i:
                for k in range(2):
                    sp.wait_ge(slot_done[k], i * B)
                    for dst, src in ((wg, "wg"), (wu, "wu"), (wd, "wd")):
                        sp.dma_start(dst[k][:, :], d[src][i * 2 + k, :, :]).then_inc(w_in[k], 16)
            with sp.Fori(0, B // 2) as j:
                for s in range(2):
                    sp.wait_ge(out_ready, j * 2 + (s + 1))
                    sp.dma_start(d["out"][j * 2 + s, :, :].rearrange("(t p) d -> p t d", p=P), tail[s][:, :, :])\
                        .then_inc(stored, 16)
            sp.wait_ge(stored, 16 * B)

        @block.tensor
        def _(pe):
            def hidden(i, k, b, s, n):
                if s == 0:
                    pe.wait_ge(w_in[k], i * 48 + 48)
                x = st["hsT"][:, bass.ds(b * S, S)]
                for f in range(F):
                    if f >= 2:
                        pe.wait_ge(act_ready, n * F + (f - 1))
                    else:
                        pe.wait_ge(act_ready, n * F)
                    ff = slice(f * P, (f + 1) * P)
                    nc.tensor.matmul(g_ps[f % 2][:, :], wg[k][:, ff], x, start=True, stop=True)
                    nc.tensor.matmul(u_ps[f % 2][:, :], wu[k][:, ff], x, start=True, stop=True).then_inc(gu_done, 1)

            def down(i, k, b, s, n):
                pe.wait_ge(act_ready, n * F + F)
                pe.wait_ge(sum_ready, n)
                for t in range(NB):
                    for f in range(F):
                        last = nc.tensor.matmul(y_ps[s][:, t * P:(t + 1) * P], act[s][:, f, t * P:(t + 1) * P],
                                                wd[k][:, f * P:(f + 1) * P], start=(f == 0), stop=(f == F - 1))
                last.then_inc(slot_done[k], 1)

            units(pe, hidden, down)

        @block.scalar
        def _(a):
            def unit(i, k, b, s, n):
                for f in range(F):
                    a.wait_ge(gu_done, n * F + (f + 1))
                    if f >= 2:
                        a.wait_ge(act_ready, n * F + (f - 1))
                    else:
                        a.wait_ge(act_ready, n * F)
                    nc.scalar.activation(g[f % 2][:, :], g_ps[f % 2][:, :], ACT.Silu).then_inc(g_ready, 1)

            units(a, unit, lambda *_: None)
            with a.Fori(0, B // 2) as j:
                for s in range(2):
                    b = j * 2 + s
                    a.wait_ge(sum_ready, NE2 * B + 1)
                    a.wait_ge(out_ready, j * 2)
                    nc.scalar.activation(g[s][:, :].rearrange("p (t d) -> p t d", d=P),
                                         st["sum1"][:, bass.ds(b * NB, NB), :], ACT.Silu).then_inc(silu_ready, 1)

        @block.vector
        def _(v):
            nc.vector.memset(st["sum1"][:, :, :], 0.0).then_inc(sum_ready, 1)
            v.wait_ge(sum_ready, 1)

            def hidden(i, k, b, s, n):
                v.wait_ge(slot_done[1 - k], i * B + (B if k else 0))
                if isinstance(b, int) and b < 2:
                    v.wait_ge(slot_done[k], i * B)
                else:
                    v.wait_ge(slot_done[k], i * B + (b - 1))
                for f in range(F):
                    v.wait_ge(g_ready, n * F + (f + 1))
                    nc.vector.tensor_tensor(act[s][:, f, :], g[f % 2][:, :], u_ps[f % 2][:, :], ALU.mult)\
                        .then_inc(act_ready, 1)

            def add(i, k, b, s, n):
                v.wait_ge(slot_done[k], i * B + (b + 1))
                nc.vector.tensor_copy(gb[s][:, :], st["gates1"][:, bass.ds(b * NB, NB), bass.ds(i * 2 + k, 1)]
                                      .rearrange("p t e -> p (t e)")).then_inc(gb_ready, 1)
                v.wait_ge(gb_ready, n + 1)
                for t in range(NB):
                    at = st["sum1"][:, b * NB + t, :]
                    last = nc.vector.scalar_tensor_tensor(out=at, in0=y_ps[s][:, t * P:(t + 1) * P],
                                                          scalar=gb[s][:, t:t + 1], in1=at, op0=ALU.mult, op1=ALU.add)
                last.then_inc(sum_ready, 1)

            units(v, hidden, add)
            with v.Fori(0, B // 2) as j:
                for s in range(2):
                    b = j * 2 + s
                    v.wait_ge(silu_ready, j * 2 + (s + 1))
                    v.wait_ge(stored, j * 32)
                    nc.vector.tensor_tensor(tail[s][:, :, :], st["s1"][:, bass.ds(b * NB, NB), :],
                                            g[s][:, :].rearrange("p (t d) -> p t d", d=P), ALU.mult).then_inc(mul_ready, 1)
                    v.wait_ge(mul_ready, j * 2 + (s + 1))
                    nc.vector.tensor_tensor(tail[s][:, :, :], tail[s][:, :, :], st["acc"][:, bass.ds(b * NB, NB), :],
                                            ALU.add).then_inc(out_ready, 1)



def program(nc, d):
    with ExitStack() as ctx:
        sb = lambda name, shape, dt=F32, c=ctx: c.enter_context(nc.sbuf_tensor(name, shape, dt))
        st = state(nc, ctx)
        st["acc"] = sb("acc", [P, NT, P])
        st["hsT"] = sb("hsT", [P, B * S])
        with ExitStack() as c1:
            st["ctx0"] = sb("ctx0", [P, NT, P], F32, c1)
            with ExitStack() as c2:
                st["v0"] = sb("v0", [P, NT, H0, D0 + 1], F32, c2)
                prepare(nc, d, st)
                attn0(nc, d, st)
            attn1(nc, d, st)
            route(nc, d, st)
            experts(nc, d, st)
            join0(nc, d, st)
        st["s1"] = sb("s1", [P, NT, P])
        with ExitStack() as c1:
            st["vd"] = sb("vd", [P, B * (NB + 1), P], F32, c1)
            st["short"] = sb("short", [P, NT, P], F32, c1)
            st["long"] = sb("long", [P, NT, P], F32, c1)
            st["delta"] = sb("delta", [P, NT, P], F32, c1)
            project1(nc, d, st)
            filter_and_solve(nc, d, st)
            scan(nc, d, st)
            gate1(nc, d, st)
        st["gates1"] = sb("gates1", [P, NT, NE2])
        st["sum1"] = sb("sum1", [P, NT, P])
        sinkhorn(nc, d, st)
        experts1(nc, d, st)



def layout(inputs):
    f = lambda name: np.asarray(inputs[name])
    swap = np.arange(P) ^ 1
    a = {"x": f("L0_attn_x")}
    wq, wk, wv, wo = (f("L0_attn_" + n) for n in ("wq", "wk", "wv", "wo"))
    a["w0"] = np.concatenate([wq.T, wq[swap].T, wk.T, wk[swap].T, wv.T, wo.T], axis=1)
    inv = (np.float32(10000.0) ** (-np.arange(0, D0, 2, dtype=np.float32) / np.float32(D0))).astype(np.float32)
    angles = np.outer(np.arange(S, dtype=np.float32), inv).astype(np.float32)
    lane = (np.arange(P) % D0) // 2
    sign = np.where(np.arange(P) % 2 == 0, -1.0, 1.0).astype(np.float32)
    a["cos0"] = np.cos(angles).astype(np.float32).T[lane]
    a["sin0"] = np.sin(angles).astype(np.float32).T[lane] * sign[:, None]
    a["sign"] = sign[:, None]
    a["ident"] = np.eye(P, dtype=np.float32)
    a["flip"] = np.ascontiguousarray(a["ident"][::-1])
    q, k = np.indices((P, P))
    a["mask_q"] = np.where(k > q, np.float32(NEG), np.float32(0))
    a["mask_k"] = np.ascontiguousarray(a["mask_q"].T)
    a["pos"] = np.arange(S, dtype=np.float32)[None]
    a["theta"] = f("L0_ffn_theta")[(np.arange(P) % D1) // 2][:, None]
    sel = np.zeros((4, 2, P), np.float32)
    sel[0:2, 0] = 1
    sel[2:4, 1] = 1
    a["sel"] = sel
    a["gamma1"] = f("L0_ffn_gamma1")[None]
    a["o_b"] = f("L0_ffn_o_b")[None]
    qw, kw, vw, ow = (f("L0_ffn_" + n) for n in ("q_w", "k_w", "v_w", "o_w"))
    qb, kb = f("L0_ffn_q_b"), f("L0_ffn_k_b")
    cols = [np.arange(P) + P * p for p in range(NPAIR)]
    a["w1"] = np.stack([np.concatenate([qw[:, c], qw[:, c][:, swap], kw[:, c], kw[:, c][:, swap], vw[:, c],
                                        qb[c][:, None], qb[c][swap][:, None], kb[c][:, None], kb[c][swap][:, None]],
                                       axis=1) for c in cols])
    a["wo1"] = np.concatenate([ow.reshape(NPAIR, P, P), f("L0_ffn_v_b").reshape(NPAIR, P, 1)], axis=2)
    a["gamma2"] = f("L0_ffn_gamma2")[None]
    a["router_w"] = f("L0_ffn_router_w")
    a["router_b"] = f("L0_ffn_router_b")[None]
    a["down"] = np.arange(NE, 0, -1, dtype=np.float32)[None]
    w1s = np.concatenate([f("L0_ffn_sh_w1")[None], f("L0_ffn_re_w1")])
    w2s = np.concatenate([f("L0_ffn_sh_w2")[None], f("L0_ffn_re_w2")])
    b1s = np.concatenate([f("L0_ffn_sh_b1")[None], f("L0_ffn_re_b1")])
    a["w2"] = np.concatenate([w1s, w2s, b1s[:, :, None]], axis=2)
    a["b2"] = f("L0_ffn_re_b2")
    a["sh_b2"] = f("L0_ffn_sh_b2")[:, None]
    a["sel_e"] = np.tile(np.repeat(np.eye(NE, dtype=np.float32), P, axis=1).reshape(NE, NE, P), (3, 1, 1))
    l = lambda name: f("L1_attn_" + name)
    a["w3"] = np.concatenate([l("q_w").T, l("k_w").T, l("v_w").T, l("b_w").T], axis=1)
    a["cw"] = np.stack([l("q_cw"), l("k_cw"), l("v_cw")], axis=1)
    a["fir_short"] = l("fir_short_w").reshape(P, KF)
    taps = np.zeros((P, 3 * P), np.float32)
    taps[:, P - 1:P - 1 + KL] = l("fir_long_w").reshape(P, KL)[:, ::-1]
    a["fir_long"] = taps
    same = (q // CH) == (k // CH)
    a["mask_m"] = np.where(same & (k < q), np.float32(-1), np.float32(0))
    a["mask_a"] = np.where(same & (k >= q), np.float32(1), np.float32(0))
    a["mask_h"] = same.astype(np.float32)
    mlp1 = l("mlp1_w")
    blocks = [mlp1[:, :P].T]
    for head in range(HL):
        block = np.zeros((P, P), np.float32)
        block[head * CH:head * CH + 16] = mlp1[:, P:].T
        blocks.append(block)
    a["mlp1"] = np.concatenate(blocks, axis=1)
    a["mlp1_b"] = l("mlp1_b")[:, None]
    a["mlp2"] = l("mlp2_w").T
    a["mlp2_b"] = l("mlp2_b")[None]
    a["wo3"] = l("o_w").T
    a["norm_w"] = l("norm_w")[None]
    a["temp"] = l("logit_temp")[None]
    a["res"] = l("conv_res_logit")[None]
    m = lambda name: f("L1_ffn_" + name)
    a["gate_w"] = m("gate_W").T
    a["down2"] = np.arange(NE2, 0, -1, dtype=np.float32)[None]
    a["wg"] = m("W_gate").transpose(0, 2, 1)
    a["wu"] = m("W_up").transpose(0, 2, 1)
    a["wd"] = m("W_down").transpose(0, 2, 1).reshape(NE2, DF // P, P, P).transpose(0, 2, 1, 3).reshape(NE2, P, DF)
    return {k: np.ascontiguousarray(v) for k, v in a.items()}



def scratch(nc, d):
    dr = lambda name, shape, dt=F32: nc.dram_tensor(name, shape, dt, kind="Internal").ap()
    d["xfT"] = dr("xfT_d", (B, P, S))
    d["parts"] = dr("parts_d", (2, B, 3, P, S), BF16)
    d["anT"] = dr("anT_d", (B, P, S))
    d["g3T"] = dr("g3T_d", (B, 3 * NE, S), BF16)
    d["gT"] = dr("gT_d", (B, NE, S))
    d["yT"] = dr("yT_d", (B, P, S))
    d["tok"] = dr("tok_d", (3, B, NB, P, P))
    d["chan"] = dr("chan_d", (2, B, P, S))
    d["m"] = dr("m_d", (B, HL, NB, NB, CH, CH))
    d["t"] = dr("t_d", (B, HL, NB, NB, CH, CH))



def kernel(**inputs):
    import concourse.bacc as bacc
    from concourse.bass_utils import run_bass_kernel_spmd

    nc = bacc.Bacc("TRN2", target_bir_lowering=False, num_devices=1)
    arrays = {"in_" + name: a for name, a in layout(inputs).items()}
    d = {name[3:]: nc.dram_tensor(name, a.shape, mybir.dt.from_np(a.dtype), kind="ExternalInput").ap()
         for name, a in arrays.items()}
    d["out"] = nc.dram_tensor("out", (B, S, P), F32, kind="ExternalOutput").ap()
    scratch(nc, d)
    program(nc, d)
    return run_bass_kernel_spmd(nc, [arrays], core_ids=[0]).results[0]["out"]
```
